# Optimizing a Trainium2 kernel written in Bass

```python
import numpy as np
import jax
import jax.numpy as jnp

def _softmax(x, axis=-1):
    return jax.nn.softmax(x, axis=axis)

def _gelu(x):
    return jax.nn.gelu(x, approximate=True)

def _silu(x):
    return jax.nn.silu(x)

def _sigmoid(x):
    return jax.nn.sigmoid(x)

def _layernorm(x, axis=-1, eps=1e-05):
    m = jnp.mean(x, axis=axis, keepdims=True)
    v = jnp.var(x, axis=axis, keepdims=True)
    return (x - m) / jnp.sqrt(v + eps)

def _scatter_add(tgt, idx, src, axis=0):
    return tgt.at[idx].add(src)

def _segment_sum(src, seg, n):
    return jax.ops.segment_sum(src, seg, n)
kernel_name = 'mk_hybrid_d1_jaxref_r8_59172a'

def setup_inputs(seed: int=0):
    np.random.seed(seed)
    _w = jnp.asarray

    def _L0_attn_a_setup():
        import math
        import jax, jax.numpy as jnp
        import numpy as np
        NUM_BUCKETS = 32
        MAX_DISTANCE = 128
        HEADS = 16
        D_MODEL = 128
        SEQ = 128
        BATCH = 4
        SCALE = (D_MODEL // HEADS) ** (-0.5)

        def _rel_pos_bucket_causal(seq_len):
            pos = jnp.arange(seq_len)
            n = jnp.maximum(pos[:, None] - pos[None, :], 0)
            max_exact = NUM_BUCKETS // 2
            val_large = max_exact + (jnp.log(jnp.maximum(n, 1).astype(jnp.float32) / max_exact) / math.log(MAX_DISTANCE / max_exact) * (NUM_BUCKETS - max_exact)).astype(jnp.int32)
            val_large = jnp.minimum(val_large, NUM_BUCKETS - 1)
            return jnp.where(n < max_exact, n, val_large)
        key = jax.random.key(seed)
        ks = jax.random.split(key, 6)
        s = 0.02
        return {'x': jax.random.normal(ks[0], (BATCH, SEQ, D_MODEL), jnp.float32), 'Wq': jax.random.normal(ks[1], (D_MODEL, D_MODEL), jnp.float32) * s, 'bq': jnp.zeros((D_MODEL,), jnp.float32), 'Wk': jax.random.normal(ks[2], (D_MODEL, D_MODEL), jnp.float32) * s, 'bk': jnp.zeros((D_MODEL,), jnp.float32), 'Wv': jax.random.normal(ks[3], (D_MODEL, D_MODEL), jnp.float32) * s, 'bv': jnp.zeros((D_MODEL,), jnp.float32), 'Wo': jax.random.normal(ks[4], (D_MODEL, D_MODEL), jnp.float32) * s, 'bo': jnp.zeros((D_MODEL,), jnp.float32), 'rel_emb': jax.random.normal(ks[5], (NUM_BUCKETS, HEADS), jnp.float32) * s}
    _L0_attn_a_in = _L0_attn_a_setup()

    def _L0_attn_b_setup():
        import jax, jax.numpy as jnp
        import numpy as np
        B, T, C = (4, 128, 128)
        H = 16
        DH = C // H
        key = jax.random.key(seed)
        ks = jax.random.split(key, 10)
        s = 0.02
        return {'x': jax.random.normal(ks[0], (B, T, C), dtype=jnp.float32), 'Wq': jax.random.normal(ks[1], (C, C), dtype=jnp.float32) * s, 'bq': jnp.zeros((C,), dtype=jnp.float32), 'Wk': jax.random.normal(ks[2], (C, C), dtype=jnp.float32) * s, 'bk': jnp.zeros((C,), dtype=jnp.float32), 'Wv': jax.random.normal(ks[3], (C, C), dtype=jnp.float32) * s, 'bv': jnp.zeros((C,), dtype=jnp.float32), 'Wp': jax.random.normal(ks[4], (C, C), dtype=jnp.float32) * s, 'bp': jnp.zeros((C,), dtype=jnp.float32)}
    _L0_attn_b_in = _L0_attn_b_setup()

    def _L0_ffn_setup():
        import jax, jax.numpy as jnp
        import numpy as np
        B, S, DIM = (4, 256, 128)
        E, K, HID = (8, 2, 512)
        key = jax.random.key(seed)
        ks = jax.random.split(key, 8)
        init = lambda k, sh: jax.random.normal(k, sh, jnp.float32) * 0.02
        return {'x': jax.random.normal(ks[0], (B, S, DIM), jnp.float32), 'gate_w': init(ks[1], (DIM, E)), 'gate_b': jnp.zeros((E,), jnp.float32), 'w1': init(ks[2], (E, DIM, HID)), 'b1': jnp.zeros((E, HID), jnp.float32), 'w2': init(ks[3], (E, HID, DIM)), 'b2': jnp.zeros((E, DIM), jnp.float32), 'ws1': init(ks[4], (DIM, HID)), 'bs1': jnp.zeros((HID,), jnp.float32), 'ws2': init(ks[5], (HID, DIM)), 'bs2': jnp.zeros((DIM,), jnp.float32)}
    _L0_ffn_in = _L0_ffn_setup()
    _d = {'L0_attn_a_x': _L0_attn_a_in['x'], 'L0_attn_a_Wq': _L0_attn_a_in['Wq'], 'L0_attn_a_bq': _L0_attn_a_in['bq'], 'L0_attn_a_Wk': _L0_attn_a_in['Wk'], 'L0_attn_a_bk': _L0_attn_a_in['bk'], 'L0_attn_a_Wv': _L0_attn_a_in['Wv'], 'L0_attn_a_bv': _L0_attn_a_in['bv'], 'L0_attn_a_Wo': _L0_attn_a_in['Wo'], 'L0_attn_a_bo': _L0_attn_a_in['bo'], 'L0_attn_a_rel_emb': _L0_attn_a_in['rel_emb'], 'L0_attn_b_Wq': _L0_attn_b_in['Wq'], 'L0_attn_b_bq': _L0_attn_b_in['bq'], 'L0_attn_b_Wk': _L0_attn_b_in['Wk'], 'L0_attn_b_bk': _L0_attn_b_in['bk'], 'L0_attn_b_Wv': _L0_attn_b_in['Wv'], 'L0_attn_b_bv': _L0_attn_b_in['bv'], 'L0_attn_b_Wp': _L0_attn_b_in['Wp'], 'L0_attn_b_bp': _L0_attn_b_in['bp'], 'L0_ffn_gate_w': _L0_ffn_in['gate_w'], 'L0_ffn_gate_b': _L0_ffn_in['gate_b'], 'L0_ffn_w1': _L0_ffn_in['w1'], 'L0_ffn_b1': _L0_ffn_in['b1'], 'L0_ffn_w2': _L0_ffn_in['w2'], 'L0_ffn_b2': _L0_ffn_in['b2'], 'L0_ffn_ws1': _L0_ffn_in['ws1'], 'L0_ffn_bs1': _L0_ffn_in['bs1'], 'L0_ffn_ws2': _L0_ffn_in['ws2'], 'L0_ffn_bs2': _L0_ffn_in['bs2']}
    _x0 = _d['L0_attn_a_x']
    _d['L0_attn_a_x'] = jax.random.normal(jax.random.fold_in(jax.random.key(seed), 1), (8, 512, 128), dtype=_x0.dtype)
    del _x0
    return _d

def reference(L0_attn_a_x, L0_attn_a_Wq, L0_attn_a_bq, L0_attn_a_Wk, L0_attn_a_bk, L0_attn_a_Wv, L0_attn_a_bv, L0_attn_a_Wo, L0_attn_a_bo, L0_attn_a_rel_emb, L0_attn_b_Wq, L0_attn_b_bq, L0_attn_b_Wk, L0_attn_b_bk, L0_attn_b_Wv, L0_attn_b_bv, L0_attn_b_Wp, L0_attn_b_bp, L0_ffn_gate_w, L0_ffn_gate_b, L0_ffn_w1, L0_ffn_b1, L0_ffn_w2, L0_ffn_b2, L0_ffn_ws1, L0_ffn_bs1, L0_ffn_ws2, L0_ffn_bs2):

    def _L0_attn_a_ref(x, Wq, bq, Wk, bk, Wv, bv, Wo, bo, rel_emb):
        import math
        import jax, jax.numpy as jnp
        import numpy as np
        NUM_BUCKETS = 32
        MAX_DISTANCE = 128
        HEADS = 16
        D_MODEL = 128
        SEQ = 128
        BATCH = 4
        SCALE = (D_MODEL // HEADS) ** (-0.5)

        def _rel_pos_bucket_causal(seq_len):
            pos = jnp.arange(seq_len)
            n = jnp.maximum(pos[:, None] - pos[None, :], 0)
            max_exact = NUM_BUCKETS // 2
            val_large = max_exact + (jnp.log(jnp.maximum(n, 1).astype(jnp.float32) / max_exact) / math.log(MAX_DISTANCE / max_exact) * (NUM_BUCKETS - max_exact)).astype(jnp.int32)
            val_large = jnp.minimum(val_large, NUM_BUCKETS - 1)
            return jnp.where(n < max_exact, n, val_large)
        b, n, d = x.shape
        h, hd = (HEADS, d // HEADS)
        q = (x @ Wq.T + bq).reshape(b, n, h, hd).transpose(0, 2, 1, 3)
        k = (x @ Wk.T + bk).reshape(b, n, h, hd).transpose(0, 2, 1, 3)
        v = (x @ Wv.T + bv).reshape(b, n, h, hd).transpose(0, 2, 1, 3)
        sim = jnp.einsum('bhid,bhjd->bhij', q, k)
        rp_bucket = _rel_pos_bucket_causal(n)
        bias = rel_emb[rp_bucket]
        sim = sim + jnp.transpose(bias, (2, 0, 1)) * SCALE
        i = jnp.arange(n)
        causal = jnp.where(i[None, :] > i[:, None], -jnp.inf, 0.0).astype(sim.dtype)
        sim = sim + causal
        attn = jax.nn.softmax(sim, axis=-1)
        out = jnp.einsum('bhij,bhjd->bhid', attn, v)
        out = out.transpose(0, 2, 1, 3).reshape(b, n, d)
        return out @ Wo.T + bo

    def _L0_attn_b_ref(x, Wq, bq, Wk, bk, Wv, bv, Wp, bp):
        import jax, jax.numpy as jnp
        import numpy as np
        B, T, C = (4, 128, 128)
        H = 16
        DH = C // H
        b, t, c = x.shape

        def heads(y):
            return y.reshape(b, t, H, DH).transpose(0, 2, 1, 3)
        q = heads(x @ Wq + bq)
        k = heads(x @ Wk + bk)
        v = heads(x @ Wv + bv)
        scores = jnp.einsum('bhqd,bhkd->bhqk', q, k) * DH ** (-0.5)
        causal = jnp.tril(jnp.ones((t, t), dtype=bool))
        scores = jnp.where(causal, scores, -jnp.inf)
        attn = jax.nn.softmax(scores, axis=-1)
        ctx = jnp.einsum('bhqk,bhkd->bhqd', attn, v)
        ctx = ctx.transpose(0, 2, 1, 3).reshape(b, t, c)
        return ctx @ Wp + bp

    def _L0_ffn_ref(x, gate_w, gate_b, w1, b1, w2, b2, ws1, bs1, ws2, bs2):
        import jax, jax.numpy as jnp
        import numpy as np
        B, S, DIM = (4, 256, 128)
        E, K, HID = (8, 2, 512)
        orig_shape = x.shape
        xf = x.reshape(-1, DIM)
        logits = xf @ gate_w + gate_b
        top_w, top_i = jax.lax.top_k(logits, K)
        gw = jax.nn.softmax(top_w, axis=-1).astype(xf.dtype)
        combine = (gw[:, :, None] * jax.nn.one_hot(top_i, E, dtype=xf.dtype)).sum(axis=1)
        out = jnp.zeros_like(xf)
        for e in range(E):
            h = jax.nn.gelu(xf @ w1[e] + b1[e], approximate=False)
            out = out + combine[:, e:e + 1] * (h @ w2[e] + b2[e])
        shared = jax.nn.gelu(xf @ ws1 + bs1, approximate=False) @ ws2 + bs2
        return (out + shared).reshape(orig_shape)
    x = L0_attn_a_x
    x = x + _L0_attn_a_ref(_layernorm(x, axis=-1), L0_attn_a_Wq, L0_attn_a_bq, L0_attn_a_Wk, L0_attn_a_bk, L0_attn_a_Wv, L0_attn_a_bv, L0_attn_a_Wo, L0_attn_a_bo, L0_attn_a_rel_emb)
    x = x + _L0_ffn_ref(_layernorm(x, axis=-1), L0_ffn_gate_w, L0_ffn_gate_b, L0_ffn_w1, L0_ffn_b1, L0_ffn_w2, L0_ffn_b2, L0_ffn_ws1, L0_ffn_bs1, L0_ffn_ws2, L0_ffn_bs2)
    x = x + _L0_attn_b_ref(_layernorm(x, axis=-1), L0_attn_b_Wq, L0_attn_b_bq, L0_attn_b_Wk, L0_attn_b_bk, L0_attn_b_Wv, L0_attn_b_bv, L0_attn_b_Wp, L0_attn_b_bp)
    x = x + _L0_ffn_ref(_layernorm(x, axis=-1), L0_ffn_gate_w, L0_ffn_gate_b, L0_ffn_w1, L0_ffn_b1, L0_ffn_w2, L0_ffn_b2, L0_ffn_ws1, L0_ffn_bs1, L0_ffn_ws2, L0_ffn_bs2)
    return x

_drawn_inputs = setup_inputs


def setup_inputs(seed=0):
    import zlib

    import numpy as np

    out = dict(_drawn_inputs(seed))
    spreads = {'L0_attn_a_bq': (0.0, 0.8),
     'L0_attn_a_bk': (0.0, 2.0),
     'L0_attn_a_bv': (0.0, 0.269),
     'L0_attn_a_bo': (0.0, 0.1),
     'L0_attn_b_bq': (0.0, 0.8),
     'L0_attn_b_bk': (0.0, 2.0),
     'L0_attn_b_bv': (0.0, 0.304),
     'L0_attn_b_bp': (0.0, 0.1),
     'L0_ffn_gate_b': (0.0, 0.1),
     'L0_ffn_b1': (0.0, 0.1),
     'L0_ffn_b2': (0.0, 0.1),
     'L0_ffn_bs1': (0.0, 0.1),
     'L0_ffn_bs2': (0.0, 0.1)}
    factors = {'L0_attn_a_Wq': 8.0,
     'L0_attn_a_Wk': 8.0,
     'L0_attn_a_Wv': 6.466,
     'L0_attn_a_rel_emb': 64.0,
     'L0_attn_b_Wq': 8.0,
     'L0_attn_b_Wk': 8.0,
     'L0_attn_b_Wv': 5.107}
    for name, (base, spread) in spreads.items():
        noise = np.random.default_rng([zlib.crc32(name.encode()), seed]).standard_normal(out[name].shape)
        drawn = base * np.exp(spread * noise) if base else spread * noise
        out[name] = jnp.asarray(drawn.astype(out[name].dtype))
    for name, factor in factors.items():
        out[name] = (out[name] * factor).astype(out[name].dtype)
    return out
```

```python
from contextlib import ExitStack

import concourse.bass as bass
from concourse import mybir

F32 = mybir.dt.float32
F32R = mybir.dt.float32r
BF16 = mybir.dt.bfloat16
ALU = mybir.AluOpType
ACT = mybir.ActivationFunctionType
AX = mybir.AxisListType

P = 128
NB, SEQ, D = 8, 512, 128
KB = SEQ // P
NBLK = NB * KB
H, HD = 16, 8
HH = H // 2
NGRP = H // 4
E, NE, HID = 8, 9, 512
HC = HID // P
BUCKETS, MAX_DIST = 32, 128
NV = 3 * P
EPS = 1e-5
MASK = -1e30
SCALE = float(HD) ** -0.5
PQ = [0, 0, 0, 1, 1, 2]
PK = [0, 1, 2, 0, 1, 0]
NTERM = len(PQ)
MROW = 96
KROWS = MROW + 3
NPB = 8
PW = SEQ + (SEQ - P) + P + (SEQ - 2 * P)
PCOL = {0: (0, 0), 1: (SEQ, P), 3: (2 * SEQ - P, 3 * P), 2: (2 * SEQ, 2 * P)}
ROWBANKS = [[(3, 0, 512)], [(2, 0, 384), (0, 384, 128)], [(1, 0, 256)]]
COLBANKS = [[(0, 0, 512)], [(1, 0, 384), (3, 384, 128)], [(2, 0, 256)]]


def settle(eng, passed):
    eng.sem_inc(passed, 1)


class Core:

    def __init__(self, nc, ctx, prefix):
        self.nc, self.ctx, self.prefix = nc, ctx, prefix

    def sb(self, name, shape, dt=F32):
        return self.ctx.enter_context(self.nc.sbuf_tensor(f"{self.prefix}_{name}", shape, dt))

    def bank(self, name, dt=F32):
        return self.ctx.enter_context(self.nc.psum_tensor(f"{self.prefix}_{name}_ps", [P, 2048 // (4 if dt == F32 else 2)], dt))

    def sem(self, name):
        return self.ctx.enter_context(self.nc.semaphore(f"{self.prefix}_{name}"))


def load_constants(nc, ctx, x, resid, ident, identb, half_power):
    c = Core(nc, ctx, "init")
    loaded, zeroed, made = c.sem("loaded"), c.sem("zeroed"), c.sem("made")
    block = ctx.enter_context(nc.Block())
    rows = x.rearrange("b (k p) d -> p (b k) d", p=P)

    @block.sync
    def _(sp):
        sp.dma_start(resid[:, 0:NBLK // 2, :], rows[:, 0:NBLK // 2, :]).then_inc(loaded, 16)
        sp.dma_start(resid[:, NBLK // 2:, :], rows[:, NBLK // 2:, :]).then_inc(loaded, 16)
        sp.wait_ge(loaded, 32)

    @block.gpsimd
    def _(pool):
        nc.gpsimd.memset(half_power[:], -0.5)
        nc.gpsimd.memset(ident[:], 0.0).then_inc(zeroed, 1)
        nc.gpsimd.memset(identb[:], 0.0).then_inc(zeroed, 1)
        pool.wait_ge(zeroed, 2)
        for m in (ident, identb):
            nc.gpsimd.affine_select(out=m[:], in_=m[:], compare_op=ALU.not_equal, fill=1.0, base=0,
                                    pattern=[[-1, P]], channel_multiplier=1).then_inc(made, 1)


def relative_tables(nc, c, ctx, rel_emb, onehot, scratch, keybias, rowbias):
    COP = 16
    rel = c.sb("rel", [BUCKETS, H])
    hot = c.sb("hot", [BUCKETS, 2, NV])
    far = c.sb("far", [H, 1])
    vec = c.sb("vec", [H, 2, NV])
    rest = c.sb("rest", [H, NV])
    rest2 = c.sb("rest2", [H, NV])
    parts = c.sb("parts", [H, 4, NV], BF16)
    up, down = c.bank("up"), c.bank("down")
    loaded, vec_ps, chain = c.sem("rel_loaded"), c.sem("rel_vec_ps"), c.sem("rel_chain")
    stored, spread, zeros = c.sem("rel_stored"), c.sem("rel_spread"), c.sem("rel_zeros")
    block = ctx.enter_context(nc.Block())

    @block.sync
    def _(sp):
        sp.dma_start(rel[:], rel_emb).then_inc(loaded, 16)
        sp.dma_start(hot[:], onehot.rearrange("t b n -> b t n")).then_inc(loaded, 16)
        sp.wait_ge(chain, 8)
        dst = scratch.rearrange("t h c n -> h t c n")
        for t in range(4):
            sp.dma_start(dst[:, t], parts[:, t, :].unsqueeze(1).broadcast_to([H, COP, NV])).then_inc(stored, 16)
        sp.wait_ge(stored, 64)
        n = 0
        for a in range(P // COP):
            for t in (3, 0, 1, 2):
                src = bass.AP(scratch.tensor, t * H * COP * NV + P - 1 - COP * a,
                              [[NV - 1, COP], [COP * NV, H], [1, 2 * P]])
                into = slice(COP * a, COP * (a + 1))
                dst = rowbias[into, :, 2 * P:] if t == 3 else keybias[into, :, t, :]
                sp.dma_start(dst, src).then_inc(spread, 16)
                n += 16
        sp.wait_ge(spread, n)

    @block.gpsimd
    def _(pool):
        nc.gpsimd.memset(rowbias[:, :, 0:2 * P], 0.0).then_inc(zeros, 1)

    @block.tensor
    def _(pe):
        pe.wait_ge(loaded, 32)
        nc.tensor.matmul(up[0:H, 0:NV], rel[:], hot[:, 0, :], start=True, stop=True).then_inc(vec_ps, 1)
        nc.tensor.matmul(down[0:H, 0:NV], rel[:], hot[:, 1, :], start=True, stop=True).then_inc(vec_ps, 1)

    @block.vector
    def _(dve):
        done = [0]

        def link(ins):
            done[0] += 1
            ins.then_inc(chain, 1)
            dve.wait_ge(chain, done[0])

        dve.wait_ge(vec_ps, 2)
        link(nc.vector.tensor_copy(far[:], up[0:H, NV - 1:NV]))
        nc.vector.tensor_scalar(vec[:, 0, :], up[0:H, 0:NV], far[:, 0:1], SCALE, ALU.subtract, ALU.mult)
        link(nc.vector.tensor_scalar(vec[:, 1, :], down[0:H, 0:NV], far[:, 0:1], SCALE, ALU.subtract, ALU.mult))
        nc.vector.memset(vec[:, 0, 0:P - 1], MASK)
        link(nc.vector.memset(vec[:, 1, 2 * P:], MASK))
        nc.vector.tensor_copy(parts[:, 3, :], vec[:, 1, :])
        link(nc.vector.tensor_copy(parts[:, 0, :], vec[:, 0, :]))
        link(nc.vector.tensor_tensor(rest[:], vec[:, 0, :], parts[:, 0, :], ALU.subtract))
        link(nc.vector.tensor_copy(parts[:, 1, :], rest[:]))
        link(nc.vector.tensor_tensor(rest2[:], rest[:], parts[:, 1, :], ALU.subtract))
        link(nc.vector.tensor_copy(parts[:, 2, :], rest2[:]))


def causal_tables(nc, c, ctx, keymask, rowmask):
    zeros = c.sem("mask_zeros")
    block = ctx.enter_context(nc.Block())

    @block.gpsimd
    def _(pool):
        nc.gpsimd.memset(keymask[:], 0.0).then_inc(zeros, 1)
        nc.gpsimd.memset(rowmask[:], 0.0).then_inc(zeros, 1)
        pool.wait_ge(zeros, 2)
        nc.gpsimd.affine_select(out=keymask[:], in_=keymask[:], compare_op=ALU.is_ge, fill=MASK, base=0,
                                pattern=[[1, P]], channel_multiplier=-1)
        nc.gpsimd.affine_select(out=rowmask[:, 3 * P:], in_=rowmask[:, 3 * P:], compare_op=ALU.is_ge, fill=MASK,
                                base=0, pattern=[[-1, P]], channel_multiplier=1)


def attention(nc, name, resid, ident, identb, half_power, w, relative, scratch, maxima):
    with ExitStack() as ctx:
        c = Core(nc, ctx, name)
        scale = 1.0 if relative else SCALE
        NPART = 3 if relative else 1
        if relative:
            keybias = c.sb("keybias", [P, H, 3, 2 * P], BF16)
            rowbias = c.sb("rowbias", [P, H, SEQ], BF16)
        else:
            keybias = c.sb("keymask", [P, P], BF16)
            rowbias = c.sb("rowmask", [P, SEQ], BF16)
        with ExitStack() as inner:
            ci = Core(nc, inner, name + "t")
            if relative:
                relative_tables(nc, ci, inner, relative[0], relative[1], relative[2], keybias, rowbias)
            else:
                causal_tables(nc, ci, inner, keybias, rowbias)

        qs = [c.sb(f"qs{i}", [P, H, SEQ], BF16) for i in range(2)]
        ks = [c.sb(f"ks{i}", [P, H, SEQ], BF16) for i in range(2)]
        wt = {n: c.sb(n, [P, D]) for n in ("wq", "wk", "wv", "wo")}
        bias_q, bias_k = c.sb("bias_q", [P, 1]), c.sb("bias_k", [P, 1])
        bias_qs = c.sb("bias_qs", [P, 1])
        bias_v, bias_o = c.sb("bias_v", [P, D]), c.sb("bias_o", [P, D])
        stats = c.sb("stats", [P, KB, 6])
        meanvar = c.sb("meanvar", [P, KB, 2])
        var_eps = c.sb("var_eps", [P, KB])
        rstd = c.sb("rstd", [P, KB])
        xn = c.sb("xn", [P, KB, D])
        xnT = [c.sb(f"xnT{i}", [P, SEQ]) for i in range(2)]
        qk32 = [c.sb(f"qk32_{i}", [P, SEQ]) for i in range(2)]
        rest = c.sb("rest", [P, SEQ])
        qkp = [c.sb(f"qkp{i}", [P, 3, SEQ], BF16) for i in range(2)]
        vaug = [c.sb(f"vaug{i}", [P, KB, H, 32]) for i in range(2)]
        rowmax = c.sb("rowmax", [P, H, KB])
        mrest = c.sb("mrest", [P, 2, KB, HH])
        mparts = c.sb("mparts", [P, KB, 3, HH], BF16)
        mT = c.sb("mT", [3 * HH, SEQ], BF16)
        prob = [c.sb(f"prob{i}", [P, PW]) for i in range(NPB)]
        osb = [c.sb(f"osb{i}", [P, SEQ]) for i in range(2)]
        rsum = c.sb("rsum", [P, KB * 4])
        ctxn = c.sb("ctxn", [P, KB, H, HD])
        ctxT = c.sb("ctxT", [P, SEQ])

        row_ps = [c.bank(f"row{i}") for i in range(3)]
        col_ps = [c.bank(f"col{i}") for i in range(3)]
        out_ps = c.bank("out")
        work = c.bank("work")

        names = ("w_loaded zeroed setup bq_scaled ln_stats ln_mv ln_eps ln_rstd xn_ready qk_chain split_q split_k "
                 "scr_written half0_loaded half1_loaded row_full row_read m_chain m_split m_stored m_loaded col_full exp_done "
                 "dve_passed pool_passed pv_done out_read work_full work_read r_ready bias_added").split()
        s = {n: c.sem(n) for n in names}
        block = ctx.enter_context(nc.Block())

        SLOTS = [(1, "turn_ctx", 3, "old"), (2, "turn_max", 1, "cur"), (3, "turn_out", 0, "old"), (4, "project", 0, "old"),
                 (5, "turn_ctx", 0, "cur"), (6, "turn_x", 0, "new2"), (7, "q", 0, "new2"), (8, "k", 0, "new2"),
                 (9, "turn_ctx", 1, "cur"), (10, "turn_max", 0, "new"), (11, "v", 0, "new"), (13, "turn_ctx", 2, "cur")]

        def valid(b, which):
            n = {"old": b - 1, "cur": b, "new": b + 1, "new2": b + 2}[which]
            return 0 <= n < NB

        uses = {b: [u for u in SLOTS if valid(b, u[3])] for b in range(-2, NB + 1)}
        first_use, total = {}, 0
        for b in range(-2, NB + 1):
            first_use[b] = total
            total += len(uses[b])
        LOOP0, LOOPS = 1, 2

        def run(eng, step):
            for b in range(-2, LOOP0):
                step(b, b, first_use[b])
            with eng.Fori(0, LOOPS) as i:
                for r in range(2):
                    step(i * 2 + LOOP0 + r, LOOP0 + r, i * (2 * len(SLOTS)) + first_use[LOOP0 + r])
            for b in range(LOOP0 + 2 * LOOPS, NB + 1):
                step(b, b, first_use[b])

        def work_uses(kind_b, base, slot):
            for n, u in enumerate(uses[kind_b]):
                if u[0] == slot:
                    yield u, base + n

        def earlier(like, base, what, arg):
            before = uses[like - 1]
            at = [n for n, u in enumerate(before) if u[1:3] == (what, arg)][0]
            return base - len(before) + at

        def number_of(like, base, what, arg):
            return base + [n for n, u in enumerate(uses[like]) if u[1:3] == (what, arg)][0]

        def batch_of(b, which):
            return b + {"old": -1, "cur": 0, "new": 1, "new2": 2}[which]

        @block.sync
        def _(sp):
            for n in ("wq", "wk", "wv", "wo"):
                sp.dma_start(wt[n][:], w[n]).then_inc(s["w_loaded"], 16)
            sp.dma_start(bias_q[:], w["bq"].unsqueeze(1)).then_inc(s["w_loaded"], 16)
            sp.dma_start(bias_k[:], w["bk"].unsqueeze(1)).then_inc(s["w_loaded"], 16)
            sp.dma_start(bias_v[:], w["bv"].partition_broadcast(P)).then_inc(s["w_loaded"], 16)
            sp.dma_start(bias_o[:], w["bo"].partition_broadcast(P)).then_inc(s["w_loaded"], 16)

            def load_half(m, par, half):
                for which, (dst, pick) in enumerate(((qs[par], PQ), (ks[par], PK))):
                    for t, part in enumerate(pick):
                        src = scratch[par, which].rearrange("(h d) q n -> q d h n", d=HD)[part]
                        sp.dma_start(dst[HD * t:HD * (t + 1), HH * half:HH * (half + 1), :],
                                     src[:, HH * half:HH * (half + 1), :]).then_inc(s[f"half{half}_loaded"], 16)

            def load_max(number, par, half, stored):
                sp.wait_ge(s["work_read"], number + 1)
                sp.dma_start(maxima[half], mT[:]).then_inc(s["m_stored"], 16)
                sp.wait_ge(s["m_stored"], stored)
                sp.dma_start(qs[par][MROW:MROW + 3, HH * half:HH * (half + 1), :],
                             maxima[half].rearrange("(a h) q -> a h q", a=3)).then_inc(s["m_loaded"], 16)

            def step(b, like, base):
                par = like % 2
                if 0 <= like < NB:
                    load_max(number_of(like, base, "turn_max", 1), par, 1, b * 32 + 32)
                if 0 <= like + 2 < NB:
                    m = b + 2
                    for which in range(2):
                        sp.wait_ge(s["split_q" if which == 0 else "split_k"], m + 1)
                        sp.dma_start(scratch[par, which], qkp[which][:]).then_inc(s["scr_written"], 16)
                    sp.wait_ge(s["scr_written"], (m + 1) * 32)
                    if like == -2 or like == -1:
                        sp.wait_ge(s["setup"], 4)
                    if like >= 0:
                        sp.wait_ge(s["col_full"], b * (3 * H) + 3 * HH)
                    load_half(m, par, 0)
                if 0 <= like + 1 < NB:
                    load_max(number_of(like, base, "turn_max", 0), 1 - par, 0, b * 32 + 48)
                if 0 <= like + 2 < NB:
                    if like >= 0:
                        sp.wait_ge(s["col_full"], b * (3 * H) + 3 * H)
                    load_half(b + 2, par, 1)

            run(sp, step)
            sp.wait_ge(s["w_loaded"], 128)

        @block.gpsimd
        def _(pool):
            for t in (*qs, *ks, *vaug):
                nc.gpsimd.memset(t[:], 0.0).then_inc(s["zeroed"], 1)
            pool.wait_ge(s["zeroed"], 6)
            for t in ks:
                nc.gpsimd.memset(t[MROW:P, :, :], 1.0).then_inc(s["setup"], 1)
            pool.wait_ge(s["setup"], 2)
            for v in vaug:
                nc.gpsimd.memset(v[:, :, :, HD:HD + 1], 1.0).then_inc(s["setup"], 1)
            pool.wait_ge(s["w_loaded"], 128)
            nc.gpsimd.tensor_scalar(bias_qs[:], bias_q[:], scale, None, ALU.mult).then_inc(s["bq_scaled"], 1)

            def step(b, like, base):
                if 0 <= like + 2 < NB:
                    m = b + 2
                    pool.wait_ge(s["ln_mv"], m + 1)
                    settle(pool, s["pool_passed"])
                    nc.gpsimd.tensor_scalar(var_eps[:], meanvar[:, :, 1], EPS, None, ALU.add).then_inc(s["ln_eps"], 1)
                    pool.wait_ge(s["ln_eps"], m + 1)
                    nc.gpsimd.tensor_tensor(rstd[:], var_eps[:], half_power[:], ALU.pow).then_inc(s["ln_rstd"], 1)
                    pool.wait_ge(s["xn_ready"], m + 1)
                    for k in range(KB):
                        ins = nc.gpsimd.tensor_tensor(resid[:, bass.ds(m * KB + k, 1), :].squeeze(1),
                                                      resid[:, bass.ds(m * KB + k, 1), :].squeeze(1),
                                                      bias_o[:], ALU.add)
                    ins.then_inc(s["bias_added"], 1)

            run(pool, step)

        @block.tensor
        def _(pe):
            pe.wait_ge(s["w_loaded"], 128)
            pe.wait_ge(s["setup"], 4)

            def rows(n, par, h):
                if h % HH == 0:
                    pe.wait_ge(s[f"half{h // HH}_loaded"], (n + 1) * (2 * NTERM * 16))
                for i, held in enumerate(ROWBANKS):
                    if not (isinstance(n, int) and n == 0 and h == 0):
                        pe.wait_ge(s["row_read"], n * (3 * H) + 3 * (h - 1) + i + 1)
                    for blk, col, width in held:
                        ins = nc.tensor.matmul(row_ps[i][:, col:col + width], qs[par][0:MROW, h, P * blk:P * (blk + 1)],
                                               ks[par][0:MROW, h, 0:width], start=True, stop=True)
                    ins.then_inc(s["row_full"], 1)

            def cols(b, par, h):
                if h % HH == 0:
                    pe.wait_ge(s["m_loaded"], b * 32 + (h // HH + 1) * 16)
                for i, held in enumerate(COLBANKS):
                    if not (isinstance(b, int) and b == 0 and h == 0):
                        pe.wait_ge(s["exp_done"], b * (3 * H) + 3 * (h - 1) + i + 1)
                    for n, (blk, col, width) in enumerate(held):
                        nc.tensor.matmul(col_ps[i][:, col:col + width], ks[par][0:KROWS, h, P * blk:P * (blk + 1)],
                                         qs[par][0:KROWS, h, P * blk:P * blk + width],
                                         start=(n == 0), stop=False, skip_group_check=True)
                    for n, (blk, col, width) in enumerate(held):
                        wide = min(width, 2 * P) if relative else P
                        for part in range(NPART):
                            bias = keybias[:, h, part, 0:wide] if relative else keybias[:, :]
                            ins = nc.tensor.matmul(col_ps[i][:, col:col + wide], identb[:], bias, start=False,
                                                   stop=(part == NPART - 1), skip_group_check=True)
                    ins.then_inc(s["col_full"], 1)

            def values(b, par, g):
                pe.wait_ge(s["exp_done"], b * (3 * H) + 12 * (g + 1))
                if not (isinstance(b, int) and b == 0 and g == 0):
                    pe.wait_ge(s["out_read"], b * NGRP + g)
                for j in (0, 1, 2, 3):
                    pcol, q0 = PCOL[j]
                    for t in range(4):
                        h = 4 * g + t
                        ins = nc.tensor.matmul(out_ps[32 * t:32 * (t + 1), q0:SEQ], vaug[par][:, j, h, :],
                                               prob[h % NPB][:, pcol:pcol + SEQ - q0],
                                               start=(j == 0), stop=(j == 3), skip_group_check=True)
                ins.then_inc(s["pv_done"], 1)

            def use(u, number, b, par):
                _, what, arg, which = u
                n = batch_of(b, which)
                npar = (par + {"old": 1, "cur": 0, "new": 1, "new2": 0}[which]) % 2
                if not (isinstance(number, int) and number == 0):
                    pe.wait_ge(s["work_read"], number)
                if what == "turn_x":
                    pe.wait_ge(s["xn_ready"], n + 1)
                    for k in range(KB):
                        ins = nc.tensor.transpose(work[:, P * k:P * (k + 1)], xn[:, k, :], ident[:])
                elif what in "qk":
                    ins = nc.tensor.matmul(work[:], wt["w" + what][:], xnT[npar][:], start=True, stop=True)
                elif what == "v":
                    for k in range(KB):
                        ins = nc.tensor.matmul(work[:, P * k:P * (k + 1)], xnT[npar][:, P * k:P * (k + 1)], wt["wv"][:],
                                               start=True, stop=True)
                elif what == "turn_max":
                    pe.wait_ge(s["m_split"], 2 * n + arg + 1)
                    view = work[0:3 * HH, :].bitcast(BF16)
                    for k in range(KB):
                        ins = nc.tensor.transpose(view[:, P * k:P * (k + 1)],
                                                  mparts[:, k].rearrange("p a h -> p (a h)"), identb[:])
                elif what == "turn_ctx":
                    pe.wait_ge(s["out_read"], n * NGRP + arg + 1)
                    for k in range(KB):
                        ins = nc.tensor.transpose(work[:, P * k:P * (k + 1)], osb[arg % 2][:, P * k:P * (k + 1)], ident[:])
                elif what == "turn_out":
                    for k in range(KB):
                        ins = nc.tensor.transpose(work[:, P * k:P * (k + 1)],
                                                  ctxn[:, k].rearrange("p h d -> p (h d)"), ident[:])
                elif what == "project":
                    for k in range(KB):
                        ins = nc.tensor.matmul(work[:, P * k:P * (k + 1)], ctxT[:, P * k:P * (k + 1)], wt["wo"][:],
                                               start=True, stop=True)
                ins.then_inc(s["work_full"], 1)

            def step(b, like, base):
                par = like % 2
                for h in range(H):
                    if 0 <= like < NB:
                        cols(b, par, h)
                    if 0 <= like + 1 < NB:
                        rows(b + 1, 1 - par, h)
                    if h == 0 and 0 <= like - 1 < NB:
                        values(b - 1, 1 - par, 3)
                    if h in (4, 8, 12) and 0 <= like < NB:
                        values(b, par, h // 4 - 1)
                    for u, number in work_uses(like, base, h):
                        use(u, number, b, par)

            run(pe, step)

        @block.scalar
        def _(act):
            act.wait_ge(s["w_loaded"], 128)
            act.wait_ge(s["bq_scaled"], 1)

            def probabilities(b, h):
                if h >= NPB or not (isinstance(b, int) and b == 0):
                    if h % 4 == 0:
                        act.wait_ge(s["pv_done"], b * NGRP + h // 4 - 1)
                for i in range(3):
                    act.wait_ge(s["col_full"], b * (3 * H) + 3 * h + i + 1)
                    width = sum(x[2] for x in COLBANKS[i])
                    nc.scalar.activation(prob[h % NPB][:, SEQ * i:SEQ * i + width], col_ps[i][:, 0:width],
                                         ACT.Exp).then_inc(s["exp_done"], 1)

            def outputs(b, g):
                act.wait_ge(s["pv_done"], b * NGRP + g + 1)
                nc.scalar.copy(osb[g % 2][:], out_ps[:]).then_inc(s["out_read"], 1)

            def read(u, number, b, par):
                _, what, arg, which = u
                n = batch_of(b, which)
                npar = (par + {"old": 1, "cur": 0, "new": 1, "new2": 0}[which]) % 2
                if what not in ("turn_x", "q", "k", "turn_max", "turn_out"):
                    return
                act.wait_ge(s["work_full"], number + 1)
                if what == "turn_x":
                    ins = nc.scalar.copy(xnT[npar][:], work[:])
                elif what == "q":
                    if not (isinstance(n, int) and n == 0):
                        act.wait_ge(s["split_q"], n)
                    ins = nc.scalar.activation(qk32[0][:], work[:], ACT.Identity, bias=bias_qs[:], scale=scale)
                elif what == "k":
                    if not (isinstance(n, int) and n == 0):
                        act.wait_ge(s["split_k"], n)
                    ins = nc.scalar.activation(qk32[1][:], work[:], ACT.Identity, bias=bias_k[:])
                elif what == "turn_max":
                    if not (isinstance(n, int) and n == 0 and arg == 0):
                        act.wait_ge(s["m_stored"], n * 32 + 16 * arg)
                    ins = nc.scalar.copy(mT[:], work[0:3 * HH, :].bitcast(BF16)[:, 0:SEQ])
                else:
                    ins = nc.scalar.copy(ctxT[:], work[:])
                ins.then_inc(s["work_read"], 1)

            def step(b, like, base):
                par = like % 2
                for h in range(H):
                    if 0 <= like < NB:
                        probabilities(b, h)
                    if h == 0 and 0 <= like - 1 < NB:
                        outputs(b - 1, 3)
                    if h in (4, 8, 12) and 0 <= like < NB:
                        outputs(b, h // 4 - 1)
                    for u, number in work_uses(like, base, h):
                        read(u, number, b, par)

            run(act, step)

        @block.vector
        def _(dve):
            def norm_stats(m):
                for k in range(KB):
                    ins = nc.vector.bn_stats(stats[:, k, :], resid[:, bass.ds(m * KB + k, 1), :].squeeze(1))
                ins.then_inc(s["ln_stats"], 1)
                dve.wait_ge(s["ln_stats"], m + 1)
                if not (isinstance(m, int) and m == 0):
                    dve.wait_ge(s["ln_rstd"], m)
                settle(dve, s["dve_passed"])
                for k in range(KB):
                    ins = nc.vector.bn_aggr(meanvar[:, k, :], stats[:, k, :])
                ins.then_inc(s["ln_mv"], 1)

            def norm(m):
                dve.wait_ge(s["ln_rstd"], m + 1)
                dve.wait_ge(s["ln_mv"], m + 1)
                for k in range(KB):
                    ins = nc.vector.tensor_scalar(xn[:, k, :], resid[:, bass.ds(m * KB + k, 1), :].squeeze(1),
                                                  meanvar[:, k, 0:1], rstd[:, k:k + 1], ALU.subtract, ALU.mult)
                ins.then_inc(s["xn_ready"], 1)

            def maxima(n, h):
                for i, held in enumerate(ROWBANKS):
                    dve.wait_ge(s["row_full"], n * (3 * H) + 3 * h + i + 1)
                    settle(dve, s["dve_passed"])
                    for blk, col, width in held:
                        bias = rowbias[:, h, SEQ - width:] if relative else rowbias[:, SEQ - width:]
                        ins = nc.vector.tensor_tensor_reduce(row_ps[i][:, col:col + width], row_ps[i][:, col:col + width], bias, 1.0,
                                                             MASK, ALU.add, ALU.max, rowmax[:, h, blk:blk + 1])
                    ins.then_inc(s["row_read"], 1)

            def split_max(n, half, turned):
                src = rowmax[:, HH * half:HH * (half + 1), :].rearrange("p h k -> p k h")
                dve.wait_ge(s["row_read"], n * (3 * H) + 3 * HH * (half + 1))
                at = n * 8 + 4 * half
                if turned is not None:
                    dve.wait_ge(s["work_read"], turned + 1)
                nc.vector.tensor_scalar(mparts[:, :, 0, :], src, -1.0, None, ALU.mult).then_inc(s["m_chain"], 1)
                dve.wait_ge(s["m_chain"], at + 1)
                nc.vector.scalar_tensor_tensor(mrest[:, 0], src, -1.0, mparts[:, :, 0, :], ALU.mult,
                                               ALU.subtract).then_inc(s["m_chain"], 1)
                dve.wait_ge(s["m_chain"], at + 2)
                nc.vector.tensor_copy(mparts[:, :, 1, :], mrest[:, 0]).then_inc(s["m_chain"], 1)
                dve.wait_ge(s["m_chain"], at + 3)
                nc.vector.tensor_tensor(mrest[:, 1], mrest[:, 0], mparts[:, :, 1, :], ALU.subtract).then_inc(s["m_chain"], 1)
                dve.wait_ge(s["m_chain"], at + 4)
                nc.vector.tensor_copy(mparts[:, :, 2, :], mrest[:, 1]).then_inc(s["m_split"], 1)

            def split_qk(m, which):
                x, p = qk32[which], qkp[which]
                at = m * 8 + 4 * which
                if not (isinstance(m, int) and m == 0):
                    dve.wait_ge(s["scr_written"], m * 32)
                nc.vector.tensor_copy(p[:, 0], x[:]).then_inc(s["qk_chain"], 1)
                dve.wait_ge(s["qk_chain"], at + 1)
                nc.vector.tensor_tensor(rest[:], x[:], p[:, 0], ALU.subtract).then_inc(s["qk_chain"], 1)
                dve.wait_ge(s["qk_chain"], at + 2)
                nc.vector.tensor_copy(p[:, 1], rest[:]).then_inc(s["qk_chain"], 1)
                dve.wait_ge(s["qk_chain"], at + 3)
                nc.vector.tensor_tensor(x[:], rest[:], p[:, 1], ALU.subtract).then_inc(s["qk_chain"], 1)
                dve.wait_ge(s["qk_chain"], at + 4)
                nc.vector.tensor_copy(p[:, 2], x[:]).then_inc(s["split_q" if which == 0 else "split_k"], 1)

            def read(u, number, b, par):
                _, what, arg, which = u
                n = batch_of(b, which)
                npar = (par + {"old": 1, "cur": 0, "new": 1, "new2": 0}[which]) % 2
                if what in "qk":
                    dve.wait_ge(s["work_read"], number + 1)
                    split_qk(n, "qk".index(what))
                elif what == "turn_ctx":
                    dve.wait_ge(s["work_full"], number + 1)
                    turned = work[:].rearrange("p (x c) -> p x c", c=32)
                    count = n * NGRP + arg
                    nc.vector.reciprocal(rsum[:], turned[:, :, HD]).then_inc(s["r_ready"], 1)
                    dve.wait_ge(s["r_ready"], count + 1)
                    inv = rsum[:].rearrange("p (k t) -> p k t", t=4)
                    for k in range(KB):
                        ins = nc.vector.tensor_tensor(ctxn[:, k, 4 * arg:4 * arg + 4, :], turned[:, 4 * k:4 * k + 4, 0:HD],
                                                      inv[:, k, :].unsqueeze(2).broadcast_to([P, 4, HD]), ALU.mult)
                    ins.then_inc(s["work_read"], 1)
                elif what == "v":
                    dve.wait_ge(s["work_full"], number + 1)
                    for k in range(KB):
                        ins = nc.vector.tensor_tensor(vaug[npar][:, k, :, 0:HD],
                                                      work[:, P * k:P * (k + 1)].rearrange("p (h d) -> p h d", d=HD),
                                                      bias_v[:].rearrange("p (h d) -> p h d", d=HD), ALU.add)
                    ins.then_inc(s["work_read"], 1)
                elif what == "project":
                    dve.wait_ge(s["work_full"], number + 1)
                    dve.wait_ge(s["bias_added"], n + 1)
                    for k in range(KB):
                        blk = resid[:, bass.ds(n * KB + k, 1), :].squeeze(1)
                        ins = nc.vector.tensor_tensor(blk, work[:, P * k:P * (k + 1)], blk, ALU.add)
                    ins.then_inc(s["work_read"], 1)

            dve.wait_ge(s["setup"], 4)
            dve.wait_ge(s["w_loaded"], 128)

            def step(b, like, base):
                par = like % 2
                if 0 <= like < NB:
                    split_max(b, 1, earlier(like, base, "turn_max", 0))
                for h in range(H):
                    if 0 <= like + 1 < NB:
                        maxima(b + 1, h)
                    if h == 9 and 0 <= like + 1 < NB:
                        split_max(b + 1, 0, number_of(like, base, "turn_max", 1) if like >= 0 else None)
                    if h == 2 and 0 <= like + 2 < NB:
                        norm_stats(b + 2)
                    if h == 4 and 0 <= like + 2 < NB:
                        norm(b + 2)
                    for u, number in work_uses(like, base, h):
                        read(u, number, b, par)

            run(dve, step)


def ffn(nc, name, resid, ident, identb, half_power, w):
    with ExitStack() as ctx:
        c = Core(nc, ctx, name)
        xh, xl = c.sb("xh", [P, NBLK * P], F32R), c.sb("xl", [P, NBLK * P], F32R)
        acc = c.sb("acc", [P, NBLK * P])
        combT = c.sb("combT", [P, NBLK * P], BF16)
        pick = c.sb("pick", [P, E, P], BF16)
        b1, b2 = c.sb("b1", [P, NE, HC]), c.sb("b2", [P, NE])
        ffn_gate(nc, name + "g", resid, ident, identb, half_power, w, xh, xl, combT, pick, b1, b2)
        ffn_experts(nc, name + "e", w, xh, xl, combT, pick, b1, b2, acc)
        ffn_add(nc, name + "a", resid, ident, acc)


def ffn_gate(nc, name, resid, ident, identb, half_power, w, xh, xl, combT, pick, b1, b2):
    with ExitStack() as ctx:
        c = Core(nc, ctx, name)
        gate_w, gate_b = c.sb("gate_w", [P, E]), c.sb("gate_b", [P, E])
        stats = c.sb("stats", [P, KB, 6])
        meanvar = c.sb("meanvar", [P, KB, 2])
        var_eps = c.sb("var_eps", [P, KB])
        rstd = c.sb("rstd", [P, KB])
        xn = [c.sb(f"xn{i}", [P, KB, D]) for i in range(2)]
        xnT = [c.sb(f"xnT{i}", [P, SEQ]) for i in range(2)]
        logit = c.sb("logit", [P, NBLK, E])
        tri = c.sb("tri", [P, E, E])
        above = c.sb("above", [P, NBLK, E, E])
        tied = c.sb("tied", [P, NBLK, E, E])
        rank = c.sb("rank", [P, NBLK, E])
        first, second = c.sb("first", [P, NBLK, E]), c.sb("second", [P, NBLK, E])
        prod = c.sb("prod", [P, 2, NBLK, E])
        top = c.sb("top", [P, 2, NBLK])
        gap, ratio, wsum, w1st, w2nd = (c.sb(n, [P, NBLK]) for n in ("gap", "ratio", "wsum", "w1st", "w2nd"))
        comb, crest, crest2 = (c.sb(n, [P, NBLK, E]) for n in ("comb", "crest", "crest2"))
        cparts = c.sb("cparts", [P, NBLK, 3, E], BF16)
        turn = [c.bank(f"turn{i}") for i in range(2)]
        logit_ps = [c.bank(f"logit{i}") for i in range(2)]
        comb_ps = [c.bank(f"comb{i}", BF16) for i in range(2)]
        names = ("w_loaded dve_passed pool_passed made zeroed ln_stats ln_mv ln_eps ln_rstd xn_ready turned xnT_ready xh_ready xl_ready logit_full "
                 "logit_read chain gap_ready ratio_ready parts_ready comb_full comb_read").split()
        s = {n: c.sem(n) for n in names}
        block = ctx.enter_context(nc.Block())
        TURNS = NBLK // 8

        @block.sync
        def _(sp):
            sp.dma_start(gate_w[:], w["gate_w"]).then_inc(s["w_loaded"], 16)
            sp.dma_start(gate_b[:], w["gate_b"].partition_broadcast(P)).then_inc(s["w_loaded"], 16)
            sp.dma_start(b1[:], w["b1"]).then_inc(s["w_loaded"], 16)
            sp.dma_start(b2[:], w["b2"]).then_inc(s["w_loaded"], 16)
            sp.wait_ge(s["w_loaded"], 64)

        @block.gpsimd
        def _(pool):
            nc.gpsimd.memset(tri[:], 1.0).then_inc(s["zeroed"], 1)
            nc.gpsimd.memset(pick[:], 0.0).then_inc(s["zeroed"], 1)
            nc.gpsimd.memset(combT[:], 0.0).then_inc(s["zeroed"], 1)
            pool.wait_ge(s["zeroed"], 3)
            nc.gpsimd.affine_select(out=tri[:], in_=tri[:], compare_op=ALU.is_gt, fill=0.0, base=0,
                                    pattern=[[1, E], [-1, E]], channel_multiplier=0).then_inc(s["made"], 1)
            for part in range(3):
                pool.wait_ge(s["made"], part + 1)
                nc.gpsimd.affine_select(out=pick[:], in_=pick[:], compare_op=ALU.not_equal, fill=1.0, base=-E * part,
                                        pattern=[[-1, E], [0, P]], channel_multiplier=1).then_inc(s["made"], 1)
            with pool.Fori(0, NB) as b:
                pool.wait_ge(s["ln_mv"], b + 1)
                settle(pool, s["pool_passed"])
                nc.gpsimd.tensor_scalar(var_eps[:], meanvar[:, :, 1], EPS, None, ALU.add).then_inc(s["ln_eps"], 1)
                pool.wait_ge(s["ln_eps"], b + 1)
                nc.gpsimd.tensor_tensor(rstd[:], var_eps[:], half_power[:], ALU.pow).then_inc(s["ln_rstd"], 1)

        @block.tensor
        def _(pe):
            pe.wait_ge(s["w_loaded"], 64)

            def turn_x(b, par):
                pe.wait_ge(s["xn_ready"], b + 1)
                if not (isinstance(b, int) and b < 2):
                    pe.wait_ge(s["xnT_ready"], b - 1)
                for k in range(KB):
                    ins = nc.tensor.transpose(turn[par][:, P * k:P * (k + 1)], xn[par][:, k, :], ident[:])
                ins.then_inc(s["turned"], 1)

            def gate(b, par):
                pe.wait_ge(s["xnT_ready"], b + 1)
                if not (isinstance(b, int) and b < 2):
                    pe.wait_ge(s["logit_read"], b - 1)
                for k in range(KB):
                    ins = nc.tensor.matmul(logit_ps[par][:, E * k:E * (k + 1)], xnT[par][:, P * k:P * (k + 1)], gate_w[:],
                                           start=True, stop=True)
                ins.then_inc(s["logit_full"], 1)

            turn_x(0, 0)
            turn_x(1, 1)
            gate(0, 0)
            with pe.Fori(0, (NB - 2) // 2) as i:
                for r in range(2):
                    turn_x(i * 2 + 2 + r, r)
                    gate(i * 2 + 1 + r, 1 - r)
            gate(NB - 1, 1)
            pe.wait_ge(s["parts_ready"], 1)
            for t in range(TURNS):
                if t >= 2:
                    pe.wait_ge(s["comb_read"], t - 1)
                for k in range(8):
                    ins = nc.tensor.transpose(comb_ps[t % 2][0:3 * E, P * k:P * (k + 1)],
                                              cparts[:, 8 * t + k].rearrange("p a e -> p (a e)"), identb[:])
                ins.then_inc(s["comb_full"], 1)

        @block.scalar
        def _(act):
            def bring(b, par):
                act.wait_ge(s["turned"], b + 1)
                if not (isinstance(b, int) and b < 2):
                    act.wait_ge(s["logit_full"], b - 1)
                    act.wait_ge(s["xl_ready"], b - 1)
                nc.scalar.copy(xnT[par][:], turn[par][:]).then_inc(s["xnT_ready"], 1)

            bring(0, 0)
            bring(1, 1)
            with act.Fori(0, (NB - 2) // 2) as i:
                for r in range(2):
                    bring(i * 2 + 2 + r, r)
            act.wait_ge(s["gap_ready"], 1)
            nc.scalar.activation(ratio[:], gap[:], ACT.Exp).then_inc(s["ratio_ready"], 1)
            act.wait_ge(s["zeroed"], 3)
            for t in range(TURNS):
                act.wait_ge(s["comb_full"], t + 1)
                nc.scalar.copy(combT[0:3 * E, 8 * P * t:8 * P * (t + 1)], comb_ps[t % 2][0:3 * E, :]).then_inc(s["comb_read"], 1)

        @block.vector
        def _(dve):
            def norm(b, par):
                for k in range(KB):
                    ins = nc.vector.bn_stats(stats[:, k, :], resid[:, bass.ds(b * KB + k, 1), :].squeeze(1))
                ins.then_inc(s["ln_stats"], 1)
                dve.wait_ge(s["ln_stats"], b + 1)
                settle(dve, s["dve_passed"])
                for k in range(KB):
                    ins = nc.vector.bn_aggr(meanvar[:, k, :], stats[:, k, :])
                ins.then_inc(s["ln_mv"], 1)
                dve.wait_ge(s["ln_rstd"], b + 1)
                if not (isinstance(b, int) and b < 2):
                    dve.wait_ge(s["turned"], b - 1)
                for k in range(KB):
                    ins = nc.vector.tensor_scalar(xn[par][:, k, :], resid[:, bass.ds(b * KB + k, 1), :].squeeze(1),
                                                  meanvar[:, k, 0:1], rstd[:, k:k + 1], ALU.subtract, ALU.mult)
                ins.then_inc(s["xn_ready"], 1)

            def split(b, par):
                at = bass.ds(b * SEQ, SEQ)
                dve.wait_ge(s["xnT_ready"], b + 1)
                nc.vector.tensor_copy(xh[:, at], xnT[par][:]).then_inc(s["xh_ready"], 1)
                dve.wait_ge(s["xh_ready"], b + 1)
                nc.vector.tensor_tensor(xl[:, at], xnT[par][:], xh[:, at].bitcast(F32), ALU.subtract).then_inc(s["xl_ready"], 1)

            def logits(b, par):
                dve.wait_ge(s["logit_full"], b + 1)
                nc.vector.tensor_tensor(logit[:, bass.ds(b * KB, KB), :],
                                        logit_ps[par][:, 0:KB * E].rearrange("p (k e) -> p k e", e=E),
                                        gate_b[:].unsqueeze(1).broadcast_to([P, KB, E]), ALU.add).then_inc(s["logit_read"], 1)

            dve.wait_ge(s["w_loaded"], 64)
            norm(0, 0)
            norm(1, 1)
            split(0, 0)
            logits(0, 0)
            with dve.Fori(0, (NB - 2) // 2) as i:
                for r in range(2):
                    norm(i * 2 + 2 + r, r)
                    split(i * 2 + 1 + r, 1 - r)
                    logits(i * 2 + 1 + r, 1 - r)
            split(NB - 1, 1)
            logits(NB - 1, 1)

            done = [0]

            def link(ins):
                done[0] += 1
                ins.then_inc(s["chain"], 1)
                dve.wait_ge(s["chain"], done[0])

            dve.wait_ge(s["logit_read"], NB)
            dve.wait_ge(s["made"], 1)
            other = logit[:].unsqueeze(2).broadcast_to([P, NBLK, E, E])
            own = logit[:].unsqueeze(3).broadcast_to([P, NBLK, E, E])
            nc.vector.tensor_tensor(above[:], other, own, ALU.is_gt)
            link(nc.vector.tensor_tensor(tied[:], other, own, ALU.is_equal))
            link(nc.vector.tensor_tensor(tied[:], tied[:], tri[:].unsqueeze(1).broadcast_to([P, NBLK, E, E]), ALU.mult))
            link(nc.vector.tensor_tensor(above[:], above[:], tied[:], ALU.add))
            link(nc.vector.tensor_reduce(rank[:], above[:], AX.X, ALU.add))
            nc.vector.tensor_scalar(first[:], rank[:], 0.0, None, ALU.is_equal)
            link(nc.vector.tensor_scalar(second[:], rank[:], 1.0, None, ALU.is_equal))
            nc.vector.tensor_tensor(prod[:, 0], first[:], logit[:], ALU.mult)
            link(nc.vector.tensor_tensor(prod[:, 1], second[:], logit[:], ALU.mult))
            link(nc.vector.tensor_reduce(top[:], prod[:], AX.X, ALU.add))
            nc.vector.tensor_tensor(gap[:], top[:, 1], top[:, 0], ALU.subtract).then_inc(s["gap_ready"], 1)
            dve.wait_ge(s["ratio_ready"], 1)
            link(nc.vector.tensor_scalar(wsum[:], ratio[:], 1.0, None, ALU.add))
            link(nc.vector.reciprocal(w1st[:], wsum[:]))
            link(nc.vector.tensor_tensor(w2nd[:], ratio[:], w1st[:], ALU.mult))
            nc.vector.tensor_tensor(prod[:, 0], first[:], w1st[:].unsqueeze(2).broadcast_to([P, NBLK, E]), ALU.mult)
            link(nc.vector.tensor_tensor(prod[:, 1], second[:], w2nd[:].unsqueeze(2).broadcast_to([P, NBLK, E]), ALU.mult))
            link(nc.vector.tensor_tensor(comb[:], prod[:, 0], prod[:, 1], ALU.add))
            link(nc.vector.tensor_copy(cparts[:, :, 0, :], comb[:]))
            link(nc.vector.tensor_tensor(crest[:], comb[:], cparts[:, :, 0, :], ALU.subtract))
            link(nc.vector.tensor_copy(cparts[:, :, 1, :], crest[:]))
            link(nc.vector.tensor_tensor(crest2[:], crest[:], cparts[:, :, 1, :], ALU.subtract))
            nc.vector.tensor_copy(cparts[:, :, 2, :], crest2[:]).then_inc(s["parts_ready"], 1)


def ffn_experts(nc, name, w, xh, xl, combT, pick, b1, b2, acc):
    with ExitStack() as ctx:
        c = Core(nc, ctx, name)
        w1 = [c.sb(f"w1_{i}", [P, HID]) for i in range(2)]
        w2 = [c.sb(f"w2_{i}", [P, HC, D]) for i in range(2)]
        w1h, w1l = ([c.sb(f"{n}{i}", [P, HID], F32R) for i in range(2)] for n in ("w1h", "w1l"))
        w2h, w2l = ([c.sb(f"{n}{i}", [P, HC, D], F32R) for i in range(2)] for n in ("w2h", "w2l"))
        hid = [c.sb(f"hid{i}", [P, SEQ]) for i in range(HC)]
        hh, hl = ([c.sb(f"{n}{i}", [P, HC, SEQ], F32R) for i in range(2)] for n in ("hh", "hl"))
        weight = [c.sb(f"weight{i}", [P, SEQ]) for i in range(2)]
        scaled = [c.sb(f"scaled{i}", [P, SEQ]) for i in range(2)]
        hid_ps = [c.bank(f"hid{i}") for i in range(HC)]
        out_ps = [c.bank(f"out{i}") for i in range(2)]
        weight_ps = c.bank("weight")
        names = ("pool_passed w0_loaded w1_loaded w_high w_split hid_full gelu_done h_high h_split out_full weight_full weight_read "
                 "combined added").split()
        s = {n: c.sem(n) for n in names}
        block = ctx.enter_context(nc.Block())

        def run(eng, turn):
            for e in (0, 1):
                for b in range(NB):
                    turn(e, e, b)
            with eng.Fori(0, (NE - 3) // 2) as i:
                for r in range(2):
                    for b in range(NB):
                        turn(i * 2 + 2 + r, 2 + r, b)
            for b in range(NB):
                turn(NE - 1, NE - 1, b)

        @block.sync
        def _(sp):
            def load(e, like):
                par = like % 2
                if like >= 2:
                    sp.wait_ge(s["w_split"], e - 1)
                sp.dma_start(w1[par][:], w["w1"][bass.ds(e, 1)].squeeze(0)).then_inc(s[f"w{par}_loaded"], 16)
                sp.dma_start(w2[par][:], w["w2"][bass.ds(e, 1)].squeeze(0)).then_inc(s[f"w{par}_loaded"], 16)

            load(0, 0)
            load(1, 1)
            with sp.Fori(0, (NE - 3) // 2) as i:
                load(i * 2 + 2, 2)
                load(i * 2 + 3, 3)
            load(NE - 1, NE - 1)
            sp.wait_ge(s["w0_loaded"], 16 * (NE + 1))

        @block.gpsimd
        def _(pool):
            def parts(e, like):
                par = like % 2
                pool.wait_ge(s[f"w{par}_loaded"], (e - par) * 16 + 32)
                if like >= 2:
                    pool.wait_ge(s["out_full"], e * NB - NB)
                settle(pool, s["pool_passed"])
                nc.gpsimd.tensor_copy(w1h[par][:], w1[par][:])
                nc.gpsimd.tensor_copy(w2h[par][:], w2[par][:]).then_inc(s["w_high"], 1)
                pool.wait_ge(s["w_high"], e + 1)
                nc.gpsimd.tensor_tensor(w1l[par][:], w1[par][:], w1h[par][:].bitcast(F32), ALU.subtract)
                nc.gpsimd.tensor_tensor(w2l[par][:], w2[par][:], w2h[par][:].bitcast(F32), ALU.subtract).then_inc(s["w_split"], 1)

            def turn(e, like, b):
                if b == 1 and like + 1 < NE:
                    parts(e + 1, like + 1)
                if like > 0:
                    pool.wait_ge(s["combined"], e * NB + b + 1)
                    sl = slice(SEQ * b, SEQ * (b + 1))
                    nc.gpsimd.tensor_tensor(acc[:, sl], acc[:, sl], scaled[b % 2][:], ALU.add).then_inc(s["added"], 1)

            parts(0, 0)
            run(pool, turn)

        @block.tensor
        def _(pe):
            def hidden(e, like, b):
                par, t = like % 2, e * NB + b
                if b == 0:
                    pe.wait_ge(s["w_split"], e + 1)
                sl = slice(SEQ * b, SEQ * (b + 1))
                for k in range(HC):
                    if not (like == 0 and b == 0):
                        pe.wait_ge(s["gelu_done"], t * HC - HC + k + 1)
                    cols = slice(P * k, P * (k + 1))
                    nc.tensor.matmul(hid_ps[k][:], w1h[par][:, cols], xh[:, sl], start=True, stop=False)
                    nc.tensor.matmul(hid_ps[k][:], w1h[par][:, cols], xl[:, sl], start=False, stop=False)
                    nc.tensor.matmul(hid_ps[k][:], w1l[par][:, cols], xh[:, sl], start=False,
                                     stop=True).then_inc(s["hid_full"], 1)

            def output(e, like, b):
                par, t = like % 2, e * NB + b
                if like > 0:
                    if not (like == 1 and b == 0):
                        pe.wait_ge(s["weight_read"], t - NB)
                    nc.tensor.matmul(weight_ps[:], pick[:, bass.ds(e - 1, 1), :].squeeze(1), combT[:, SEQ * b:SEQ * (b + 1)],
                                     start=True, stop=True).then_inc(s["weight_full"], 1)
                if not (like == 0 and b < 2):
                    pe.wait_ge(s["combined"], t - 1)
                for k in range(HC):
                    pe.wait_ge(s["h_split"], t * HC + k + 1)
                    nc.tensor.matmul(out_ps[b % 2][:], w2h[par][:, k, :], hh[b % 2][:, k, :], start=(k == 0), stop=False)
                    nc.tensor.matmul(out_ps[b % 2][:], w2h[par][:, k, :], hl[b % 2][:, k, :], start=False, stop=False)
                    ins = nc.tensor.matmul(out_ps[b % 2][:], w2l[par][:, k, :], hh[b % 2][:, k, :], start=False,
                                           stop=(k == HC - 1))
                ins.then_inc(s["out_full"], 1)

            def turn(e, like, b):
                hidden(e, like, b)
                if b > 0:
                    output(e, like, b - 1)
                elif like > 0:
                    output(e - 1, like - 1, NB - 1)

            run(pe, turn)
            output(NE - 1, NE - 1, NB - 1)

        @block.scalar
        def _(act):
            def broadcast(e, like, b):
                if like == 0:
                    return
                t = e * NB + b
                act.wait_ge(s["weight_full"], t - NB + 1)
                if not (like == 1 and b < 2):
                    act.wait_ge(s["combined"], t - 1)
                nc.scalar.copy(weight[b % 2][:], weight_ps[:]).then_inc(s["weight_read"], 1)

            def turn(e, like, b):
                t = e * NB + b
                for k in range(HC):
                    act.wait_ge(s["hid_full"], t * HC + k + 1)
                    if not (like == 0 and b == 0):
                        act.wait_ge(s["h_split"], t * HC - HC + k + 1)
                    nc.scalar.activation(hid[k][:], hid_ps[k][:], ACT.Gelu,
                                         bias=b1[:, bass.ds(e, 1), k:k + 1].squeeze(1)).then_inc(s["gelu_done"], 1)
                if b > 0:
                    broadcast(e, like, b - 1)
                elif like > 0:
                    broadcast(e - 1, like - 1, NB - 1)

            run(act, turn)
            broadcast(NE - 1, NE - 1, NB - 1)

        @block.vector
        def _(dve):
            def combine(e, like, b):
                t = e * NB + b
                sl = slice(SEQ * b, SEQ * (b + 1))
                bias = b2[:, bass.ds(e, 1)]
                dve.wait_ge(s["out_full"], t + 1)
                if like == 0:
                    nc.vector.tensor_scalar(acc[:, sl], out_ps[b % 2][:], bias, None, ALU.add).then_inc(s["combined"], 1)
                    return
                dve.wait_ge(s["weight_read"], t - NB + 1)
                if not (like == 1 and b < 2):
                    dve.wait_ge(s["added"], t - NB - 1)
                nc.vector.scalar_tensor_tensor(scaled[b % 2][:], out_ps[b % 2][:], bias, weight[b % 2][:], ALU.add,
                                               ALU.mult).then_inc(s["combined"], 1)

            def turn(e, like, b):
                t = e * NB + b
                for k in range(HC):
                    if k == 0 and not (like == 0 and b < 2):
                        dve.wait_ge(s["out_full"], t - 1)
                    dve.wait_ge(s["gelu_done"], t * HC + k + 1)
                    nc.vector.tensor_copy(hh[b % 2][:, k, :], hid[k][:]).then_inc(s["h_high"], 1)
                    dve.wait_ge(s["h_high"], t * HC + k + 1)
                    nc.vector.tensor_tensor(hl[b % 2][:, k, :], hid[k][:], hh[b % 2][:, k, :].bitcast(F32),
                                            ALU.subtract).then_inc(s["h_split"], 1)
                if b > 0:
                    combine(e, like, b - 1)
                elif like > 0:
                    combine(e - 1, like - 1, NB - 1)

            run(dve, turn)
            combine(NE - 1, NE - 1, NB - 1)


def ffn_add(nc, name, resid, ident, acc):
    with ExitStack() as ctx:
        c = Core(nc, ctx, name)
        turn = [c.bank(f"turn{i}") for i in range(2)]
        turned, added = c.sem("turned"), c.sem("added")
        block = ctx.enter_context(nc.Block())

        @block.tensor
        def _(pe):
            for b in range(NB):
                if b >= 2:
                    pe.wait_ge(added, b - 1)
                for k in range(KB):
                    n = b * KB + k
                    ins = nc.tensor.transpose(turn[b % 2][:, P * k:P * (k + 1)], acc[:, P * n:P * (n + 1)], ident[:])
                ins.then_inc(turned, 1)

        @block.vector
        def _(dve):
            for b in range(NB):
                dve.wait_ge(turned, b + 1)
                rows = resid[:, KB * b:KB * (b + 1), :].rearrange("p k d -> p (k d)")
                nc.vector.tensor_tensor(rows, turn[b % 2][:], rows, ALU.add).then_inc(added, 1)


def hybrid(nc, x, a, m, f, rel_emb, onehot, out):
    nc.disable_value_cache = True
    with ExitStack() as ctx:
        resid = ctx.enter_context(nc.sbuf_tensor("resid", [P, NBLK, D], F32))
        ident = ctx.enter_context(nc.sbuf_tensor("ident", [P, P], F32))
        identb = ctx.enter_context(nc.sbuf_tensor("identb", [P, P], BF16))
        half_power = ctx.enter_context(nc.sbuf_tensor("half_power", [P, KB], F32))
        scratch = nc.dram_tensor("qk_parts", (2, 2, P, 3, SEQ), BF16, kind="Internal").ap()
        maxima = nc.dram_tensor("maxima", (2, 3 * HH, SEQ), BF16, kind="Internal").ap()
        vectors = nc.dram_tensor("bias_vectors", (4, H, 16, NV), BF16, kind="Internal").ap()
        with ExitStack() as first:
            load_constants(nc, first, x, resid, ident, identb, half_power)
        attention(nc, "a", resid, ident, identb, half_power, a, (rel_emb, onehot, vectors), scratch, maxima)
        ffn(nc, "f", resid, ident, identb, half_power, f)
        attention(nc, "m", resid, ident, identb, half_power, m, None, scratch, maxima)
        ffn(nc, "g", resid, ident, identb, half_power, f)
        with ExitStack() as last:
            stored = last.enter_context(nc.semaphore("stored"))
            block = last.enter_context(nc.Block())
            rows = out.rearrange("b (k p) d -> p (b k) d", p=P)

            @block.sync
            def _(sp):
                sp.dma_start(rows[:, 0:NBLK // 2, :], resid[:, 0:NBLK // 2, :]).then_inc(stored, 16)
                sp.dma_start(rows[:, NBLK // 2:, :], resid[:, NBLK // 2:, :]).then_inc(stored, 16)
                sp.wait_ge(stored, 32)


def distance_onehot():
    import math
    import numpy as np

    n = np.maximum(np.stack([np.arange(NV) - (P - 1), 2 * P - 1 - np.arange(NV)]), 0)
    exact = BUCKETS // 2
    far = exact + (np.log(np.maximum(n, 1).astype(np.float32) / exact) / math.log(MAX_DIST / exact)
                   * (BUCKETS - exact)).astype(np.int32)
    bucket = np.where(n < exact, n, np.minimum(far, BUCKETS - 1))
    return (bucket[:, None, :] == np.arange(BUCKETS)[None, :, None]).astype(np.float32)


def kernel(**inputs):
    import numpy as np
    import concourse.bacc as bacc
    from concourse.bass_utils import run_bass_kernel_spmd

    nc = bacc.Bacc("TRN2", target_bir_lowering=False, num_devices=1)
    arrays = {}

    def given(name, a):
        a = np.ascontiguousarray(a)
        arrays[f"in_{name}"] = a
        return nc.dram_tensor(f"in_{name}", a.shape, mybir.dt.from_np(a.dtype), kind="ExternalInput").ap()

    def of(prefix, name):
        return np.asarray(inputs[f"L0_{prefix}_{name}"])

    x = given("x", of("attn_a", "x"))
    a = {n: given("a_" + n, of("attn_a", n.replace("w", "W")).T) for n in ("wq", "wk", "wv", "wo")}
    m = {n: given("b_" + n, of("attn_b", k)) for n, k in (("wq", "Wq"), ("wk", "Wk"), ("wv", "Wv"), ("wo", "Wp"))}
    for n in ("bq", "bk", "bv"):
        a[n], m[n] = given("a_" + n, of("attn_a", n)), given("b_" + n, of("attn_b", n))
    a["bo"], m["bo"] = given("a_bo", of("attn_a", "bo")), given("b_bo", of("attn_b", "bp"))
    w1 = np.concatenate([of("ffn", "ws1")[None], of("ffn", "w1")])
    w2 = np.concatenate([of("ffn", "ws2")[None], of("ffn", "w2")])
    b1 = np.concatenate([of("ffn", "bs1")[None], of("ffn", "b1")])
    b2 = np.concatenate([of("ffn", "bs2")[None], of("ffn", "b2")])
    f = {
        "gate_w": given("gate_w", of("ffn", "gate_w")), "gate_b": given("gate_b", of("ffn", "gate_b")),
        "w1": given("w1", w1), "w2": given("w2", w2.reshape(NE, HC, P, D).transpose(0, 2, 1, 3)),
        "b1": given("b1", b1.reshape(NE, HC, P).transpose(2, 0, 1)), "b2": given("b2", b2.T),
    }
    rel_emb = given("rel_emb", of("attn_a", "rel_emb"))
    onehot = given("onehot", distance_onehot())
    out = nc.dram_tensor("out", (NB, SEQ, D), F32, kind="ExternalOutput").ap()
    hybrid(nc, x, a, m, f, rel_emb, onehot, out)
    r = run_bass_kernel_spmd(nc, [arrays], core_ids=[0])
    return r.results[0]["out"]
```

```python
from contextlib import ExitStack

import concourse.bass as bass
from concourse import mybir

F32 = mybir.dt.float32
F32R = mybir.dt.float32r
BF16 = mybir.dt.bfloat16
F16 = mybir.dt.float16
ALU = mybir.AluOpType
ACT = mybir.ActivationFunctionType
AX = mybir.AxisListType

P = 128
NB, SEQ, D = 8, 512, 128
KB = SEQ // P
NBLK = NB * KB
H, HD = 16, 8
HH = H // 2
NGRP = H // 4
E, NE, HID = 8, 9, 512
HC = HID // P
BUCKETS, MAX_DIST = 32, 128
NV = 3 * P
EPS = 1e-5
MASK = -1e30
SCALE = float(HD) ** -0.5
PQ = [0, 0, 0, 1, 1, 2]
PK = [0, 1, 2, 0, 1, 0]
NTERM = len(PQ)
QRUNS = [(0, 0, 3), (1, 0, 2), (2, 0, 1)]
KRUNS = [(0, 1, 3), (0, 1, 2), (0, 0, 1)]
MROW = 96
FAR = 113
NEAR = P + FAR - 1
NPB = 8
PW = SEQ + (SEQ - P) + P + (SEQ - 2 * P)
PCOL = {0: (0, 0), 1: (SEQ, P), 3: (2 * SEQ - P, 3 * P), 2: (2 * SEQ, 2 * P)}
ROWBANKS = [[(3, 0, 512)], [(2, 0, 384), (0, 384, 128)], [(1, 0, 256)]]
COLBANKS = [[(0, 0, 512)], [(1, 0, 384), (3, 384, 128)], [(2, 0, 256)]]


def settle(eng, passed):
    eng.sem_inc(passed, 1)


class Core:

    def __init__(self, nc, ctx, prefix):
        self.nc, self.ctx, self.prefix = nc, ctx, prefix

    def sb(self, name, shape, dt=F32):
        return self.ctx.enter_context(self.nc.sbuf_tensor(f"{self.prefix}_{name}", shape, dt))

    def bank(self, name, dt=F32):
        return self.ctx.enter_context(self.nc.psum_tensor(f"{self.prefix}_{name}_ps", [P, 2048 // (4 if dt == F32 else 2)], dt))

    def sem(self, name):
        return self.ctx.enter_context(self.nc.semaphore(f"{self.prefix}_{name}"))


def load_constants(nc, ctx, x, resid, ident, identb, half_power, loaded):
    c = Core(nc, ctx, "init")
    zeroed, made = c.sem("zeroed"), c.sem("made")
    block = ctx.enter_context(nc.Block())
    rows = x.rearrange("b (k p) d -> p (b k) d", p=P)

    @block.sync
    def _(sp):
        for sem, blocks in zip(loaded, (slice(0, KB), slice(KB, NBLK))):
            sp.dma_start(resid[:, blocks, :], rows[:, blocks, :]).then_inc(sem, 16)

    @block.gpsimd
    def _(pool):
        nc.gpsimd.memset(half_power[:], -0.5)
        nc.gpsimd.memset(ident[:], 0.0).then_inc(zeroed, 1)
        nc.gpsimd.memset(identb[:], 0.0).then_inc(zeroed, 1)
        pool.wait_ge(zeroed, 2)
        for m in (ident, identb):
            nc.gpsimd.affine_select(out=m[:], in_=m[:], compare_op=ALU.not_equal, fill=1.0, base=0,
                                    pattern=[[-1, P]], channel_multiplier=1).then_inc(made, 1)


class RelativeTables:

    COPIES = 16

    def __init__(self, nc, c, given, psum, room):
        self.nc = nc
        self.rel_emb, self.onehot, self.scratch = given
        self.keyhigh = c.sb("keyhigh", [P, H, NEAR], BF16)
        self.keylow = c.sb("keylow", [P, H, NEAR], F16)
        self.rowbias = c.sb("rowbias", [P, H, SEQ], BF16)
        self.rel, self.far = room[0][0:BUCKETS, 0:H], room[1][0:H, 2 * NV:2 * NV + 1]
        self.hot = room[0][0:BUCKETS, H:H + 2 * NV].rearrange("b (t n) -> b t n", t=2)
        self.vec = room[1][0:H, 0:2 * NV].rearrange("h (t n) -> h t n", t=2)
        self.parts = room[2][0:H, 0:3 * NV // 2].bitcast(BF16).rearrange("h (t n) -> h t n", t=3)
        self.up, self.down = psum
        names = "rel_loaded vec_full vec_chain vec_ready stored row_spread key_spread far_zeroed"
        self.s = {n: c.sem(n) for n in names.split()}

    def load(self, sp):
        sp.dma_start(self.rel, self.rel_emb).then_inc(self.s["rel_loaded"], 16)
        sp.dma_start(self.hot, self.onehot.rearrange("t b n -> b t n")).then_inc(self.s["rel_loaded"], 16)

    def store(self, sp):
        sp.wait_ge(self.s["vec_ready"], 1)
        dst = self.scratch.rearrange("t h c n -> h t c n")
        for t in range(3):
            sp.dma_start(dst[:, t], self.parts[:, t, :].unsqueeze(1).broadcast_to([H, self.COPIES, NV])).then_inc(
                self.s["stored"], 16)
        sp.wait_ge(self.s["stored"], 48)

    def spread(self, sp, t, tile, at, width, sem):
        for a in range(P // self.COPIES):
            src = bass.AP(self.scratch.tensor, t * H * self.COPIES * NV + P - 1 - self.COPIES * a,
                          [[NV - 1, self.COPIES], [self.COPIES * NV, H], [1, width]])
            into = slice(self.COPIES * a, self.COPIES * (a + 1))
            sp.dma_start(tile[into, :, at:at + width], src).then_inc(self.s[sem], 16)

    def spread_rows(self, sp):
        self.spread(sp, 2, self.rowbias, 2 * P, 2 * P, "row_spread")

    def spread_keys(self, sp):
        self.spread(sp, 0, self.keyhigh, 0, NEAR, "key_spread")
        self.spread(sp, 1, self.keylow[:].bitcast(BF16), 0, NEAR, "key_spread")

    def zero_far(self, pool):
        self.nc.gpsimd.memset(self.rowbias[:, :, 0:2 * P], 0.0).then_inc(self.s["far_zeroed"], 1)

    def look_up(self, pe):
        pe.wait_ge(self.s["rel_loaded"], 32)
        for t, bank in enumerate((self.up, self.down)):
            self.nc.tensor.matmul(bank[0:H, 0:NV], self.rel, self.hot[:, t, :], start=True,
                                  stop=True).then_inc(self.s["vec_full"], 1)

    def make_vectors(self, dve):
        nc, vec, parts, done = self.nc, self.vec, self.parts, [0]

        def link(ins):
            done[0] += 1
            ins.then_inc(self.s["vec_chain"], 1)
            dve.wait_ge(self.s["vec_chain"], done[0])

        dve.wait_ge(self.s["vec_full"], 2)
        link(nc.vector.tensor_copy(self.far, self.up[0:H, NV - 1:NV]))
        for t, bank in enumerate((self.up, self.down)):
            ins = nc.vector.tensor_scalar(vec[:, t, :], bank[0:H, 0:NV], self.far[:, 0:1], SCALE, ALU.subtract, ALU.mult)
        link(ins)
        nc.vector.memset(vec[:, 0, 0:P - 1], MASK)
        link(nc.vector.memset(vec[:, 1, 2 * P:], MASK))
        nc.vector.tensor_copy(parts[:, 2, :], vec[:, 1, :])
        link(nc.vector.tensor_copy(parts[:, 0, :], vec[:, 0, :]))
        low = parts[:, 1, :].bitcast(F16)
        link(nc.vector.tensor_tensor(low, vec[:, 0, :], parts[:, 0, :], ALU.subtract))
        nc.vector.memset(low[:, 0:P - 1], 0.0).then_inc(self.s["vec_ready"], 1)

    def rows_ready(self, dve):
        dve.wait_ge(self.s["row_spread"], 16 * P // self.COPIES)
        dve.wait_ge(self.s["far_zeroed"], 1)

    def keys_ready(self, pe):
        pe.wait_ge(self.s["key_spread"], 32 * P // self.COPIES)

    def key_parts(self, h, width):
        width = min(width, NEAR)
        return [(self.keyhigh[:, h, 0:width], width), (self.keylow[:, h, 0:width], width)]

    def row_bias(self, h, width):
        return self.rowbias[:, h, SEQ - width:]


class CausalTables:

    def __init__(self, nc, c):
        self.nc = nc
        self.keymask = c.sb("keymask", [P, P], BF16)
        self.rowmask = c.sb("rowmask", [P, SEQ], BF16)
        self.zeroed, self.made = c.sem("mask_zeroed"), c.sem("mask_made")

    def load(self, sp):
        pass

    store = spread_rows = spread_keys = look_up = make_vectors = load

    def zero_far(self, pool):
        nc = self.nc
        nc.gpsimd.memset(self.keymask[:], 0.0).then_inc(self.zeroed, 1)
        nc.gpsimd.memset(self.rowmask[:], 0.0).then_inc(self.zeroed, 1)
        pool.wait_ge(self.zeroed, 2)
        nc.gpsimd.affine_select(out=self.keymask[:], in_=self.keymask[:], compare_op=ALU.is_ge, fill=MASK, base=0,
                                pattern=[[1, P]], channel_multiplier=-1).then_inc(self.made, 1)
        nc.gpsimd.affine_select(out=self.rowmask[:, 3 * P:], in_=self.rowmask[:, 3 * P:], compare_op=ALU.is_ge,
                                fill=MASK, base=0, pattern=[[-1, P]], channel_multiplier=1).then_inc(self.made, 1)

    def rows_ready(self, eng):
        eng.wait_ge(self.made, 2)

    keys_ready = rows_ready

    def key_parts(self, h, width):
        return [(self.keymask[:], P)]

    def row_bias(self, h, width):
        return self.rowmask[:, SEQ - width:]


def attention(nc, name, resid, ident, identb, half_power, passed, w, relative, scratch, maxima, zeros, loaded):
    with ExitStack() as ctx:
        c = Core(nc, ctx, name)
        scale = 1.0 if relative else SCALE
        qs = [c.sb(f"qs{i}", [P, H, SEQ], BF16) for i in range(2)]
        ks = [c.sb(f"ks{i}", [P, H, SEQ], BF16) for i in range(2)]
        wt = {n: c.sb(n, [P, D]) for n in ("wq", "wk", "wv", "wo")}
        bias_q, bias_k = c.sb("bias_q", [P, 1]), c.sb("bias_k", [P, 1])
        bias_qs = c.sb("bias_qs", [P, 1])
        bias_v, bias_o = c.sb("bias_v", [P, D]), c.sb("bias_o", [P, D])
        stats = c.sb("stats", [P, KB, 6])
        meanvar = c.sb("meanvar", [P, KB, 2])
        var_eps = c.sb("var_eps", [P, KB])
        rstd = c.sb("rstd", [P, KB])
        xn = c.sb("xn", [P, KB, D])
        xnT = [c.sb(f"xnT{i}", [P, SEQ]) for i in range(2)]
        qk32 = [c.sb(f"qk32_{i}", [P, SEQ]) for i in range(2)]
        rest = [c.sb(f"rest{i}", [P, SEQ]) for i in range(2)]
        qkp = [c.sb(f"qkp{i}", [P, 3, SEQ], BF16) for i in range(2)]
        vaug = [c.sb(f"vaug{i}", [P, KB, H, 32]) for i in range(2)]
        rowmax = c.sb("rowmax", [P, H, KB])
        mrest = c.sb("mrest", [P, 2, KB, HH])
        mparts = c.sb("mparts", [P, KB, 3, HH], BF16)
        mT = c.sb("mT", [3 * HH, SEQ], BF16)
        prob = [c.sb(f"prob{i}", [P, PW]) for i in range(NPB)]
        osb = [c.sb(f"osb{i}", [P, SEQ]) for i in range(2)]
        rsum = c.sb("rsum", [P, KB * 4])
        ctxn = c.sb("ctxn", [P, KB, H, HD])
        ctxT = c.sb("ctxT", [P, SEQ])

        row_ps = [c.bank(f"row{i}") for i in range(3)]
        col_ps = [c.bank(f"col{i}") for i in range(3)]
        out_ps = c.bank("out")
        work = c.bank("work")
        tables = RelativeTables(nc, c, relative, row_ps[0:2], prob) if relative else CausalTables(nc, c)

        names = ("w_loaded zeros_stored setup v_set bq_scaled ln_stats ln_mv ln_eps ln_rstd xn_ready part_q part_k rest_q rest_k "
                 "scr_written half0_loaded half1_loaded row_full row_read m_chain m_split m_stored m_loaded col_full exp_done "
                 " pv_done out_read work_full work_read r_ready bias_added").split()
        s = {n: c.sem(n) for n in names}
        block = ctx.enter_context(nc.Block())

        SLOTS = [(1, "turn_ctx", 3, "old"), (2, "turn_max", 1, "cur"), (3, "turn_out", 0, "old"), (4, "project", 0, "old"),
                 (5, "turn_ctx", 0, "cur"), (6, "turn_x", 0, "new2"), (7, "q", 0, "new2"), (8, "k", 0, "new2"),
                 (9, "turn_ctx", 1, "cur"), (10, "turn_max", 0, "new"), (11, "v", 0, "new"), (13, "turn_ctx", 2, "cur")]

        def valid(b, which):
            n = {"old": b - 1, "cur": b, "new": b + 1, "new2": b + 2}[which]
            return 0 <= n < NB

        uses = {b: [u for u in SLOTS if valid(b, u[3])] for b in range(-2, NB + 1)}
        first_use, total = {}, 0
        for b in range(-2, NB + 1):
            first_use[b] = total
            total += len(uses[b])
        LOOP0, LOOPS = 1, 2

        def run(eng, step):
            for b in range(-2, LOOP0):
                step(b, b, first_use[b])
            with eng.Fori(0, LOOPS) as i:
                for r in range(2):
                    step(i * 2 + LOOP0 + r, LOOP0 + r, i * (2 * len(SLOTS)) + first_use[LOOP0 + r])
            for b in range(LOOP0 + 2 * LOOPS, NB + 1):
                step(b, b, first_use[b])

        def work_uses(kind_b, base, slot):
            for n, u in enumerate(uses[kind_b]):
                if u[0] == slot:
                    yield u, base + n

        def earlier(like, base, what, arg):
            before = uses[like - 1]
            at = [n for n, u in enumerate(before) if u[1:3] == (what, arg)][0]
            return base - len(before) + at

        def number_of(like, base, what, arg):
            return base + [n for n, u in enumerate(uses[like]) if u[1:3] == (what, arg)][0]

        def batch_of(b, which):
            return b + {"old": -1, "cur": 0, "new": 1, "new2": 2}[which]

        @block.sync
        def _(sp):
            tables.load(sp)
            for n in ("wq", "wk", "wv", "wo"):
                sp.dma_start(wt[n][:], w[n]).then_inc(s["w_loaded"], 16)
            sp.dma_start(bias_q[:], w["bq"].unsqueeze(1)).then_inc(s["w_loaded"], 16)
            sp.dma_start(bias_k[:], w["bk"].unsqueeze(1)).then_inc(s["w_loaded"], 16)
            sp.dma_start(bias_v[:], w["bv"].partition_broadcast(P)).then_inc(s["w_loaded"], 16)
            sp.dma_start(bias_o[:], w["bo"].partition_broadcast(P)).then_inc(s["w_loaded"], 16)
            tables.store(sp)
            tables.spread_rows(sp)

            def load_half(m, par, half):
                sp.dma_start(qs[par][MROW:MROW + 3, HH * half:HH * (half + 1), :], zeros).then_inc(s[f"half{half}_loaded"], 16)
                heads = slice(HH * half, HH * (half + 1))
                for which, (dst, runs) in enumerate(((qs[par], QRUNS), (ks[par], KRUNS))):
                    t = 0
                    for first, stride, count in runs:
                        of = scratch[par, which, first:first + (count if stride else 1), :, heads, :]
                        if not stride:
                            of = of.broadcast_to([count, HD, HH, SEQ])
                        of = of.rearrange("t d h n -> t d (h n)")
                        sp.dma_start(dst[HD * t:HD * (t + count), heads, :], of).then_inc(s[f"half{half}_loaded"], 16)
                        t += count

            def load_max(number, par, half, stored):
                sp.wait_ge(s["work_read"], number + 1)
                sp.dma_start(maxima[half], mT[:]).then_inc(s["m_stored"], 16)
                sp.wait_ge(s["m_stored"], stored)
                sp.dma_start(qs[par][MROW:MROW + 3, HH * half:HH * (half + 1), :],
                             maxima[half].rearrange("(a h) q -> a h q", a=3)).then_inc(s["m_loaded"], 16)

            def step(b, like, base):
                par = like % 2
                if 0 <= like < NB:
                    load_max(number_of(like, base, "turn_max", 1), par, 1, b * 32 + 32)
                if 0 <= like + 1 < NB:
                    load_max(number_of(like, base, "turn_max", 0), 1 - par, 0, b * 32 + 48)
                if 0 <= like + 2 < NB:
                    m = b + 2
                    for part in range(3):
                        for which in range(2):
                            sp.wait_ge(s[f"part_{'qk'[which]}"], m * 3 + part + 1)
                            sp.dma_start(scratch[par, which, part].rearrange("d h n -> h d n"),
                                         qkp[which][:, part]).then_inc(s["scr_written"], 16)
                    sp.wait_ge(s["scr_written"], (m + 1) * 96)
                    if like < 0:
                        sp.wait_ge(s["setup"], 2 * like + 6)
                    if like == -2:
                        sp.dma_start(zeros, qs[0][0:3, 0:HH, :]).then_inc(s["zeros_stored"], 16)
                        sp.wait_ge(s["zeros_stored"], 16)
                    if like >= 0:
                        sp.wait_ge(s["col_full"], b * (3 * H) + 3 * HH)
                    load_half(m, par, 0)
                if 0 <= like + 2 < NB:
                    if like >= 0:
                        sp.wait_ge(s["col_full"], b * (3 * H) + 3 * H)
                    load_half(b + 2, par, 1)
                if like == -2:
                    tables.spread_keys(sp)

            run(sp, step)
            sp.wait_ge(s["w_loaded"], 128)

        @block.gpsimd
        def _(pool):
            for i in range(2):
                nc.gpsimd.memset(qs[i][:].bitcast(F32), 0.0).then_inc(s["setup"], 1)
                nc.gpsimd.memset(ks[i][:], 1.0).then_inc(s["setup"], 1)
            tables.zero_far(pool)
            pool.wait_ge(s["w_loaded"], 128)
            nc.gpsimd.tensor_scalar(bias_qs[:], bias_q[:], scale, None, ALU.mult).then_inc(s["bq_scaled"], 1)

            def step(b, like, base):
                if 0 <= like + 2 < NB:
                    m = b + 2
                    pool.wait_ge(s["ln_mv"], m + 1)
                    settle(pool, passed["pool"])
                    nc.gpsimd.tensor_scalar(var_eps[:], meanvar[:, :, 1], EPS, None, ALU.add).then_inc(s["ln_eps"], 1)
                    pool.wait_ge(s["ln_eps"], m + 1)
                    nc.gpsimd.tensor_tensor(rstd[:], var_eps[:], half_power[:], ALU.pow).then_inc(s["ln_rstd"], 1)
                    pool.wait_ge(s["xn_ready"], m + 1)
                    for k in range(KB):
                        ins = nc.gpsimd.tensor_tensor(resid[:, bass.ds(m * KB + k, 1), :].squeeze(1),
                                                      resid[:, bass.ds(m * KB + k, 1), :].squeeze(1),
                                                      bias_o[:], ALU.add)
                    ins.then_inc(s["bias_added"], 1)
                    for part in range(2):
                        for which in range(2):
                            pool.wait_ge(s[f"part_{'qk'[which]}"], m * 3 + part + 1)
                            src, dst = ((qk32, rest), (rest, qk32))[part]
                            nc.gpsimd.tensor_tensor(dst[which][:], src[which][:], qkp[which][:, part],
                                                    ALU.subtract).then_inc(s[f"rest_{'qk'[which]}"], 1)

            run(pool, step)

        @block.tensor
        def _(pe):
            tables.look_up(pe)
            pe.wait_ge(s["w_loaded"], 128)

            def rows(n, par, h):
                if h % HH == 0:
                    pe.wait_ge(s[f"half{h // HH}_loaded"], (n + 1) * ((len(QRUNS + KRUNS) + 1) * 16))
                for i, held in enumerate(ROWBANKS):
                    if not (isinstance(n, int) and n == 0 and h == 0):
                        pe.wait_ge(s["row_read"], n * (3 * H) + 3 * (h - 1) + i + 1)
                    for blk, col, width in held:
                        ins = nc.tensor.matmul(row_ps[i][:, col:col + width], qs[par][:, h, P * blk:P * (blk + 1)],
                                               ks[par][:, h, 0:width], start=True, stop=True)
                    ins.then_inc(s["row_full"], 1)

            def cols(b, par, h):
                if h % HH == 0:
                    pe.wait_ge(s["m_loaded"], b * 32 + (h // HH + 1) * 16)
                for i, held in enumerate(COLBANKS):
                    if not (isinstance(b, int) and b == 0 and h == 0):
                        pe.wait_ge(s["exp_done"], b * (3 * H) + 3 * (h - 1) + i + 1)
                    for n, (blk, col, width) in enumerate(held):
                        nc.tensor.matmul(col_ps[i][:, col:col + width], ks[par][:, h, P * blk:P * (blk + 1)],
                                         qs[par][:, h, P * blk:P * blk + width],
                                         start=(n == 0), stop=False, skip_group_check=True)
                    for blk, col, width in held:
                        for bias, wide in tables.key_parts(h, width):
                            ins = nc.tensor.matmul(col_ps[i][:, col:col + wide], identb[:], bias, start=False,
                                                   stop=True, skip_group_check=True)
                    ins.then_inc(s["col_full"], 1)

            def values(b, par, g):
                pe.wait_ge(s["exp_done"], b * (3 * H) + 12 * (g + 1))
                if not (isinstance(b, int) and b == 0 and g == 0):
                    pe.wait_ge(s["out_read"], b * NGRP + g)
                for j in (0, 1, 2, 3):
                    pcol, q0 = PCOL[j]
                    for t in range(4):
                        h = 4 * g + t
                        ins = nc.tensor.matmul(out_ps[32 * t:32 * (t + 1), q0:SEQ], vaug[par][:, j, h, :],
                                               prob[h % NPB][:, pcol:pcol + SEQ - q0],
                                               start=(j == 0), stop=(j == 3), skip_group_check=True)
                ins.then_inc(s["pv_done"], 1)

            def use(u, number, b, par):
                _, what, arg, which = u
                n = batch_of(b, which)
                npar = (par + {"old": 1, "cur": 0, "new": 1, "new2": 0}[which]) % 2
                if not (isinstance(number, int) and number == 0):
                    pe.wait_ge(s["work_read"], number)
                if what == "turn_x":
                    pe.wait_ge(s["xn_ready"], n + 1)
                    for k in range(KB):
                        ins = nc.tensor.transpose(work[:, P * k:P * (k + 1)], xn[:, k, :], ident[:])
                elif what in "qk":
                    ins = nc.tensor.matmul(work[:], wt["w" + what][:], xnT[npar][:], start=True, stop=True)
                elif what == "v":
                    for k in range(KB):
                        ins = nc.tensor.matmul(work[:, P * k:P * (k + 1)], xnT[npar][:, P * k:P * (k + 1)], wt["wv"][:],
                                               start=True, stop=True)
                elif what == "turn_max":
                    pe.wait_ge(s["m_split"], 2 * n + arg + 1)
                    view = work[0:3 * HH, :].bitcast(BF16)
                    for k in range(KB):
                        ins = nc.tensor.transpose(view[:, P * k:P * (k + 1)],
                                                  mparts[:, k].rearrange("p a h -> p (a h)"), identb[:])
                elif what == "turn_ctx":
                    pe.wait_ge(s["out_read"], n * NGRP + arg + 1)
                    for k in range(KB):
                        ins = nc.tensor.transpose(work[:, P * k:P * (k + 1)], osb[arg % 2][:, P * k:P * (k + 1)], ident[:])
                elif what == "turn_out":
                    for k in range(KB):
                        ins = nc.tensor.transpose(work[:, P * k:P * (k + 1)],
                                                  ctxn[:, k].rearrange("p h d -> p (h d)"), ident[:])
                elif what == "project":
                    for k in range(KB):
                        ins = nc.tensor.matmul(work[:, P * k:P * (k + 1)], ctxT[:, P * k:P * (k + 1)], wt["wo"][:],
                                               start=True, stop=True)
                ins.then_inc(s["work_full"], 1)

            def step(b, like, base):
                par = like % 2
                if like == 0:
                    tables.keys_ready(pe)
                for h in range(H):
                    if 0 <= like < NB:
                        cols(b, par, h)
                    if 0 <= like + 1 < NB:
                        rows(b + 1, 1 - par, h)
                    if h == 0 and 0 <= like - 1 < NB:
                        values(b - 1, 1 - par, 3)
                    if h in (4, 8, 12) and 0 <= like < NB:
                        values(b, par, h // 4 - 1)
                    for u, number in work_uses(like, base, h):
                        use(u, number, b, par)

            run(pe, step)

        @block.scalar
        def _(act):
            act.wait_ge(s["w_loaded"], 128)
            act.wait_ge(s["bq_scaled"], 1)

            def probabilities(b, h):
                if h >= NPB or not (isinstance(b, int) and b == 0):
                    if h % 4 == 0:
                        act.wait_ge(s["pv_done"], b * NGRP + h // 4 - 1)
                for i in range(3):
                    act.wait_ge(s["col_full"], b * (3 * H) + 3 * h + i + 1)
                    width = sum(x[2] for x in COLBANKS[i])
                    nc.scalar.activation(prob[h % NPB][:, SEQ * i:SEQ * i + width], col_ps[i][:, 0:width],
                                         ACT.Exp).then_inc(s["exp_done"], 1)

            def outputs(b, g):
                act.wait_ge(s["pv_done"], b * NGRP + g + 1)
                nc.scalar.copy(osb[g % 2][:], out_ps[:]).then_inc(s["out_read"], 1)

            def read(u, number, b, par):
                _, what, arg, which = u
                n = batch_of(b, which)
                npar = (par + {"old": 1, "cur": 0, "new": 1, "new2": 0}[which]) % 2
                if what not in ("turn_x", "q", "k", "turn_max", "turn_out"):
                    return
                act.wait_ge(s["work_full"], number + 1)
                if what == "turn_x":
                    ins = nc.scalar.copy(xnT[npar][:], work[:])
                elif what == "q":
                    ins = nc.scalar.activation(qk32[0][:], work[:], ACT.Identity, bias=bias_qs[:], scale=scale)
                elif what == "k":
                    ins = nc.scalar.activation(qk32[1][:], work[:], ACT.Identity, bias=bias_k[:])
                elif what == "turn_max":
                    if not (isinstance(n, int) and n == 0 and arg == 0):
                        act.wait_ge(s["m_stored"], n * 32 + 16 * arg)
                    ins = nc.scalar.copy(mT[:], work[0:3 * HH, :].bitcast(BF16)[:, 0:SEQ])
                else:
                    ins = nc.scalar.copy(ctxT[:], work[:])
                ins.then_inc(s["work_read"], 1)

            def round_part(b, like, base, h):
                for which, first in ((0, 7), (1, 8)):
                    part = h - first
                    if not 0 <= part < 3:
                        continue
                    m = b + 2
                    if part == 0:
                        act.wait_ge(s["work_read"], number_of(like, base, "qk"[which], 0) + 1)
                        if not (isinstance(m, int) and m == 0):
                            act.wait_ge(s["scr_written"], m * 96)
                    else:
                        act.wait_ge(s[f"rest_{'qk'[which]}"], m * 2 + part)
                    src = (qk32[which], rest[which], qk32[which])[part]
                    nc.scalar.copy(qkp[which][:, part], src[:]).then_inc(s[f"part_{'qk'[which]}"], 1)

            def step(b, like, base):
                par = like % 2
                for h in range(H):
                    if 0 <= like < NB:
                        probabilities(b, h)
                    if h == 0 and 0 <= like - 1 < NB:
                        outputs(b - 1, 3)
                    if h in (4, 8, 12) and 0 <= like < NB:
                        outputs(b, h // 4 - 1)
                    for u, number in work_uses(like, base, h):
                        read(u, number, b, par)
                    if 0 <= like + 2 < NB:
                        round_part(b, like, base, h)

            run(act, step)

        @block.vector
        def _(dve):
            def norm_stats(m):
                for k in range(KB):
                    ins = nc.vector.bn_stats(stats[:, k, :], resid[:, bass.ds(m * KB + k, 1), :].squeeze(1))
                ins.then_inc(s["ln_stats"], 1)
                dve.wait_ge(s["ln_stats"], m + 1)
                if not (isinstance(m, int) and m == 0):
                    dve.wait_ge(s["ln_rstd"], m)
                settle(dve, passed["dve"])
                for k in range(KB):
                    ins = nc.vector.bn_aggr(meanvar[:, k, :], stats[:, k, :])
                ins.then_inc(s["ln_mv"], 1)

            def norm(m):
                dve.wait_ge(s["ln_rstd"], m + 1)
                dve.wait_ge(s["ln_mv"], m + 1)
                for k in range(KB):
                    ins = nc.vector.tensor_scalar(xn[:, k, :], resid[:, bass.ds(m * KB + k, 1), :].squeeze(1),
                                                  meanvar[:, k, 0:1], rstd[:, k:k + 1], ALU.subtract, ALU.mult)
                ins.then_inc(s["xn_ready"], 1)

            def maxima(n, h):
                for i, held in enumerate(ROWBANKS):
                    dve.wait_ge(s["row_full"], n * (3 * H) + 3 * h + i + 1)
                    settle(dve, passed["dve"])
                    for blk, col, width in held:
                        bias = tables.row_bias(h, width)
                        ins = nc.vector.tensor_tensor_reduce(row_ps[i][:, col:col + width], row_ps[i][:, col:col + width], bias, 1.0,
                                                             MASK, ALU.add, ALU.max, rowmax[:, h, blk:blk + 1])
                    ins.then_inc(s["row_read"], 1)

            def split_max(n, half, turned):
                src = rowmax[:, HH * half:HH * (half + 1), :].rearrange("p h k -> p k h")
                dve.wait_ge(s["row_read"], n * (3 * H) + 3 * HH * (half + 1))
                at = n * 8 + 4 * half
                if turned is not None:
                    dve.wait_ge(s["work_read"], turned + 1)
                nc.vector.tensor_scalar(mparts[:, :, 0, :], src, -1.0, None, ALU.mult).then_inc(s["m_chain"], 1)
                dve.wait_ge(s["m_chain"], at + 1)
                nc.vector.scalar_tensor_tensor(mrest[:, 0], src, -1.0, mparts[:, :, 0, :], ALU.mult,
                                               ALU.subtract).then_inc(s["m_chain"], 1)
                dve.wait_ge(s["m_chain"], at + 2)
                nc.vector.tensor_copy(mparts[:, :, 1, :], mrest[:, 0]).then_inc(s["m_chain"], 1)
                dve.wait_ge(s["m_chain"], at + 3)
                nc.vector.tensor_tensor(mrest[:, 1], mrest[:, 0], mparts[:, :, 1, :], ALU.subtract).then_inc(s["m_chain"], 1)
                dve.wait_ge(s["m_chain"], at + 4)
                nc.vector.tensor_copy(mparts[:, :, 2, :], mrest[:, 1]).then_inc(s["m_split"], 1)

            def read(u, number, b, par):
                _, what, arg, which = u
                n = batch_of(b, which)
                npar = (par + {"old": 1, "cur": 0, "new": 1, "new2": 0}[which]) % 2
                if what == "turn_ctx":
                    dve.wait_ge(s["work_full"], number + 1)
                    turned = work[:].rearrange("p (x c) -> p x c", c=32)
                    count = n * NGRP + arg
                    nc.vector.reciprocal(rsum[:], turned[:, :, HD]).then_inc(s["r_ready"], 1)
                    dve.wait_ge(s["r_ready"], count + 1)
                    inv = rsum[:].rearrange("p (k t) -> p k t", t=4)
                    ins = nc.vector.tensor_tensor(ctxn[:, :, 4 * arg:4 * arg + 4, :],
                                                  turned.rearrange("p (k t) c -> p k t c", t=4)[:, :, :, 0:HD],
                                                  inv.unsqueeze(3).broadcast_to([P, KB, 4, HD]), ALU.mult)
                    ins.then_inc(s["work_read"], 1)
                elif what == "v":
                    dve.wait_ge(s["work_full"], number + 1)
                    bias = bias_v[:].rearrange("p (h d) -> p h d", d=HD).unsqueeze(1).broadcast_to([P, KB, H, HD])
                    ins = nc.vector.tensor_tensor(vaug[npar][:, :, :, 0:HD],
                                                  work[:].rearrange("p (k h d) -> p k h d", h=H, d=HD), bias, ALU.add)
                    ins.then_inc(s["work_read"], 1)
                elif what == "project":
                    dve.wait_ge(s["work_full"], number + 1)
                    dve.wait_ge(s["bias_added"], n + 1)
                    rows = resid[:, bass.ds(n * KB, KB), :]
                    ins = nc.vector.tensor_tensor(rows, work[:].rearrange("p (k d) -> p k d", d=D), rows, ALU.add)
                    ins.then_inc(s["work_read"], 1)

            for v in vaug:
                nc.vector.memset(v[:, :, :, HD:32], 0.0).then_inc(s["v_set"], 1)
            tables.make_vectors(dve)
            dve.wait_ge(s["v_set"], 2)
            for v in vaug:
                nc.vector.memset(v[:, :, :, HD:HD + 1], 1.0).then_inc(s["v_set"], 1)
            dve.wait_ge(s["w_loaded"], 128)

            def step(b, like, base):
                par = like % 2
                if 0 <= like < NB:
                    split_max(b, 1, earlier(like, base, "turn_max", 0))
                for h in range(H):
                    if like == -1 and h == 0:
                        tables.rows_ready(dve)
                    if 0 <= like + 1 < NB:
                        maxima(b + 1, h)
                    if h == 9 and 0 <= like + 1 < NB:
                        split_max(b + 1, 0, number_of(like, base, "turn_max", 1) if like >= 0 else None)
                    if h == 2 and 0 <= like + 2 < NB:
                        if loaded and like < 0:
                            dve.wait_ge(loaded[like + 2], 16)
                        norm_stats(b + 2)
                    if h == 4 and 0 <= like + 2 < NB:
                        norm(b + 2)
                    for u, number in work_uses(like, base, h):
                        read(u, number, b, par)

            run(dve, step)


def ffn(nc, name, resid, ident, identb, half_power, passed, w, out=None):
    with ExitStack() as ctx:
        c = Core(nc, ctx, name)
        xh, xl = c.sb("xh", [P, NBLK * P], F32R), c.sb("xl", [P, NBLK * P], F32R)
        acc = c.sb("acc", [P, NBLK * P])
        combT = c.sb("combT", [P, NBLK * P], BF16)
        pick = c.sb("pick", [P, E, P], BF16)
        b1, b2 = c.sb("b1", [P, NE, HC]), c.sb("b2", [P, NE])
        gate_w, gate_b = c.sb("gate_w", [P, E]), c.sb("gate_b", [P, E])
        stats = c.sb("stats", [P, 2, KB, 6])
        meanvar = c.sb("meanvar", [P, 2, KB, 2])
        var_eps = c.sb("var_eps", [P, 2, KB])
        rstd = c.sb("rstd", [P, 2, KB])
        xn = [c.sb(f"xn{i}", [P, KB, D]) for i in range(2)]
        xnT = [c.sb(f"xnT{i}", [P, SEQ]) for i in range(2)]
        logit = c.sb("logit", [P, NBLK, E])
        tri = c.sb("tri", [P, E, E])
        want = c.sb("want", [P, E + 1])
        beats = [c.sb(f"beats{i}", [P, KB, E, E]) for i in range(2)]
        less = c.sb("less", [P, KB, E, E])
        margin = c.sb("margin", [P, NBLK, E])
        top2 = c.sb("top2", [P, 2, NBLK, E])
        prod = c.sb("prod", [P, 2, NBLK, E])
        top = c.sb("top", [P, 2, NBLK])
        gap, ratio, wsum = (c.sb(n, [P, NBLK]) for n in ("gap", "ratio", "wsum"))
        share = c.sb("share", [P, 2, NBLK])
        comb, crest, crest2 = (c.sb(n, [P, NBLK, E]) for n in ("comb", "crest", "crest2"))
        cparts = c.sb("cparts", [P, NBLK, 3, E], BF16)
        w1 = [c.sb(f"w1_{i}", [P, HID]) for i in range(2)]
        w2 = [c.sb(f"w2_{i}", [P, HC, D]) for i in range(2)]
        w1h, w1l = ([c.sb(f"{n}{i}", [P, HID], F32R) for i in range(2)] for n in ("w1h", "w1l"))
        w2h, w2l = ([c.sb(f"{n}{i}", [P, HC, D], F32R) for i in range(2)] for n in ("w2h", "w2l"))
        hid = [c.sb(f"hid{i}", [P, SEQ]) for i in range(HC)]
        hh, hl = ([c.sb(f"{n}{i}", [P, HC, SEQ], F32R) for i in range(2)] for n in ("hh", "hl"))
        weight = [c.sb(f"weight{i}", [P, SEQ]) for i in range(2)]
        scaled = [c.sb(f"scaled{i}", [P, SEQ]) for i in range(2)]
        hid_ps = [c.bank(f"hid{i}") for i in range(HC)]
        out_ps = [c.bank(f"out{i}") for i in range(2)]
        weight_ps, turn_ps = c.bank("weight"), c.bank("turn")
        logit_ps = weight_ps[:, 0:KB * E]
        names = ("gate_loaded w0_loaded w1_loaded w_high w_split  zeroed made ln_stats ln_mv ln_eps "
                 "ln_rstd xn_ready turned xnT_ready xh_ready xl_ready logit_full logit_read rank_chain ranked top_chain "
                 "compared gap_ready ratio_ready parts_ready comb_full comb_read hid_full gelu_done h_high h_split out_full weight_full "
                 "weight_read combined added resid_added").split() + (["out_stored"] if out is not None else [])
        s = {n: c.sem(n) for n in names}
        block = ctx.enter_context(nc.Block())
        LAST = NE - 1
        LAG = 3

        def run(eng, turn):
            for e in (0, 1):
                for b in range(NB):
                    turn(e, e, b)
            with eng.Fori(0, (NE - 3) // 2) as i:
                for r in range(2):
                    for b in range(NB):
                        turn(i * 2 + 2 + r, 2 + r, b)
            for b in range(NB):
                turn(LAST, LAST, b)

        def tokens(b):
            return slice(SEQ * b, SEQ * (b + 1))

        def blocks(b):
            return slice(KB * b, KB * (b + 1))

        @block.sync
        def _(sp):
            def load(e, like):
                par = like % 2
                if like >= 2:
                    sp.wait_ge(s["w_split"], 2 * e - 2)
                sp.dma_start(w1[par][:], w["w1"][bass.ds(e, 1)].squeeze(0)).then_inc(s[f"w{par}_loaded"], 16)
                sp.dma_start(w2[par][:], w["w2"][bass.ds(e, 1)].squeeze(0)).then_inc(s[f"w{par}_loaded"], 16)

            load(0, 0)
            sp.dma_start(gate_w[:], w["gate_w"]).then_inc(s["gate_loaded"], 16)
            sp.dma_start(gate_b[:], w["gate_b"].partition_broadcast(P)).then_inc(s["gate_loaded"], 16)
            sp.dma_start(b1[:], w["b1"]).then_inc(s["gate_loaded"], 16)
            sp.dma_start(b2[:], w["b2"]).then_inc(s["gate_loaded"], 16)
            load(1, 1)
            with sp.Fori(0, (NE - 3) // 2) as i:
                load(i * 2 + 2, 2)
                load(i * 2 + 3, 3)
            load(LAST, LAST)
            if out is not None:
                rows = out.rearrange("b (k p) d -> p (b k) d", p=P)
                for b in range(NB):
                    sp.wait_ge(s["resid_added"], b + 1)
                    sp.dma_start(rows[:, blocks(b), :], resid[:, blocks(b), :]).then_inc(s["out_stored"], 16)
                sp.wait_ge(s["out_stored"], 16 * NB)
            sp.wait_ge(s["w0_loaded"], 16 * (NE + 1))

        @block.gpsimd
        def _(pool):
            def rstds(b):
                pool.wait_ge(s["ln_mv"], b + 1)
                nc.gpsimd.tensor_scalar(var_eps[:, b % 2], meanvar[:, b % 2, :, 1], EPS, None, ALU.add).then_inc(s["ln_eps"], 1)
                pool.wait_ge(s["ln_eps"], b + 1)
                nc.gpsimd.tensor_tensor(rstd[:, b % 2], var_eps[:, b % 2], half_power[:], ALU.pow).then_inc(s["ln_rstd"], 1)

            def low_part(b):
                pool.wait_ge(s["xh_ready"], b + 1)
                nc.gpsimd.tensor_tensor(xl[:, tokens(b)], xnT[b % 2][:], xh[:, tokens(b)].bitcast(F32),
                                        ALU.subtract).then_inc(s["xl_ready"], 1)

            def rank(b):
                count = 4 * b

                def link(ins):
                    nonlocal count
                    count += 1
                    ins.then_inc(s["rank_chain"], 1)
                    pool.wait_ge(s["rank_chain"], count)

                pool.wait_ge(s["compared"], b + 1)
                ge = beats[b % 2]
                link(nc.gpsimd.tensor_tensor(ge[:], ge[:], tri[:].unsqueeze(1).broadcast_to([P, KB, E, E]), ALU.mult))
                link(nc.gpsimd.tensor_tensor(less[:], ge[:], ge[:].rearrange("p k e f -> p k f e"), ALU.subtract))
                for n in (4, 2):
                    link(nc.gpsimd.tensor_tensor(less[:, :, :, 0:n], less[:, :, :, 0:n], less[:, :, :, n:2 * n], ALU.add))
                nc.gpsimd.tensor_tensor(margin[:, blocks(b), :], less[:, :, :, 0], less[:, :, :, 1], ALU.add).then_inc(s["ranked"], 1)
                pool.wait_ge(s["ranked"], b + 1)

            def masks():
                nc.gpsimd.memset(tri[:], 1.0).then_inc(s["zeroed"], 1)
                nc.gpsimd.memset(pick[:].bitcast(F32), 0.0).then_inc(s["zeroed"], 1)
                nc.gpsimd.memset(combT[:].bitcast(F32), 0.0).then_inc(s["zeroed"], 1)
                pool.wait_ge(s["zeroed"], 3)
                nc.gpsimd.affine_select(out=tri[:], in_=tri[:], compare_op=ALU.is_gt, fill=0.0, base=0,
                                        pattern=[[1, E], [-1, E]], channel_multiplier=0).then_inc(s["made"], 1)
                for part in range(3):
                    pool.wait_ge(s["made"], part + 1)
                    nc.gpsimd.affine_select(out=pick[:], in_=pick[:], compare_op=ALU.not_equal, fill=1.0, base=-E * part,
                                            pattern=[[-1, E], [0, P]], channel_multiplier=1).then_inc(s["made"], 1)
                for n in range(E + 1):
                    ins = nc.gpsimd.memset(want[:, n:n + 1], float(n + 1 - E))
                ins.then_inc(s["made"], 1)
                pool.wait_ge(s["made"], 5)

            def high(e, like):
                par = like % 2
                pool.wait_ge(s[f"w{par}_loaded"], (e - par) * 16 + 32)
                if like >= 2:
                    pool.wait_ge(s["out_full"], e * NB - NB)
                settle(pool, passed["pool"])
                nc.gpsimd.tensor_copy(w1h[par][:], w1[par][:])
                nc.gpsimd.tensor_copy(w2h[par][:], w2[par][:]).then_inc(s["w_high"], 1)

            def low(e, like):
                par = like % 2
                for n, (whole, part, left) in enumerate(((w1, w1h, w1l), (w2, w2h, w2l))):
                    pool.wait_ge(s["w_high"], n + 1 if like == 0 else e + 2)
                    nc.gpsimd.tensor_tensor(left[par][:].rearrange("p k d -> p (k d)") if n else left[par][:],
                                            whole[par][:].rearrange("p k d -> p (k d)") if n else whole[par][:],
                                            (part[par][:].rearrange("p k d -> p (k d)") if n else part[par][:]).bitcast(F32),
                                            ALU.subtract).then_inc(s["w_split"], 1)

            def turn(e, like, b):
                if like == 0:
                    if b + 4 < NB:
                        rstds(b + 4)
                    if b + 2 < NB:
                        low_part(b + 2)
                if b == 1 and like + 1 < NE:
                    high(e + 1, like + 1)
                    low(e + 1, like + 1)
                if like == 0:
                    if b == 0:
                        masks()
                    rank(b)
                else:
                    pool.wait_ge(s["combined"], e * NB + b + 1)
                    nc.gpsimd.tensor_tensor(acc[:, tokens(b)], acc[:, tokens(b)], scaled[b % 2][:], ALU.add).then_inc(s["added"], 1)

            rstds(0)
            rstds(1)
            low(0, 0)
            low_part(0)
            rstds(2)
            low_part(1)
            rstds(3)
            run(pool, turn)

        @block.tensor
        def _(pe):
            def turn_x(b):
                pe.wait_ge(s["xn_ready"], b + 1)
                if b > 0:
                    pe.wait_ge(s["xh_ready"], b)
                for k in range(KB):
                    ins = nc.tensor.transpose(turn_ps[:, P * k:P * (k + 1)], xn[b % 2][:, k, :], ident[:])
                ins.then_inc(s["turned"], 1)

            def gate(b):
                pe.wait_ge(s["xnT_ready"], b + 1)
                if b > 0:
                    pe.wait_ge(s["logit_read"], b)
                for k in range(KB):
                    ins = nc.tensor.matmul(logit_ps[:, E * k:E * (k + 1)], xnT[b % 2][:, P * k:P * (k + 1)], gate_w[:],
                                           start=True, stop=True)
                ins.then_inc(s["logit_full"], 1)

            def turn_comb():
                pe.wait_ge(s["parts_ready"], 1)
                for t in range(NBLK // 8):
                    bank = (turn_ps, weight_ps)[t % 2]
                    if t >= 2:
                        pe.wait_ge(s["comb_read"], t - 1)
                    for k in range(8):
                        ins = nc.tensor.transpose(bank[0:3 * E, P // 2 * k:P // 2 * (k + 1)].bitcast(BF16),
                                                  cparts[:, 8 * t + k].rearrange("p a e -> p (a e)"), identb[:])
                    ins.then_inc(s["comb_full"], 1)
                pe.wait_ge(s["comb_read"], NBLK // 8)

            def hidden(e, like, b):
                par, t = like % 2, e * NB + b
                if b == 0:
                    pe.wait_ge(s["w_split"], 2 * e + 1)
                if like == 0:
                    pe.wait_ge(s["xl_ready"], b + 1)
                for k in range(HC):
                    if not (like == 0 and b == 0):
                        pe.wait_ge(s["gelu_done"], t * HC - HC + k + 1)
                    cols = slice(P * k, P * (k + 1))
                    nc.tensor.matmul(hid_ps[k][:], w1h[par][:, cols], xh[:, tokens(b)], start=True, stop=False)
                    nc.tensor.matmul(hid_ps[k][:], w1h[par][:, cols], xl[:, tokens(b)], start=False, stop=False)
                    nc.tensor.matmul(hid_ps[k][:], w1l[par][:, cols], xh[:, tokens(b)], start=False,
                                     stop=True).then_inc(s["hid_full"], 1)

            def output(e, like, b):
                par, t = like % 2, e * NB + b
                if like > 0:
                    if not (like == 1 and b == 0):
                        pe.wait_ge(s["weight_read"], t - NB)
                    nc.tensor.matmul(weight_ps[:], pick[:, bass.ds(e - 1, 1), :].squeeze(1), combT[:, tokens(b)],
                                     start=True, stop=True).then_inc(s["weight_full"], 1)
                if b == 0:
                    pe.wait_ge(s["w_split"], 2 * e + 2)
                if not (like == 0 and b < 2):
                    pe.wait_ge(s["combined"], t - 1)
                for k in range(HC):
                    pe.wait_ge(s["h_split"], t * HC + k + 1)
                    nc.tensor.matmul(out_ps[b % 2][:], w2h[par][:, k, :], hh[b % 2][:, k, :], start=(k == 0), stop=False)
                    nc.tensor.matmul(out_ps[b % 2][:], w2h[par][:, k, :], hl[b % 2][:, k, :], start=False, stop=False)
                    ins = nc.tensor.matmul(out_ps[b % 2][:], w2l[par][:, k, :], hh[b % 2][:, k, :], start=False,
                                           stop=(k == HC - 1))
                ins.then_inc(s["out_full"], 1)

            def turn_back(b):
                pe.wait_ge(s["added"], (LAST - 1) * NB + b + 1)
                if b > 0:
                    pe.wait_ge(s["resid_added"], b)
                for k in range(KB):
                    n = b * KB + k
                    ins = nc.tensor.transpose(turn_ps[:, P * k:P * (k + 1)], acc[:, P * n:P * (n + 1)], ident[:])
                ins.then_inc(s["turned"], 1)

            def turn(e, like, b):
                hidden(e, like, b)
                if like == 1 and b == 1:
                    turn_comb()
                if b > 0:
                    output(e, like, b - 1)
                elif like > 0:
                    output(e - 1, like - 1, NB - 1)
                if like == 0 and b + 2 < NB:
                    turn_x(b + 2)
                if like == 0 and b + 1 < NB:
                    gate(b + 1)
                if like == LAST and b >= LAG:
                    turn_back(b - LAG)

            turn_x(0)
            pe.wait_ge(s["gate_loaded"], 64)
            gate(0)
            turn_x(1)
            run(pe, turn)
            output(LAST, LAST, NB - 1)
            for b in range(NB - LAG, NB):
                turn_back(b)

        @block.scalar
        def _(act):
            def bring(b):
                act.wait_ge(s["turned"], b + 1)
                if b >= 2:
                    act.wait_ge(s["logit_full"], b - 1)
                    act.wait_ge(s["xl_ready"], b - 1)
                nc.scalar.copy(xnT[b % 2][:], turn_ps[:]).then_inc(s["xnT_ready"], 1)
                nc.scalar.copy(xh[:, tokens(b)], turn_ps[:]).then_inc(s["xh_ready"], 1)

            def broadcast(e, like, b):
                if like == 0:
                    return
                t = e * NB + b
                act.wait_ge(s["weight_full"], t - NB + 1)
                if not (like == 1 and b < 2):
                    act.wait_ge(s["combined"], t - 1)
                nc.scalar.copy(weight[b % 2][:], weight_ps[:]).then_inc(s["weight_read"], 1)

            def rounded(like, b, t, k):
                if k == 0 and not (like == 0 and b < 2):
                    act.wait_ge(s["out_full"], t - 1)
                act.wait_ge(s["gelu_done"], t * HC + k + 1)
                nc.scalar.copy(hh[b % 2][:, k, :], hid[k][:]).then_inc(s["h_high"], 1)

            def turn(e, like, b):
                t = e * NB + b
                for k in range(HC):
                    act.wait_ge(s["hid_full"], t * HC + k + 1)
                    if not (like == 0 and b == 0):
                        act.wait_ge(s["h_split"], t * HC - HC + k + 1)
                    nc.scalar.activation(hid[k][:], hid_ps[k][:], ACT.Gelu,
                                         bias=b1[:, bass.ds(e, 1), k:k + 1].squeeze(1)).then_inc(s["gelu_done"], 1)
                    if k > 0:
                        rounded(like, b, t, k - 1)
                rounded(like, b, t, HC - 1)
                if b > 0:
                    broadcast(e, like, b - 1)
                elif like > 0:
                    broadcast(e - 1, like - 1, NB - 1)
                if like == 0 and b + 2 < NB:
                    bring(b + 2)
                if like == 1 and b == 0:
                    act.wait_ge(s["gap_ready"], 1)
                    nc.scalar.activation(ratio[:], gap[:], ACT.Exp).then_inc(s["ratio_ready"], 1)
                    act.wait_ge(s["zeroed"], 3)
                    for n in range(NBLK // 8):
                        act.wait_ge(s["comb_full"], n + 1)
                        nc.scalar.copy(combT[0:3 * E, 8 * P * n:8 * P * (n + 1)],
                                       (turn_ps, weight_ps)[n % 2][0:3 * E, :].bitcast(BF16)).then_inc(s["comb_read"], 1)

            act.wait_ge(s["w0_loaded"], 32)
            nc.scalar.copy(w1h[0][:], w1[0][:]).then_inc(s["w_high"], 1)
            nc.scalar.copy(w2h[0][:], w2[0][:]).then_inc(s["w_high"], 1)
            bring(0)
            bring(1)
            act.wait_ge(s["gate_loaded"], 64)
            run(act, turn)
            broadcast(LAST, LAST, NB - 1)

        @block.vector
        def _(dve):
            def norm_stats(b):
                for k in range(KB):
                    ins = nc.vector.bn_stats(stats[:, b % 2, k, :], resid[:, KB * b + k, :])
                ins.then_inc(s["ln_stats"], 1)
                dve.wait_ge(s["ln_stats"], b + 1)
                for k in range(KB):
                    ins = nc.vector.bn_aggr(meanvar[:, b % 2, k, :], stats[:, b % 2, k, :])
                ins.then_inc(s["ln_mv"], 1)

            def norm(b):
                dve.wait_ge(s["ln_rstd"], b + 1)
                if b >= 2:
                    dve.wait_ge(s["turned"], b - 1)
                for k in range(KB):
                    ins = nc.vector.tensor_scalar(xn[b % 2][:, k, :], resid[:, KB * b + k, :], meanvar[:, b % 2, k, 0:1],
                                                  rstd[:, b % 2, k:k + 1], ALU.subtract, ALU.mult)
                ins.then_inc(s["xn_ready"], 1)
                dve.wait_ge(s["xn_ready"], b + 1)

            def logits(b):
                dve.wait_ge(s["logit_full"], b + 1)
                nc.vector.tensor_tensor(logit[:, blocks(b), :], logit_ps.rearrange("p (k e) -> p k e", e=E),
                                        gate_b[:].unsqueeze(1).broadcast_to([P, KB, E]), ALU.add).then_inc(s["logit_read"], 1)
                dve.wait_ge(s["logit_read"], b + 1)
                if b >= 2:
                    dve.wait_ge(s["ranked"], b - 1)
                mine = logit[:, blocks(b), :]
                nc.vector.tensor_tensor(beats[b % 2][:], mine.unsqueeze(2).broadcast_to([P, KB, E, E]),
                                        mine.unsqueeze(3).broadcast_to([P, KB, E, E]), ALU.is_ge).then_inc(s["compared"], 1)

            chained = [0]

            def link(ins):
                chained[0] += 1
                ins.then_inc(s["top_chain"], 1)
                dve.wait_ge(s["top_chain"], chained[0])

            def top_gap():
                dve.wait_ge(s["ranked"], NB)
                for r in range(2):
                    ins = nc.vector.tensor_tensor(top2[:, r], margin[:], want[:, r:r + E].unsqueeze(1).broadcast_to([P, NBLK, E]),
                                                  ALU.is_equal)
                link(ins)
                link(nc.vector.tensor_tensor(prod[:], top2[:], logit[:].unsqueeze(1).broadcast_to([P, 2, NBLK, E]), ALU.mult))
                link(nc.vector.tensor_reduce(top[:], prod[:], AX.X, ALU.add))
                nc.vector.tensor_tensor(gap[:], top[:, 1], top[:, 0], ALU.subtract).then_inc(s["gap_ready"], 1)

            def shares():
                dve.wait_ge(s["ratio_ready"], 1)
                link(nc.vector.tensor_scalar(wsum[:], ratio[:], 1.0, None, ALU.add))
                link(nc.vector.reciprocal(share[:, 0], wsum[:]))
                link(nc.vector.tensor_tensor(share[:, 1], ratio[:], share[:, 0], ALU.mult))
                link(nc.vector.tensor_tensor(prod[:], top2[:], share[:].unsqueeze(3).broadcast_to([P, 2, NBLK, E]), ALU.mult))
                link(nc.vector.tensor_tensor(comb[:], prod[:, 0], prod[:, 1], ALU.add))
                link(nc.vector.tensor_copy(cparts[:, :, 0, :], comb[:]))
                link(nc.vector.tensor_tensor(crest[:], comb[:], cparts[:, :, 0, :], ALU.subtract))
                link(nc.vector.tensor_copy(cparts[:, :, 1, :], crest[:]))
                link(nc.vector.tensor_tensor(crest2[:], crest[:], cparts[:, :, 1, :], ALU.subtract))
                nc.vector.tensor_copy(cparts[:, :, 2, :], crest2[:]).then_inc(s["parts_ready"], 1)

            def combine(e, like, b):
                t = e * NB + b
                bias = b2[:, bass.ds(e, 1)]
                dve.wait_ge(s["out_full"], t + 1)
                if like == 0:
                    nc.vector.tensor_scalar(acc[:, tokens(b)], out_ps[b % 2][:], bias, None, ALU.add).then_inc(s["combined"], 1)
                    return
                dve.wait_ge(s["weight_read"], t - NB + 1)
                if not (like == 1 and b < 2):
                    dve.wait_ge(s["added"], t - NB - 1)
                nc.vector.scalar_tensor_tensor(scaled[b % 2][:], out_ps[b % 2][:], bias, weight[b % 2][:], ALU.add,
                                               ALU.mult).then_inc(s["combined"], 1)

            def add_back(b):
                dve.wait_ge(s["turned"], NB + b + 1)
                rows = resid[:, blocks(b), :].rearrange("p k d -> p (k d)")
                nc.vector.tensor_tensor(rows, turn_ps[:], rows, ALU.add).then_inc(s["resid_added"], 1)

            def turn(e, like, b):
                t = e * NB + b
                for k in range(HC):
                    dve.wait_ge(s["h_high"], t * HC + k + 1)
                    nc.vector.tensor_tensor(hl[b % 2][:, k, :], hid[k][:], hh[b % 2][:, k, :].bitcast(F32),
                                            ALU.subtract).then_inc(s["h_split"], 1)
                if b > 0:
                    combine(e, like, b - 1)
                elif like > 0:
                    combine(e - 1, like - 1, NB - 1)
                if like == 0:
                    if b + 1 < NB:
                        logits(b + 1)
                    if b + 4 < NB:
                        norm_stats(b + 4)
                    if b + 3 < NB:
                        norm(b + 3)
                if like == 1 and b == 0:
                    top_gap()
                    shares()
                if like == LAST and b >= LAG:
                    add_back(b - LAG)

            norm_stats(0)
            norm_stats(1)
            norm(0)
            norm_stats(2)
            norm(1)
            norm_stats(3)
            dve.wait_ge(s["gate_loaded"], 64)
            logits(0)
            norm(2)
            run(dve, turn)
            combine(LAST, LAST, NB - 1)
            for b in range(NB - LAG, NB):
                add_back(b)


def hybrid(nc, x, a, m, f, rel_emb, onehot, out):
    nc.disable_value_cache = True
    with ExitStack() as ctx:
        resid = ctx.enter_context(nc.sbuf_tensor("resid", [P, NBLK, D], F32))
        ident = ctx.enter_context(nc.sbuf_tensor("ident", [P, P], F32))
        identb = ctx.enter_context(nc.sbuf_tensor("identb", [P, P], BF16))
        half_power = ctx.enter_context(nc.sbuf_tensor("half_power", [P, KB], F32))
        zeros = nc.dram_tensor("zeros", (3, HH, SEQ), BF16, kind="Internal").ap()
        scratch = nc.dram_tensor("qk_parts", (2, 2, 3, HD, H, SEQ), BF16, kind="Internal").ap()
        maxima = nc.dram_tensor("maxima", (2, 3 * HH, SEQ), BF16, kind="Internal").ap()
        vectors = nc.dram_tensor("bias_vectors", (3, H, 16, NV), BF16, kind="Internal").ap()
        loaded = [ctx.enter_context(nc.semaphore(n)) for n in ("first_loaded", "rest_loaded")]
        passed = {n: ctx.enter_context(nc.semaphore(n + "_passed")) for n in ("dve", "pool")}
        with ExitStack() as first:
            load_constants(nc, first, x, resid, ident, identb, half_power, loaded)
        attention(nc, "a", resid, ident, identb, half_power, passed, a, (rel_emb, onehot, vectors), scratch, maxima, zeros, loaded)
        ffn(nc, "f", resid, ident, identb, half_power, passed, f)
        attention(nc, "m", resid, ident, identb, half_power, passed, m, None, scratch, maxima, zeros, None)
        ffn(nc, "g", resid, ident, identb, half_power, passed, f, out)


def distance_onehot():
    import math
    import numpy as np

    n = np.maximum(np.stack([np.arange(NV) - (P - 1), 2 * P - 1 - np.arange(NV)]), 0)
    exact = BUCKETS // 2
    far = exact + (np.log(np.maximum(n, 1).astype(np.float32) / exact) / math.log(MAX_DIST / exact)
                   * (BUCKETS - exact)).astype(np.int32)
    bucket = np.where(n < exact, n, np.minimum(far, BUCKETS - 1))
    return (bucket[:, None, :] == np.arange(BUCKETS)[None, :, None]).astype(np.float32)


def kernel(**inputs):
    import numpy as np
    import concourse.bacc as bacc
    from concourse.bass_utils import run_bass_kernel_spmd

    nc = bacc.Bacc("TRN2", target_bir_lowering=False, num_devices=1)
    arrays = {}

    def given(name, a):
        a = np.ascontiguousarray(a)
        arrays[f"in_{name}"] = a
        return nc.dram_tensor(f"in_{name}", a.shape, mybir.dt.from_np(a.dtype), kind="ExternalInput").ap()

    def of(prefix, name):
        return np.asarray(inputs[f"L0_{prefix}_{name}"])

    x = given("x", of("attn_a", "x"))
    a = {n: given("a_" + n, of("attn_a", n.replace("w", "W")).T) for n in ("wq", "wk", "wv", "wo")}
    m = {n: given("b_" + n, of("attn_b", k)) for n, k in (("wq", "Wq"), ("wk", "Wk"), ("wv", "Wv"), ("wo", "Wp"))}
    for n in ("bq", "bk", "bv"):
        a[n], m[n] = given("a_" + n, of("attn_a", n)), given("b_" + n, of("attn_b", n))
    a["bo"], m["bo"] = given("a_bo", of("attn_a", "bo")), given("b_bo", of("attn_b", "bp"))
    w1 = np.concatenate([of("ffn", "ws1")[None], of("ffn", "w1")])
    w2 = np.concatenate([of("ffn", "ws2")[None], of("ffn", "w2")])
    b1 = np.concatenate([of("ffn", "bs1")[None], of("ffn", "b1")])
    b2 = np.concatenate([of("ffn", "bs2")[None], of("ffn", "b2")])
    f = {
        "gate_w": given("gate_w", of("ffn", "gate_w")), "gate_b": given("gate_b", of("ffn", "gate_b")),
        "w1": given("w1", w1), "w2": given("w2", w2.reshape(NE, HC, P, D).transpose(0, 2, 1, 3)),
        "b1": given("b1", b1.reshape(NE, HC, P).transpose(2, 0, 1)), "b2": given("b2", b2.T),
    }
    rel_emb = given("rel_emb", of("attn_a", "rel_emb"))
    onehot = given("onehot", distance_onehot())
    out = nc.dram_tensor("out", (NB, SEQ, D), F32, kind="ExternalOutput").ap()
    hybrid(nc, x, a, m, f, rel_emb, onehot, out)
    r = run_bass_kernel_spmd(nc, [arrays], core_ids=[0])
    return r.results[0]["out"]
```

```python
from contextlib import ExitStack

import concourse.bass as bass
from concourse import mybir

F32 = mybir.dt.float32
F32R = mybir.dt.float32r
BF16 = mybir.dt.bfloat16
F16 = mybir.dt.float16
ALU = mybir.AluOpType
ACT = mybir.ActivationFunctionType
AX = mybir.AxisListType

P = 128
NB, SEQ, D = 8, 512, 128
KB = SEQ // P
NBLK = NB * KB
H, HD = 16, 8
HH = H // 2
NGRP = H // 4
E, NE, HID = 8, 9, 512
HC = HID // P
BUCKETS, MAX_DIST = 32, 128
NV = 3 * P
EPS = 1e-5
MASK = -1e30
SCALE = float(HD) ** -0.5
QRUNS = [(0, 0, 3), (1, 0, 2), (2, 0, 1)]
KRUNS = [(0, 1, 3), (0, 1, 2), (0, 0, 1)]
HALF_DMAS = len(QRUNS + KRUNS) + 1
MROW = 96
FAR = 113
NEAR = P + FAR - 1
TWO_ONES = float.fromhex("0x1.007f00p+0")
NPB = 8
PW = SEQ + (SEQ - P) + P + (SEQ - 2 * P)
PCOL = {0: (0, 0), 1: (SEQ, P), 3: (2 * SEQ - P, 3 * P), 2: (2 * SEQ, 2 * P)}
ROWBANKS = [[(3, 0, 512)], [(2, 0, 384), (0, 384, 128)], [(1, 0, 256)]]
COLBANKS = [[(0, 0, 512)], [(1, 0, 384), (3, 384, 128)], [(2, 0, 256)]]


def settle(eng, passed):
    eng.sem_inc(passed, 1)


class Core:

    def __init__(self, nc, ctx, prefix, clear=False):
        self.nc, self.ctx, self.prefix, self.sems = nc, ctx, prefix, [] if clear else None
        if clear:
            ctx.callback(self.clear)

    def clear(self):
        self.nc.clear_and_free_semaphores(self.sems)
        self.nc.all_engine_barrier()

    def sb(self, name, shape, dt=F32):
        return self.ctx.enter_context(self.nc.sbuf_tensor(f"{self.prefix}_{name}", shape, dt))

    def bank(self, name, dt=F32):
        return self.ctx.enter_context(self.nc.psum_tensor(f"{self.prefix}_{name}_ps", [P, 2048 // (4 if dt == F32 else 2)], dt))

    def sem(self, name):
        if self.sems is None:
            return self.ctx.enter_context(self.nc.semaphore(f"{self.prefix}_{name}"))
        self.sems.append(self.nc.alloc_semaphore(f"{self.prefix}_{name}"))
        return self.sems[-1]


def load_constants(nc, ctx, x, resid, ident, identb, half_power, loaded):
    c = Core(nc, ctx, "init")
    zeroed, made = c.sem("zeroed"), c.sem("made")
    block = ctx.enter_context(nc.Block())
    rows = x.rearrange("b (k p) d -> p (b k) d", p=P)

    @block.sync
    def _(sp):
        for sem, blocks in zip(loaded, (slice(0, KB), slice(KB, NBLK))):
            sp.dma_start(resid[:, blocks, :], rows[:, blocks, :]).then_inc(sem, 16)

    @block.gpsimd
    def _(pool):
        nc.gpsimd.memset(half_power[:], -0.5)
        nc.gpsimd.memset(ident[:], 0.0).then_inc(zeroed, 1)
        nc.gpsimd.memset(identb[:], 0.0).then_inc(zeroed, 1)
        pool.wait_ge(zeroed, 2)
        for m in (ident, identb):
            nc.gpsimd.affine_select(out=m[:], in_=m[:], compare_op=ALU.not_equal, fill=1.0, base=0,
                                    pattern=[[-1, P]], channel_multiplier=1).then_inc(made, 1)


class RelativeTables:

    COPIES = 16

    def __init__(self, nc, c, given, psum, room):
        self.nc = nc
        self.rel_emb, self.onehot, self.scratch = given
        self.keyhigh = c.sb("keyhigh", [P, H, NEAR], BF16)
        self.keylow = c.sb("keylow", [P, H, NEAR], F16)
        self.rowbias = c.sb("rowbias", [P, H, SEQ], BF16)
        self.rel, self.far = room[0][0:BUCKETS, 0:H], room[1][0:H, 2 * NV:2 * NV + 1]
        self.hot = room[0][0:BUCKETS, H:H + 2 * NV].rearrange("b (t n) -> b t n", t=2)
        self.vec = room[1][0:H, 0:2 * NV].rearrange("h (t n) -> h t n", t=2)
        self.parts = room[2][0:H, 0:3 * NV // 2].bitcast(BF16).rearrange("h (t n) -> h t n", t=3)
        self.up, self.down = psum
        names = "rel_loaded vec_full vec_chain vec_ready stored row_spread key_spread far_zeroed"
        self.s = {n: c.sem(n) for n in names.split()}

    def load(self, sp):
        sp.dma_start(self.rel, self.rel_emb).then_inc(self.s["rel_loaded"], 16)
        sp.dma_start(self.hot, self.onehot.rearrange("t b n -> b t n")).then_inc(self.s["rel_loaded"], 16)

    def store(self, sp):
        sp.wait_ge(self.s["vec_ready"], 1)
        dst = self.scratch.rearrange("t h c n -> h t c n")
        for t in range(3):
            sp.dma_start(dst[:, t], self.parts[:, t, :].unsqueeze(1).broadcast_to([H, self.COPIES, NV])).then_inc(
                self.s["stored"], 16)
        sp.wait_ge(self.s["stored"], 48)

    def spread(self, sp, t, tile, at, width, sem):
        for a in range(P // self.COPIES):
            src = bass.AP(self.scratch.tensor, t * H * self.COPIES * NV + P - 1 - self.COPIES * a,
                          [[NV - 1, self.COPIES], [self.COPIES * NV, H], [1, width]])
            into = slice(self.COPIES * a, self.COPIES * (a + 1))
            sp.dma_start(tile[into, :, at:at + width], src).then_inc(self.s[sem], 16)

    def spread_rows(self, sp):
        self.spread(sp, 2, self.rowbias, 2 * P, 2 * P, "row_spread")

    def spread_keys(self, sp):
        self.spread(sp, 0, self.keyhigh, 0, NEAR, "key_spread")
        self.spread(sp, 1, self.keylow[:].bitcast(BF16), 0, NEAR, "key_spread")

    def zero_far(self, pool):
        self.nc.gpsimd.memset(self.rowbias[:, :, 0:2 * P], 0.0).then_inc(self.s["far_zeroed"], 1)

    def look_up(self, pe):
        pe.wait_ge(self.s["rel_loaded"], 32)
        for t, bank in enumerate((self.up, self.down)):
            self.nc.tensor.matmul(bank[0:H, 0:NV], self.rel, self.hot[:, t, :], start=True,
                                  stop=True).then_inc(self.s["vec_full"], 1)

    def make_vectors(self, dve):
        nc, vec, parts, done = self.nc, self.vec, self.parts, [0]

        def link(ins):
            done[0] += 1
            ins.then_inc(self.s["vec_chain"], 1)
            dve.wait_ge(self.s["vec_chain"], done[0])

        dve.wait_ge(self.s["vec_full"], 2)
        link(nc.vector.tensor_copy(self.far, self.up[0:H, NV - 1:NV]))
        for t, bank in enumerate((self.up, self.down)):
            ins = nc.vector.tensor_scalar(vec[:, t, :], bank[0:H, 0:NV], self.far[:, 0:1], SCALE, ALU.subtract, ALU.mult)
        link(ins)
        nc.vector.memset(vec[:, 0, 0:P - 1], MASK)
        link(nc.vector.memset(vec[:, 1, 2 * P:], MASK))
        nc.vector.tensor_copy(parts[:, 2, :], vec[:, 1, :])
        link(nc.vector.tensor_copy(parts[:, 0, :], vec[:, 0, :]))
        low = parts[:, 1, :].bitcast(F16)
        link(nc.vector.tensor_tensor(low, vec[:, 0, :], parts[:, 0, :], ALU.subtract))
        nc.vector.memset(low[:, 0:P - 1], 0.0).then_inc(self.s["vec_ready"], 1)

    def banks_free(self, pe):
        pe.wait_ge(self.s["vec_chain"], 2)

    def rows_ready(self, dve):
        dve.wait_ge(self.s["row_spread"], 16 * P // self.COPIES)
        dve.wait_ge(self.s["far_zeroed"], 1)

    def keys_ready(self, pe):
        pe.wait_ge(self.s["key_spread"], 32 * P // self.COPIES)

    def key_parts(self, h, width):
        width = min(width, NEAR)
        return [(self.keyhigh[:, h, 0:width], width), (self.keylow[:, h, 0:width], width)]

    def row_bias(self, h, width):
        return self.rowbias[:, h, SEQ - width:]


class CausalTables:

    def __init__(self, nc, c):
        self.nc = nc
        self.keymask = c.sb("keymask", [P, P], BF16)
        self.rowmask = c.sb("rowmask", [P, SEQ], BF16)
        self.zeroed, self.made = c.sem("mask_zeroed"), c.sem("mask_made")

    def load(self, sp):
        pass

    store = spread_rows = spread_keys = look_up = make_vectors = banks_free = load

    def zero_far(self, pool):
        nc = self.nc
        nc.gpsimd.memset(self.keymask[:], 0.0).then_inc(self.zeroed, 1)
        nc.gpsimd.memset(self.rowmask[:], 0.0).then_inc(self.zeroed, 1)
        pool.wait_ge(self.zeroed, 2)
        nc.gpsimd.affine_select(out=self.keymask[:], in_=self.keymask[:], compare_op=ALU.is_ge, fill=MASK, base=0,
                                pattern=[[1, P]], channel_multiplier=-1).then_inc(self.made, 1)
        nc.gpsimd.affine_select(out=self.rowmask[:, 3 * P:], in_=self.rowmask[:, 3 * P:], compare_op=ALU.is_ge,
                                fill=MASK, base=0, pattern=[[-1, P]], channel_multiplier=1).then_inc(self.made, 1)

    def rows_ready(self, eng):
        eng.wait_ge(self.made, 2)

    keys_ready = rows_ready

    def key_parts(self, h, width):
        return [(self.keymask[:], P)]

    def row_bias(self, h, width):
        return self.rowmask[:, SEQ - width:]


def attention(nc, name, resid, ident, identb, half_power, passed, w, relative, scratch, maxima, zeros, loaded):
    with ExitStack() as ctx:
        c = Core(nc, ctx, name)
        scale = 1.0 if relative else SCALE
        qs = [c.sb(f"qs{i}", [P, H, SEQ], BF16) for i in range(2)]
        ks = [c.sb(f"ks{i}", [P, H, SEQ], BF16) for i in range(2)]
        wt = {n: c.sb(n, [P, D]) for n in ("wq", "wk", "wv", "wo")}
        bias_q, bias_k = c.sb("bias_q", [P, 1]), c.sb("bias_k", [P, 1])
        bias_qs = c.sb("bias_qs", [P, 1])
        bias_v, bias_o = c.sb("bias_v", [P, D]), c.sb("bias_o", [P, D])
        stats = c.sb("stats", [P, KB, 6])
        meanvar = c.sb("meanvar", [P, KB, 2])
        var_eps = c.sb("var_eps", [P, KB])
        rstd = c.sb("rstd", [P, KB])
        xn = c.sb("xn", [P, KB, D])
        xnT = [c.sb(f"xnT{i}", [P, SEQ]) for i in range(2)]
        xh, xl = c.sb("xh", [P, SEQ], F32R), c.sb("xl", [P, SEQ], F32R)
        wh, wl = ({n: c.sb(n + m, [P, D], F32R) for n in ("wq", "wk")} for m in "hl")
        qk32 = [c.sb(f"qk32_{i}", [P, SEQ]) for i in range(2)]
        rest = [c.sb(f"rest{i}", [P, SEQ]) for i in range(2)]
        qkp = [c.sb(f"qkp{i}", [P, 3, SEQ], BF16) for i in range(2)]
        vaug = [c.sb(f"vaug{i}", [P, KB, H, 32]) for i in range(2)]
        rowmax = c.sb("rowmax", [P, H, KB])
        max_rest = c.sb("max_rest", [P, 2, KB, HH])
        mparts = c.sb("mparts", [P, KB, 3, HH], BF16)
        mT = c.sb("mT", [3 * HH, SEQ], BF16)
        prob = [c.sb(f"prob{i}", [P, PW]) for i in range(NPB)]
        osb = [c.sb(f"osb{i}", [P, SEQ]) for i in range(2)]
        rsum = c.sb("rsum", [P, KB * 4])
        ctxn = c.sb("ctxn", [P, KB, H, HD])
        ctxT = c.sb("ctxT", [P, SEQ])

        row_ps = [c.bank(f"row{i}") for i in range(3)]
        col_ps = [c.bank(f"col{i}") for i in range(3)]
        out_ps = c.bank("out")
        work = c.bank("work")
        tables = RelativeTables(nc, c, relative, row_ps[0:2], prob) if relative else CausalTables(nc, c)

        names = ("w_loaded zeros_stored q_set k_set v_set bq_scaled ln_stats ln_mv ln_eps ln_rstd xn_ready part_q part_k rest_q rest_k "
                 "q_written k_written half0_loaded0 half1_loaded0 half0_loaded1 half1_loaded1 row_full row_read m_chain m_split m_stored m_loaded col_full exp_done "
                 " pv_done out_read work_full work_read r_ready bias_added w_high w_split xl_ready").split()
        s = {n: c.sem(n) for n in names}
        block = ctx.enter_context(nc.Block())

        SLOTS = [(1, "turn_ctx", 3, "old"), (2, "turn_out", 0, "old"), (3, "project", 0, "old"), (4, "turn_x", 0, "new2"),
                 (5, "turn_max", 1, "cur"), (6, "q", 0, "new2"), (7, "k", 0, "new2"), (8, "turn_ctx", 0, "cur"),
                 (9, "turn_ctx", 1, "cur"), (10, "v", 0, "new"), (11, "turn_max", 0, "new"), (13, "turn_ctx", 2, "cur")]

        def valid(b, which):
            n = {"old": b - 1, "cur": b, "new": b + 1, "new2": b + 2}[which]
            return 0 <= n < NB

        EARLY = 4

        def slot_in(b, u):
            return u[0] - EARLY * ((b < 0 and u[3] == "new2") or (b == NB - 1 and u[1:3] == ("turn_max", 1)))

        uses = {b: sorted((slot_in(b, u),) + u[1:] for u in SLOTS if valid(b, u[3])) for b in range(-2, NB + 1)}
        first_use, total = {}, 0
        for b in range(-2, NB + 1):
            first_use[b] = total
            total += len(uses[b])
        LOOP0, LOOPS = 1, 2

        def run(eng, step):
            for b in range(-2, LOOP0):
                step(b, b, first_use[b])
            with eng.Fori(0, LOOPS) as i:
                for r in range(2):
                    step(i * 2 + LOOP0 + r, LOOP0 + r, i * (2 * len(SLOTS)) + first_use[LOOP0 + r])
            for b in range(LOOP0 + 2 * LOOPS, NB + 1):
                step(b, b, first_use[b])

        def work_uses(kind_b, base, slot):
            for n, u in enumerate(uses[kind_b]):
                if u[0] == slot:
                    yield u, base + n

        def earlier(like, base, what, arg):
            before = uses[like - 1]
            at = [n for n, u in enumerate(before) if u[1:3] == (what, arg)][0]
            return base - len(before) + at

        def number_of(like, base, what, arg):
            return base + [n for n, u in enumerate(uses[like]) if u[1:3] == (what, arg)][0]

        def batch_of(b, which):
            return b + {"old": -1, "cur": 0, "new": 1, "new2": 2}[which]

        @block.sync
        def _(sp):
            tables.load(sp)
            for n in ("wq", "wk", "wv", "wo"):
                sp.dma_start(wt[n][:], w[n]).then_inc(s["w_loaded"], 16)
            sp.dma_start(bias_q[:], w["bq"].unsqueeze(1)).then_inc(s["w_loaded"], 16)
            sp.dma_start(bias_k[:], w["bk"].unsqueeze(1)).then_inc(s["w_loaded"], 16)
            sp.dma_start(bias_v[:], w["bv"].partition_broadcast(P)).then_inc(s["w_loaded"], 16)
            sp.dma_start(bias_o[:], w["bo"].partition_broadcast(P)).then_inc(s["w_loaded"], 16)

            def load_half(m, par, half):
                heads = slice(HH * half, HH * (half + 1))
                for which, (dst, runs) in enumerate(((qs[par], QRUNS), (ks[par], KRUNS))):
                    sp.wait_ge(s[f"{'qk'[which]}_written"], (m + 1) * 48)
                    t = 0
                    for first, stride, count in runs:
                        of = scratch[par, which, first:first + (count if stride else 1), :, heads, :]
                        if not stride:
                            of = of.broadcast_to([count, HD, HH, SEQ])
                        of = of.rearrange("t d h n -> t d (h n)")
                        sp.dma_start(dst[HD * t:HD * (t + count), heads, :], of).then_inc(s[f"half{half}_loaded{par}"], 16)
                        t += count

            def clear_max(par, half):
                sp.dma_start(qs[par][MROW:MROW + 3, HH * half:HH * (half + 1), :], zeros).then_inc(s[f"half{half}_loaded{par}"], 16)

            def load_max(number, par, half, stored):
                sp.wait_ge(s["work_read"], number + 1)
                sp.dma_start(maxima[half], mT[:]).then_inc(s["m_stored"], 16)
                sp.wait_ge(s["m_stored"], stored)
                sp.dma_start(qs[par][MROW:MROW + 3, HH * half:HH * (half + 1), :],
                             maxima[half].rearrange("(a h) q -> a h q", a=3)).then_inc(s["m_loaded"], 16)

            def step(b, like, base):
                par = like % 2
                if 0 <= like < NB:
                    load_max(number_of(like, base, "turn_max", 1), par, 1, b * 32 + 32)
                if 0 <= like + 2 < NB:
                    m = b + 2
                    for part in range(3):
                        for which in range(2):
                            sp.wait_ge(s[f"part_{'qk'[which]}"], m * 3 + part + 1)
                            sp.dma_start(scratch[par, which, part].rearrange("d h n -> h d n"),
                                         qkp[which][:, part]).then_inc(s[f"{'qk'[which]}_written"], 16)
                    if like < 0:
                        sp.wait_ge(s["q_set"], like + 3)
                        sp.wait_ge(s["k_set"], like + 3)
                    if like == -2:
                        sp.dma_start(zeros, qs[0][0:3, 0:HH, :]).then_inc(s["zeros_stored"], 16)
                        sp.wait_ge(s["zeros_stored"], 16)
                    if like >= 0:
                        sp.wait_ge(s["col_full"], b * (3 * H) + 3 * HH)
                    clear_max(par, 0)
                    load_half(m, par, 0)
                    if like == -2:
                        tables.store(sp)
                        tables.spread_rows(sp)
                if 0 <= like < NB - 1:
                    load_max(number_of(like, base, "turn_max", 0), 1 - par, 0, b * 32 + 48)
                if 0 <= like + 2 < NB:
                    if like >= 0:
                        sp.wait_ge(s["col_full"], b * (3 * H) + 3 * H)
                    clear_max(par, 1)
                    load_half(m, par, 1)
                if like == -2:
                    tables.spread_keys(sp)
                if like == -1:
                    load_max(number_of(like, base, "turn_max", 0), 1 - par, 0, 16)

            run(sp, step)
            sp.wait_ge(s["w_loaded"], 128)

        @block.gpsimd
        def _(pool):
            def step(b, like, base):
                if 0 <= like + 2 < NB:
                    m = b + 2
                    pool.wait_ge(s["ln_mv"], m + 1)
                    settle(pool, passed["pool"])
                    nc.gpsimd.tensor_scalar(var_eps[:], meanvar[:, :, 1], EPS, None, ALU.add).then_inc(s["ln_eps"], 1)
                    pool.wait_ge(s["ln_eps"], m + 1)
                    nc.gpsimd.tensor_tensor(rstd[:], var_eps[:], half_power[:], ALU.pow).then_inc(s["ln_rstd"], 1)
                    if like == -2:
                        pool.wait_ge(s["w_loaded"], 128)
                        nc.gpsimd.tensor_scalar(bias_qs[:], bias_q[:], scale, None, ALU.mult).then_inc(s["bq_scaled"], 1)
                        nc.gpsimd.memset(qs[0][:].bitcast(F32), 0.0).then_inc(s["q_set"], 1)
                    for part in range(2):
                        pool.wait_ge(s["part_q"], m * 3 + part + 1)
                        src, dst = ((qk32, rest), (rest, qk32))[part]
                        nc.gpsimd.tensor_tensor(dst[0][:], src[0][:], qkp[0][:, part], ALU.subtract).then_inc(s["rest_q"], 1)
                    if like == -2:
                        nc.gpsimd.memset(qs[1][:].bitcast(F32), 0.0).then_inc(s["q_set"], 1)
                        tables.zero_far(pool)
                    pool.wait_ge(s["xn_ready"], m + 1)
                    for k in range(KB):
                        ins = nc.gpsimd.tensor_tensor(resid[:, bass.ds(m * KB + k, 1), :].squeeze(1),
                                                      resid[:, bass.ds(m * KB + k, 1), :].squeeze(1),
                                                      bias_o[:], ALU.add)
                    ins.then_inc(s["bias_added"], 1)

            run(pool, step)

        @block.tensor
        def _(pe):
            pe.wait_ge(s["w_loaded"], 128)

            def rows(n, par, h):
                if h % HH == 0:
                    pe.wait_ge(s[f"half{h // HH}_loaded{par}"], (n - par) * (HALF_DMAS * 8) + HALF_DMAS * 16)
                for i, held in enumerate(ROWBANKS):
                    if not (isinstance(n, int) and n == 0 and h == 0):
                        pe.wait_ge(s["row_read"], n * (3 * H) + 3 * (h - 1) + i + 1)
                    for blk, col, width in held:
                        ins = nc.tensor.matmul(row_ps[i][:, col:col + width], qs[par][:, h, P * blk:P * (blk + 1)],
                                               ks[par][:, h, 0:width], start=True, stop=True)
                    ins.then_inc(s["row_full"], 1)

            def cols(b, par, h):
                if h % HH == 0:
                    pe.wait_ge(s["m_loaded"], b * 32 + (h // HH + 1) * 16)
                for i, held in enumerate(COLBANKS):
                    if not (isinstance(b, int) and b == 0 and h == 0):
                        pe.wait_ge(s["exp_done"], b * (3 * H) + 3 * (h - 1) + i + 1)
                    for n, (blk, col, width) in enumerate(held):
                        nc.tensor.matmul(col_ps[i][:, col:col + width], ks[par][:, h, P * blk:P * (blk + 1)],
                                         qs[par][:, h, P * blk:P * blk + width],
                                         start=(n == 0), stop=False, skip_group_check=True)
                    for blk, col, width in held:
                        for bias, wide in tables.key_parts(h, width):
                            ins = nc.tensor.matmul(col_ps[i][:, col:col + wide], identb[:], bias, start=False,
                                                   stop=True, skip_group_check=True)
                    ins.then_inc(s["col_full"], 1)

            def values(b, par, g):
                pe.wait_ge(s["exp_done"], b * (3 * H) + 12 * (g + 1))
                if not (isinstance(b, int) and b == 0 and g == 0):
                    pe.wait_ge(s["out_read"], b * NGRP + g)
                for j in (0, 1, 2, 3):
                    pcol, q0 = PCOL[j]
                    for t in range(4):
                        h = 4 * g + t
                        ins = nc.tensor.matmul(out_ps[32 * t:32 * (t + 1), q0:SEQ], vaug[par][:, j, h, :],
                                               prob[h % NPB][:, pcol:pcol + SEQ - q0],
                                               start=(j == 0), stop=(j == 3), skip_group_check=True)
                ins.then_inc(s["pv_done"], 1)

            def use(u, number, b, par):
                _, what, arg, which = u
                n = batch_of(b, which)
                npar = (par + {"old": 1, "cur": 0, "new": 1, "new2": 0}[which]) % 2
                if not (isinstance(number, int) and number == 0):
                    pe.wait_ge(s["work_read"], number)
                if what == "turn_x":
                    pe.wait_ge(s["xn_ready"], n + 1)
                    for k in range(KB):
                        ins = nc.tensor.transpose(work[:, P * k:P * (k + 1)], xn[:, k, :], ident[:])
                elif what in "qk":
                    if what == "q":
                        if isinstance(n, int) and n == 0:
                            pe.wait_ge(s["w_split"], 2)
                        pe.wait_ge(s["xl_ready"], n + 1)
                    for m, (left, right) in enumerate(((wh, xh), (wh, xl), (wl, xh))):
                        ins = nc.tensor.matmul(work[:], left["w" + what][:], right[:], start=(m == 0), stop=(m == 2))
                elif what == "v":
                    for k in range(KB):
                        ins = nc.tensor.matmul(work[:, P * k:P * (k + 1)], xnT[npar][:, P * k:P * (k + 1)], wt["wv"][:],
                                               start=True, stop=True)
                elif what == "turn_max":
                    pe.wait_ge(s["m_split"], 2 * n + arg + 1)
                    view = work[0:3 * HH, :].bitcast(BF16)
                    for k in range(KB):
                        ins = nc.tensor.transpose(view[:, P * k:P * (k + 1)],
                                                  mparts[:, k].rearrange("p a h -> p (a h)"), identb[:])
                elif what == "turn_ctx":
                    pe.wait_ge(s["out_read"], n * NGRP + arg + 1)
                    for k in range(KB):
                        ins = nc.tensor.transpose(work[:, P * k:P * (k + 1)], osb[arg % 2][:, P * k:P * (k + 1)], ident[:])
                elif what == "turn_out":
                    for k in range(KB):
                        ins = nc.tensor.transpose(work[:, P * k:P * (k + 1)],
                                                  ctxn[:, k].rearrange("p h d -> p (h d)"), ident[:])
                elif what == "project":
                    for k in range(KB):
                        ins = nc.tensor.matmul(work[:, P * k:P * (k + 1)], ctxT[:, P * k:P * (k + 1)], wt["wo"][:],
                                               start=True, stop=True)
                ins.then_inc(s["work_full"], 1)

            def step(b, like, base):
                par = like % 2
                if like == -1:
                    tables.banks_free(pe)
                if like == 0:
                    tables.keys_ready(pe)
                for h in range(H):
                    if 0 <= like < NB:
                        cols(b, par, h)
                    if 0 <= like + 1 < NB:
                        rows(b + 1, 1 - par, h)
                    if h == 0 and 0 <= like - 1 < NB:
                        values(b - 1, 1 - par, 3)
                    if h in (4, 8, 12) and 0 <= like < NB:
                        values(b, par, h // 4 - 1)
                    for u, number in work_uses(like, base, h):
                        use(u, number, b, par)
                    if like == -2 and h == 2:
                        tables.look_up(pe)

            run(pe, step)

        @block.scalar
        def _(act):
            act.wait_ge(s["w_loaded"], 128)
            for n in ("wq", "wk"):
                nc.scalar.copy(wh[n][:], wt[n][:]).then_inc(s["w_high"], 1)
            act.wait_ge(s["bq_scaled"], 1)

            def probabilities(b, h):
                if h >= NPB or not (isinstance(b, int) and b == 0):
                    if h % 4 == 0:
                        act.wait_ge(s["pv_done"], b * NGRP + h // 4 - 1)
                for i in range(3):
                    act.wait_ge(s["col_full"], b * (3 * H) + 3 * h + i + 1)
                    width = sum(x[2] for x in COLBANKS[i])
                    nc.scalar.activation(prob[h % NPB][:, SEQ * i:SEQ * i + width], col_ps[i][:, 0:width],
                                         ACT.Exp).then_inc(s["exp_done"], 1)

            def outputs(b, g):
                act.wait_ge(s["pv_done"], b * NGRP + g + 1)
                nc.scalar.copy(osb[g % 2][:], out_ps[:]).then_inc(s["out_read"], 1)

            def read(u, number, b, par):
                _, what, arg, which = u
                n = batch_of(b, which)
                npar = (par + {"old": 1, "cur": 0, "new": 1, "new2": 0}[which]) % 2
                if what not in ("turn_x", "q", "k", "turn_max", "turn_out"):
                    return
                act.wait_ge(s["work_full"], number + 1)
                if what == "turn_x":
                    nc.scalar.copy(xh[:], work[:])
                    ins = nc.scalar.copy(xnT[npar][:], work[:])
                elif what == "q":
                    ins = nc.scalar.activation(qk32[0][:], work[:], ACT.Identity, bias=bias_qs[:], scale=scale)
                elif what == "k":
                    ins = nc.scalar.activation(qk32[1][:], work[:], ACT.Identity, bias=bias_k[:])
                elif what == "turn_max":
                    if not (isinstance(n, int) and n == 0 and arg == 0):
                        act.wait_ge(s["m_stored"], n * 32 + 16 * arg)
                    ins = nc.scalar.copy(mT[:], work[0:3 * HH, :].bitcast(BF16)[:, 0:SEQ])
                else:
                    ins = nc.scalar.copy(ctxT[:], work[:])
                ins.then_inc(s["work_read"], 1)

            def round_part(b, like, base, h):
                for which, first in ((0, 6), (1, 7)):
                    part = h - first + EARLY * (like < 0)
                    if not 0 <= part < 3:
                        continue
                    m = b + 2
                    if part == 0:
                        act.wait_ge(s["work_read"], number_of(like, base, "qk"[which], 0) + 1)
                        if not (isinstance(m, int) and m == 0):
                            act.wait_ge(s[f"{'qk'[which]}_written"], m * 48)
                    else:
                        act.wait_ge(s[f"rest_{'qk'[which]}"], m * 2 + part)
                    src = (qk32[which], rest[which], qk32[which])[part]
                    nc.scalar.copy(qkp[which][:, part], src[:]).then_inc(s[f"part_{'qk'[which]}"], 1)

            def step(b, like, base):
                par = like % 2
                for h in range(H):
                    if 0 <= like < NB:
                        probabilities(b, h)
                    if h == 0 and 0 <= like - 1 < NB:
                        outputs(b - 1, 3)
                    if h in (4, 8, 12) and 0 <= like < NB:
                        outputs(b, h // 4 - 1)
                    for u, number in work_uses(like, base, h):
                        read(u, number, b, par)
                    if 0 <= like + 2 < NB:
                        round_part(b, like, base, h)

            run(act, step)

        @block.vector
        def _(dve):
            def norm_stats(m):
                for k in range(KB):
                    ins = nc.vector.bn_stats(stats[:, k, :], resid[:, bass.ds(m * KB + k, 1), :].squeeze(1))
                ins.then_inc(s["ln_stats"], 1)
                dve.wait_ge(s["ln_stats"], m + 1)
                if not (isinstance(m, int) and m == 0):
                    dve.wait_ge(s["ln_rstd"], m)
                settle(dve, passed["dve"])
                for k in range(KB):
                    ins = nc.vector.bn_aggr(meanvar[:, k, :], stats[:, k, :])
                ins.then_inc(s["ln_mv"], 1)

            def norm(m):
                dve.wait_ge(s["ln_rstd"], m + 1)
                dve.wait_ge(s["ln_mv"], m + 1)
                for k in range(KB):
                    ins = nc.vector.tensor_scalar(xn[:, k, :], resid[:, bass.ds(m * KB + k, 1), :].squeeze(1),
                                                  meanvar[:, k, 0:1], rstd[:, k:k + 1], ALU.subtract, ALU.mult)
                ins.then_inc(s["xn_ready"], 1)

            def maxima(n, h):
                for i, held in enumerate(ROWBANKS):
                    dve.wait_ge(s["row_full"], n * (3 * H) + 3 * h + i + 1)
                    settle(dve, passed["dve"])
                    for blk, col, width in held:
                        bias = tables.row_bias(h, width)
                        ins = nc.vector.tensor_tensor_reduce(row_ps[i][:, col:col + width], row_ps[i][:, col:col + width], bias, 1.0,
                                                             MASK, ALU.add, ALU.max, rowmax[:, h, blk:blk + 1])
                    ins.then_inc(s["row_read"], 1)

            def split_max(n, half, turned):
                src = rowmax[:, HH * half:HH * (half + 1), :].rearrange("p h k -> p k h")
                dve.wait_ge(s["row_read"], n * (3 * H) + 3 * HH * (half + 1))
                at = n * 8 + 4 * half
                if turned is not None:
                    dve.wait_ge(s["work_read"], turned + 1)
                nc.vector.tensor_scalar(mparts[:, :, 0, :], src, -1.0, None, ALU.mult).then_inc(s["m_chain"], 1)
                dve.wait_ge(s["m_chain"], at + 1)
                nc.vector.scalar_tensor_tensor(max_rest[:, 0], src, -1.0, mparts[:, :, 0, :], ALU.mult,
                                               ALU.subtract).then_inc(s["m_chain"], 1)
                dve.wait_ge(s["m_chain"], at + 2)
                nc.vector.tensor_copy(mparts[:, :, 1, :], max_rest[:, 0]).then_inc(s["m_chain"], 1)
                dve.wait_ge(s["m_chain"], at + 3)
                nc.vector.tensor_tensor(max_rest[:, 1], max_rest[:, 0], mparts[:, :, 1, :], ALU.subtract).then_inc(s["m_chain"], 1)
                dve.wait_ge(s["m_chain"], at + 4)
                nc.vector.tensor_copy(mparts[:, :, 2, :], max_rest[:, 1]).then_inc(s["m_split"], 1)

            def read(u, number, b, par):
                _, what, arg, which = u
                n = batch_of(b, which)
                npar = (par + {"old": 1, "cur": 0, "new": 1, "new2": 0}[which]) % 2
                if what == "turn_ctx":
                    dve.wait_ge(s["work_full"], number + 1)
                    turned = work[:].rearrange("p (x c) -> p x c", c=32)
                    count = n * NGRP + arg
                    nc.vector.reciprocal(rsum[:], turned[:, :, HD]).then_inc(s["r_ready"], 1)
                    dve.wait_ge(s["r_ready"], count + 1)
                    inv = rsum[:].rearrange("p (k t) -> p k t", t=4)
                    ins = nc.vector.tensor_tensor(ctxn[:, :, 4 * arg:4 * arg + 4, :],
                                                  turned.rearrange("p (k t) c -> p k t c", t=4)[:, :, :, 0:HD],
                                                  inv.unsqueeze(3).broadcast_to([P, KB, 4, HD]), ALU.mult)
                    ins.then_inc(s["work_read"], 1)
                elif what == "turn_x":
                    dve.wait_ge(s["work_read"], number + 1)
                    nc.vector.tensor_tensor(xl[:], xnT[npar][:], xh[:].bitcast(F32), ALU.subtract).then_inc(s["xl_ready"], 1)
                elif what == "v":
                    dve.wait_ge(s["work_full"], number + 1)
                    bias = bias_v[:].rearrange("p (h d) -> p h d", d=HD).unsqueeze(1).broadcast_to([P, KB, H, HD])
                    ins = nc.vector.tensor_tensor(vaug[npar][:, :, :, 0:HD],
                                                  work[:].rearrange("p (k h d) -> p k h d", h=H, d=HD), bias, ALU.add)
                    ins.then_inc(s["work_read"], 1)
                elif what == "project":
                    dve.wait_ge(s["work_full"], number + 1)
                    dve.wait_ge(s["bias_added"], n + 1)
                    rows = resid[:, bass.ds(n * KB, KB), :]
                    ins = nc.vector.tensor_tensor(rows, work[:].rearrange("p (k d) -> p k d", d=D), rows, ALU.add)
                    ins.then_inc(s["work_read"], 1)

            def rest_of_k(m, part):
                if 0 <= part < 2:
                    dve.wait_ge(s["part_k"], m * 3 + part + 1)
                    src, dst = ((qk32, rest), (rest, qk32))[part]
                    nc.vector.tensor_tensor(dst[1][:], src[1][:], qkp[1][:, part], ALU.subtract).then_inc(s["rest_k"], 1)

            def prepare():
                tables.make_vectors(dve)
                for v in vaug:
                    nc.vector.memset(v[:, :, :, HD:32], 0.0).then_inc(s["v_set"], 1)
                dve.wait_ge(s["v_set"], 2)
                for v in vaug:
                    nc.vector.memset(v[:, :, :, HD:HD + 1], 1.0).then_inc(s["v_set"], 1)
                nc.vector.memset(ks[1][:].bitcast(F32), TWO_ONES).then_inc(s["k_set"], 1)

            def step(b, like, base):
                par = like % 2
                if like < 0:
                    if loaded:
                        dve.wait_ge(loaded[like + 2], 16)
                    norm_stats(b + 2)
                    norm(b + 2)
                if like == -2:
                    dve.wait_ge(s["w_high"], 2)
                    for n in ("wq", "wk"):
                        nc.vector.tensor_tensor(wl[n][:], wt[n][:], wh[n][:].bitcast(F32), ALU.subtract).then_inc(s["w_split"], 1)
                if like == NB - 1:
                    split_max(b, 1, earlier(like, base, "turn_max", 0))
                for h in range(H):
                    if like == -1 and h == 0:
                        tables.rows_ready(dve)
                    if 0 <= like + 1 < NB:
                        maxima(b + 1, h)
                    for u, number in work_uses(like, base, h):
                        read(u, number, b, par)
                    if h == 3 and 0 <= like < NB - 1:
                        split_max(b, 1, earlier(like, base, "turn_max", 0))
                    if h == 9 and 0 <= like + 1 < NB:
                        split_max(b + 1, 0, number_of(like, base, "turn_max", 1) if like >= 0 else None)
                    if h == 1 and 0 <= like and like + 2 < NB:
                        norm_stats(b + 2)
                    if h == 2 and 0 <= like and like + 2 < NB:
                        norm(b + 2)
                    if 0 <= like + 2 < NB:
                        rest_of_k(b + 2, h - 7 + EARLY * (like < 0))
                    if like == -2 and h == 0:
                        nc.vector.memset(ks[0][:].bitcast(F32), TWO_ONES).then_inc(s["k_set"], 1)
                if like == -2:
                    prepare()

            run(dve, step)


def ffn(nc, name, resid, ident, identb, half_power, passed, w, out=None):
    with ExitStack() as ctx:
        c = Core(nc, ctx, name, clear=out is None)
        xh, xl = c.sb("xh", [P, NBLK * P], F32R), c.sb("xl", [P, NBLK * P], F32R)
        acc = c.sb("acc", [P, NBLK * P])
        combT = c.sb("combT", [P, NBLK * P], BF16)
        pick = c.sb("pick", [P, E, P], BF16)
        b1, b2 = c.sb("b1", [P, NE, HC]), c.sb("b2", [P, NE])
        gate_w, gate_b = c.sb("gate_w", [P, E]), c.sb("gate_b", [P, E])
        stats = c.sb("stats", [P, 2, KB, 6])
        meanvar = c.sb("meanvar", [P, 2, KB, 2])
        var_eps = c.sb("var_eps", [P, 2, KB])
        rstd = c.sb("rstd", [P, 2, KB])
        xn = [c.sb(f"xn{i}", [P, KB, D]) for i in range(2)]
        xnT = [c.sb(f"xnT{i}", [P, SEQ]) for i in range(2)]
        logit = c.sb("logit", [P, NBLK, E])
        tri = c.sb("tri", [P, E, E])
        want = c.sb("want", [P, E + 1])
        beats = c.sb("beats", [P, NBLK, E, E])
        less = c.sb("less", [P, KB, E, E])
        margin = c.sb("margin", [P, NBLK, E])
        top2 = c.sb("top2", [P, 2, NBLK, E])
        prod = c.sb("prod", [P, 2, NBLK, E])
        top = c.sb("top", [P, 2, NBLK])
        gap, ratio, wsum = (c.sb(n, [P, NBLK]) for n in ("gap", "ratio", "wsum"))
        share = c.sb("share", [P, 2, NBLK])
        comb, crest, crest2 = (c.sb(n, [P, NBLK, E]) for n in ("comb", "crest", "crest2"))
        cparts = c.sb("cparts", [P, NBLK, 3, E], BF16)
        w1 = [c.sb(f"w1_{i}", [P, HID]) for i in range(2)]
        w2 = [c.sb(f"w2_{i}", [P, HC, D]) for i in range(2)]
        w1h, w1l = ([c.sb(f"{n}{i}", [P, HID], F32R) for i in range(2)] for n in ("w1h", "w1l"))
        w2h, w2l = ([c.sb(f"{n}{i}", [P, HC, D], F32R) for i in range(2)] for n in ("w2h", "w2l"))
        hid = [c.sb(f"hid{i}", [P, SEQ]) for i in range(HC)]
        hh, hl = ([c.sb(f"{n}{i}", [P, HC, SEQ], F32R) for i in range(2)] for n in ("hh", "hl"))
        weight = [c.sb(f"weight{i}", [P, SEQ]) for i in range(2)]
        scaled = [c.sb(f"scaled{i}", [P, SEQ]) for i in range(2)]
        hid_ps = [c.bank(f"hid{i}") for i in range(HC)]
        out_ps = [c.bank(f"out{i}") for i in range(2)]
        weight_ps, turn_ps = c.bank("weight"), c.bank("turn")
        logit_ps = weight_ps[:, 0:KB * E]
        names = ("gate_loaded w0_loaded w1_loaded w_high w_split zeroed made ln_stats ln_mv ln_eps "
                 "ln_rstd xn_ready turned xnT_ready xh_ready xl_ready logit_full logit_read rank_chain ranked top_chain "
                 "compared gap_ready ratio_ready parts_ready comb_read hid_full gelu_done h_high h_split out_full weight_full "
                 "weight_read combined added resid_added").split() + (["out_stored"] if out is not None else [])
        s = {n: c.sem(n) for n in names}
        block = ctx.enter_context(nc.Block())
        LAST = NE - 1
        LAG = 3

        def run(eng, turn):
            for e in (0, 1):
                for b in range(NB):
                    turn(e, e, b)
            with eng.Fori(0, (NE - 3) // 2) as i:
                for r in range(2):
                    for b in range(NB):
                        turn(i * 2 + 2 + r, 2 + r, b)
            for b in range(NB):
                turn(LAST, LAST, b)

        def tokens(b):
            return slice(SEQ * b, SEQ * (b + 1))

        RATIOS = [(0, NB - 1), (1, 0)]

        def halves(j):
            return slice(NBLK // 2 * j, NBLK // 2 * (j + 1))

        def blocks(b):
            return slice(KB * b, KB * (b + 1))

        @block.sync
        def _(sp):
            def load(e, like):
                par = like % 2
                if like >= 2:
                    sp.wait_ge(s["w_split"], 2 * e - 2)
                sp.dma_start(w1[par][:], w["w1"][bass.ds(e, 1)].squeeze(0)).then_inc(s[f"w{par}_loaded"], 16)
                sp.dma_start(w2[par][:], w["w2"][bass.ds(e, 1)].squeeze(0)).then_inc(s[f"w{par}_loaded"], 16)

            load(0, 0)
            sp.dma_start(gate_w[:], w["gate_w"]).then_inc(s["gate_loaded"], 16)
            sp.dma_start(gate_b[:], w["gate_b"].partition_broadcast(P)).then_inc(s["gate_loaded"], 16)
            sp.dma_start(b1[:], w["b1"]).then_inc(s["gate_loaded"], 16)
            sp.dma_start(b2[:], w["b2"]).then_inc(s["gate_loaded"], 16)
            load(1, 1)
            with sp.Fori(0, (NE - 3) // 2) as i:
                load(i * 2 + 2, 2)
                load(i * 2 + 3, 3)
            load(LAST, LAST)
            if out is not None:
                rows = out.rearrange("b (k p) d -> p (b k) d", p=P)
                for b in range(NB):
                    sp.wait_ge(s["resid_added"], b + 1)
                    sp.dma_start(rows[:, blocks(b), :], resid[:, blocks(b), :]).then_inc(s["out_stored"], 16)
                sp.wait_ge(s["out_stored"], 16 * NB)
            sp.wait_ge(s["w0_loaded"], 16 * (NE + 1))

        @block.gpsimd
        def _(pool):
            def rstds(b):
                pool.wait_ge(s["ln_mv"], b + 1)
                nc.gpsimd.tensor_scalar(var_eps[:, b % 2], meanvar[:, b % 2, :, 1], EPS, None, ALU.add).then_inc(s["ln_eps"], 1)
                pool.wait_ge(s["ln_eps"], b + 1)
                nc.gpsimd.tensor_tensor(rstd[:, b % 2], var_eps[:, b % 2], half_power[:], ALU.pow).then_inc(s["ln_rstd"], 1)

            def low_part(b):
                pool.wait_ge(s["xh_ready"], b + 1)
                nc.gpsimd.tensor_tensor(xl[:, tokens(b)], xnT[b % 2][:], xh[:, tokens(b)].bitcast(F32),
                                        ALU.subtract).then_inc(s["xl_ready"], 1)

            def rank(b):
                count = 4 * b

                def link(ins):
                    nonlocal count
                    count += 1
                    ins.then_inc(s["rank_chain"], 1)
                    pool.wait_ge(s["rank_chain"], count)

                pool.wait_ge(s["compared"], b + 1)
                ge = beats[:, blocks(b)]
                link(nc.gpsimd.tensor_tensor(ge, ge, tri[:].unsqueeze(1).broadcast_to([P, KB, E, E]), ALU.mult))
                link(nc.gpsimd.tensor_tensor(less[:], ge, ge.rearrange("p k e f -> p k f e"), ALU.subtract))
                for n in (4, 2):
                    link(nc.gpsimd.tensor_tensor(less[:, :, :, 0:n], less[:, :, :, 0:n], less[:, :, :, n:2 * n], ALU.add))
                nc.gpsimd.tensor_tensor(margin[:, blocks(b), :], less[:, :, :, 0], less[:, :, :, 1], ALU.add).then_inc(s["ranked"], 1)
                pool.wait_ge(s["ranked"], b + 1)

            def rank_constants():
                nc.gpsimd.memset(tri[:], 1.0).then_inc(s["zeroed"], 1)
                for n in range(E + 1):
                    nc.gpsimd.memset(want[:, n:n + 1], float(n + 1 - E))
                pool.wait_ge(s["zeroed"], 1)
                nc.gpsimd.affine_select(out=tri[:], in_=tri[:], compare_op=ALU.is_gt, fill=0.0, base=0,
                                        pattern=[[1, E], [-1, E]], channel_multiplier=0).then_inc(s["made"], 1)
                pool.wait_ge(s["made"], 1)

            def broadcast_constants():
                nc.gpsimd.memset(pick[:].bitcast(F32), 0.0).then_inc(s["zeroed"], 1)
                nc.gpsimd.memset(combT[:].bitcast(F32), 0.0).then_inc(s["zeroed"], 1)
                pool.wait_ge(s["zeroed"], 3)
                for part in range(3):
                    pool.wait_ge(s["made"], part + 1)
                    nc.gpsimd.affine_select(out=pick[:], in_=pick[:], compare_op=ALU.not_equal, fill=1.0, base=-E * part,
                                            pattern=[[-1, E], [0, P]], channel_multiplier=1).then_inc(s["made"], 1)

            def high(e, like):
                par = like % 2
                pool.wait_ge(s[f"w{par}_loaded"], (e - par) * 16 + 32)
                if like >= 2:
                    pool.wait_ge(s["out_full"], e * NB - NB)
                settle(pool, passed["pool"])
                nc.gpsimd.tensor_copy(w1h[par][:], w1[par][:])
                nc.gpsimd.tensor_copy(w2h[par][:], w2[par][:]).then_inc(s["w_high"], 1)

            def low(e, like):
                par = like % 2
                pool.wait_ge(s["w_high"], e + 2)
                nc.gpsimd.tensor_tensor(w1l[par][:], w1[par][:], w1h[par][:].bitcast(F32), ALU.subtract).then_inc(s["w_split"], 1)
                nc.gpsimd.tensor_tensor(w2l[par][:], w2[par][:], w2h[par][:].bitcast(F32), ALU.subtract).then_inc(s["w_split"], 1)

            def turn(e, like, b):
                if like == 0:
                    if b + 4 < NB:
                        rstds(b + 4)
                    if b + 2 < NB:
                        low_part(b + 2)
                if b == 1 and like + 1 < NE:
                    high(e + 1, like + 1)
                    low(e + 1, like + 1)
                if like == 0:
                    if 3 <= b < 7:
                        rank(2 * b - 6)
                        rank(2 * b - 5)
                else:
                    pool.wait_ge(s["combined"], e * NB + b + 1)
                    nc.gpsimd.tensor_tensor(acc[:, tokens(b)], acc[:, tokens(b)], scaled[b % 2][:], ALU.add).then_inc(s["added"], 1)

            rank_constants()
            rstds(0)
            rstds(1)
            low_part(0)
            rstds(2)
            low_part(1)
            rstds(3)
            broadcast_constants()
            run(pool, turn)

        @block.tensor
        def _(pe):
            def turn_x(b):
                pe.wait_ge(s["xn_ready"], b + 1)
                if b > 0:
                    pe.wait_ge(s["xh_ready"], b)
                for k in range(KB):
                    ins = nc.tensor.transpose(turn_ps[:, P * k:P * (k + 1)], xn[b % 2][:, k, :], ident[:])
                ins.then_inc(s["turned"], 1)

            def gate(b):
                pe.wait_ge(s["xnT_ready"], b + 1)
                if b > 0:
                    pe.wait_ge(s["logit_read"], b)
                for k in range(KB):
                    ins = nc.tensor.matmul(logit_ps[:, E * k:E * (k + 1)], xnT[b % 2][:, P * k:P * (k + 1)], gate_w[:],
                                           start=True, stop=True)
                ins.then_inc(s["logit_full"], 1)

            def turn_comb(n):
                pe.wait_ge(s["parts_ready"], n // 2 + 1)
                if n > 0:
                    pe.wait_ge(s["comb_read"], n)
                for k in range(8):
                    ins = nc.tensor.transpose(turn_ps[0:3 * E, P // 2 * k:P // 2 * (k + 1)].bitcast(BF16),
                                              cparts[:, 8 * n + k].rearrange("p a e -> p (a e)"), identb[:])
                ins.then_inc(s["turned"], 1)

            def hidden(e, like, b):
                par, t = like % 2, e * NB + b
                if b == 0:
                    pe.wait_ge(s["w_split"], 2 * e + 1)
                if like == 0:
                    pe.wait_ge(s["xl_ready"], b + 1)
                for k in range(HC):
                    if not (like == 0 and b == 0):
                        pe.wait_ge(s["gelu_done"], t * HC - HC + k + 1)
                    cols = slice(P * k, P * (k + 1))
                    nc.tensor.matmul(hid_ps[k][:], w1h[par][:, cols], xh[:, tokens(b)], start=True, stop=False)
                    nc.tensor.matmul(hid_ps[k][:], w1h[par][:, cols], xl[:, tokens(b)], start=False, stop=False)
                    nc.tensor.matmul(hid_ps[k][:], w1l[par][:, cols], xh[:, tokens(b)], start=False,
                                     stop=True).then_inc(s["hid_full"], 1)

            def output(e, like, b):
                par, t = like % 2, e * NB + b
                if like > 0:
                    if like == 1 and b % 2 == 0:
                        pe.wait_ge(s["comb_read"], b // 2 + 1)
                    if not (like == 1 and b == 0):
                        pe.wait_ge(s["weight_read"], t - NB)
                    nc.tensor.matmul(weight_ps[:], pick[:, bass.ds(e - 1, 1), :].squeeze(1), combT[:, tokens(b)],
                                     start=True, stop=True).then_inc(s["weight_full"], 1)
                if b == 0:
                    pe.wait_ge(s["w_split"], 2 * e + 2)
                if not (like == 0 and b < 2):
                    pe.wait_ge(s["combined"], t - 1)
                for k in range(HC):
                    pe.wait_ge(s["h_split"], t * HC + k + 1)
                    nc.tensor.matmul(out_ps[b % 2][:], w2h[par][:, k, :], hh[b % 2][:, k, :], start=(k == 0), stop=False)
                    nc.tensor.matmul(out_ps[b % 2][:], w2h[par][:, k, :], hl[b % 2][:, k, :], start=False, stop=False)
                    ins = nc.tensor.matmul(out_ps[b % 2][:], w2l[par][:, k, :], hh[b % 2][:, k, :], start=False,
                                           stop=(k == HC - 1))
                ins.then_inc(s["out_full"], 1)

            def turn_back(b):
                pe.wait_ge(s["added"], (LAST - 1) * NB + b + 1)
                if b > 0:
                    pe.wait_ge(s["resid_added"], b)
                for k in range(KB):
                    n = b * KB + k
                    ins = nc.tensor.transpose(turn_ps[:, P * k:P * (k + 1)], acc[:, P * n:P * (n + 1)], ident[:])
                ins.then_inc(s["turned"], 1)

            def turn(e, like, b):
                hidden(e, like, b)
                if b > 0:
                    output(e, like, b - 1)
                elif like > 0:
                    output(e - 1, like - 1, NB - 1)
                if like == 0 and b + 2 < NB:
                    turn_x(b + 2)
                if like == 0 and b + 1 < NB:
                    gate(b + 1)
                if like == 1 and b < NBLK // 8:
                    turn_comb(b)
                if like == LAST and b >= LAG:
                    turn_back(b - LAG)

            turn_x(0)
            pe.wait_ge(s["gate_loaded"], 64)
            gate(0)
            turn_x(1)
            run(pe, turn)
            output(LAST, LAST, NB - 1)
            for b in range(NB - LAG, NB):
                turn_back(b)

        @block.scalar
        def _(act):
            def bring(b):
                act.wait_ge(s["turned"], b + 1)
                if b >= 2:
                    act.wait_ge(s["logit_full"], b - 1)
                    act.wait_ge(s["xl_ready"], b - 1)
                nc.scalar.copy(xnT[b % 2][:], turn_ps[:]).then_inc(s["xnT_ready"], 1)
                nc.scalar.copy(xh[:, tokens(b)], turn_ps[:]).then_inc(s["xh_ready"], 1)

            def broadcast(e, like, b):
                if like == 0:
                    return
                t = e * NB + b
                act.wait_ge(s["weight_full"], t - NB + 1)
                if not (like == 1 and b < 2):
                    act.wait_ge(s["combined"], t - 1)
                nc.scalar.copy(weight[b % 2][:], weight_ps[:]).then_inc(s["weight_read"], 1)

            def rounded(like, b, t, k):
                if k == 0 and not (like == 0 and b < 2):
                    act.wait_ge(s["out_full"], t - 1)
                act.wait_ge(s["gelu_done"], t * HC + k + 1)
                nc.scalar.copy(hh[b % 2][:, k, :], hid[k][:]).then_inc(s["h_high"], 1)

            def turn(e, like, b):
                t = e * NB + b
                for k in range(HC):
                    if (like, b) in RATIOS and k == 2:
                        half = RATIOS.index((like, b))
                        act.wait_ge(s["gap_ready"], half + 1)
                        nc.scalar.activation(ratio[:, halves(half)], gap[:, halves(half)], ACT.Exp).then_inc(s["ratio_ready"], 1)
                    act.wait_ge(s["hid_full"], t * HC + k + 1)
                    if not (like == 0 and b == 0):
                        act.wait_ge(s["h_split"], t * HC - HC + k + 1)
                    nc.scalar.activation(hid[k][:], hid_ps[k][:], ACT.Gelu,
                                         bias=b1[:, bass.ds(e, 1), k:k + 1].squeeze(1)).then_inc(s["gelu_done"], 1)
                    if k > 0:
                        rounded(like, b, t, k - 1)
                rounded(like, b, t, HC - 1)
                if b > 0:
                    broadcast(e, like, b - 1)
                elif like > 0:
                    broadcast(e - 1, like - 1, NB - 1)
                if like == 0 and b + 2 < NB:
                    bring(b + 2)
                if like == 1 and b < NBLK // 8:
                    act.wait_ge(s["zeroed"], 3)
                    act.wait_ge(s["turned"], NB + b + 1)
                    nc.scalar.copy(combT[0:3 * E, 8 * P * b:8 * P * (b + 1)],
                                   turn_ps[0:3 * E, :].bitcast(BF16)).then_inc(s["comb_read"], 1)

            act.wait_ge(s["w0_loaded"], 32)
            nc.scalar.copy(w1h[0][:], w1[0][:]).then_inc(s["w_high"], 1)
            nc.scalar.copy(w2h[0][:], w2[0][:]).then_inc(s["w_high"], 1)
            bring(0)
            bring(1)
            act.wait_ge(s["gate_loaded"], 64)
            run(act, turn)
            broadcast(LAST, LAST, NB - 1)

        @block.vector
        def _(dve):
            def norm_stats(b):
                for k in range(KB):
                    ins = nc.vector.bn_stats(stats[:, b % 2, k, :], resid[:, KB * b + k, :])
                ins.then_inc(s["ln_stats"], 1)
                dve.wait_ge(s["ln_stats"], b + 1)
                for k in range(KB):
                    ins = nc.vector.bn_aggr(meanvar[:, b % 2, k, :], stats[:, b % 2, k, :])
                ins.then_inc(s["ln_mv"], 1)

            def norm(b):
                dve.wait_ge(s["ln_rstd"], b + 1)
                if b >= 2:
                    dve.wait_ge(s["turned"], b - 1)
                for k in range(KB):
                    ins = nc.vector.tensor_scalar(xn[b % 2][:, k, :], resid[:, KB * b + k, :], meanvar[:, b % 2, k, 0:1],
                                                  rstd[:, b % 2, k:k + 1], ALU.subtract, ALU.mult)
                ins.then_inc(s["xn_ready"], 1)
                dve.wait_ge(s["xn_ready"], b + 1)

            def logits(b):
                dve.wait_ge(s["logit_full"], b + 1)
                nc.vector.tensor_tensor(logit[:, blocks(b), :], logit_ps.rearrange("p (k e) -> p k e", e=E),
                                        gate_b[:].unsqueeze(1).broadcast_to([P, KB, E]), ALU.add).then_inc(s["logit_read"], 1)
                dve.wait_ge(s["logit_read"], b + 1)
                mine = logit[:, blocks(b), :]
                nc.vector.tensor_tensor(beats[:, blocks(b)], mine.unsqueeze(2).broadcast_to([P, KB, E, E]),
                                        mine.unsqueeze(3).broadcast_to([P, KB, E, E]), ALU.is_ge).then_inc(s["compared"], 1)

            chained = [0]

            def link(ins):
                chained[0] += 1
                ins.then_inc(s["top_chain"], 1)
                dve.wait_ge(s["top_chain"], chained[0])

            HB = NBLK // 2

            def top_gap(half):
                at = halves(half)
                dve.wait_ge(s["ranked"], NB // 2 * (half + 1))
                for r in range(2):
                    ins = nc.vector.tensor_tensor(top2[:, r, at], margin[:, at], want[:, r:r + E].unsqueeze(1).broadcast_to([P, HB, E]),
                                                  ALU.is_equal)
                link(ins)
                link(nc.vector.tensor_tensor(prod[:, :, at], top2[:, :, at],
                                             logit[:, at].unsqueeze(1).broadcast_to([P, 2, HB, E]), ALU.mult))
                link(nc.vector.tensor_reduce(top[:, :, at], prod[:, :, at], AX.X, ALU.add))
                nc.vector.tensor_tensor(gap[:, at], top[:, 1, at], top[:, 0, at], ALU.subtract).then_inc(s["gap_ready"], 1)

            def shares(half):
                at = halves(half)
                dve.wait_ge(s["ratio_ready"], half + 1)
                link(nc.vector.tensor_scalar(wsum[:, at], ratio[:, at], 1.0, None, ALU.add))
                link(nc.vector.reciprocal(share[:, 0, at], wsum[:, at]))
                link(nc.vector.tensor_tensor(share[:, 1, at], ratio[:, at], share[:, 0, at], ALU.mult))
                link(nc.vector.tensor_tensor(prod[:, :, at], top2[:, :, at],
                                             share[:, :, at].unsqueeze(3).broadcast_to([P, 2, HB, E]), ALU.mult))
                link(nc.vector.tensor_tensor(comb[:, at], prod[:, 0, at], prod[:, 1, at], ALU.add))
                link(nc.vector.tensor_copy(cparts[:, at, 0, :], comb[:, at]))
                link(nc.vector.tensor_tensor(crest[:, at], comb[:, at], cparts[:, at, 0, :], ALU.subtract))
                link(nc.vector.tensor_copy(cparts[:, at, 1, :], crest[:, at]))
                link(nc.vector.tensor_tensor(crest2[:, at], crest[:, at], cparts[:, at, 1, :], ALU.subtract))
                nc.vector.tensor_copy(cparts[:, at, 2, :], crest2[:, at]).then_inc(s["parts_ready"], 1)

            def combine(e, like, b):
                t = e * NB + b
                bias = b2[:, bass.ds(e, 1)]
                dve.wait_ge(s["out_full"], t + 1)
                if like == 0:
                    nc.vector.tensor_scalar(acc[:, tokens(b)], out_ps[b % 2][:], bias, None, ALU.add).then_inc(s["combined"], 1)
                    return
                dve.wait_ge(s["weight_read"], t - NB + 1)
                if not (like == 1 and b < 2):
                    dve.wait_ge(s["added"], t - NB - 1)
                nc.vector.scalar_tensor_tensor(scaled[b % 2][:], out_ps[b % 2][:], bias, weight[b % 2][:], ALU.add,
                                               ALU.mult).then_inc(s["combined"], 1)

            def add_back(b):
                dve.wait_ge(s["turned"], NB + NBLK // 8 + b + 1)
                rows = resid[:, blocks(b), :].rearrange("p k d -> p (k d)")
                nc.vector.tensor_tensor(rows, turn_ps[:], rows, ALU.add).then_inc(s["resid_added"], 1)

            def turn(e, like, b):
                t = e * NB + b
                for k in range(HC):
                    dve.wait_ge(s["h_high"], t * HC + k + 1)
                    nc.vector.tensor_tensor(hl[b % 2][:, k, :], hid[k][:], hh[b % 2][:, k, :].bitcast(F32),
                                            ALU.subtract).then_inc(s["h_split"], 1)
                if (like, b) in RATIOS:
                    shares(RATIOS.index((like, b)))
                if b > 0:
                    combine(e, like, b - 1)
                elif like > 0:
                    combine(e - 1, like - 1, NB - 1)
                if like == 0:
                    if b + 1 < NB:
                        logits(b + 1)
                    if b + 4 < NB:
                        norm_stats(b + 4)
                    if b + 3 < NB:
                        norm(b + 3)
                if like == 0 and b >= NB - 2:
                    top_gap(b - NB + 2)
                if like == LAST and b >= LAG:
                    add_back(b - LAG)

            norm_stats(0)
            norm_stats(1)
            norm(0)
            norm_stats(2)
            for n, (whole, part, left) in enumerate(((w1, w1h, w1l), (w2, w2h, w2l))):
                dve.wait_ge(s["w_high"], n + 1)
                nc.vector.tensor_tensor(left[0][:], whole[0][:], part[0][:].bitcast(F32), ALU.subtract).then_inc(s["w_split"], 1)
            norm(1)
            norm_stats(3)
            dve.wait_ge(s["gate_loaded"], 64)
            logits(0)
            norm(2)
            run(dve, turn)
            combine(LAST, LAST, NB - 1)
            for b in range(NB - LAG, NB):
                add_back(b)


def hybrid(nc, x, a, m, f, rel_emb, onehot, out):
    nc.disable_value_cache = True
    with ExitStack() as ctx:
        resid = ctx.enter_context(nc.sbuf_tensor("resid", [P, NBLK, D], F32))
        ident = ctx.enter_context(nc.sbuf_tensor("ident", [P, P], F32))
        identb = ctx.enter_context(nc.sbuf_tensor("identb", [P, P], BF16))
        half_power = ctx.enter_context(nc.sbuf_tensor("half_power", [P, KB], F32))
        zeros = nc.dram_tensor("zeros", (3, HH, SEQ), BF16, kind="Internal").ap()
        scratch = nc.dram_tensor("qk_parts", (2, 2, 3, HD, H, SEQ), BF16, kind="Internal").ap()
        maxima = nc.dram_tensor("maxima", (2, 3 * HH, SEQ), BF16, kind="Internal").ap()
        vectors = nc.dram_tensor("bias_vectors", (3, H, 16, NV), BF16, kind="Internal").ap()
        loaded = [ctx.enter_context(nc.semaphore(n)) for n in ("first_loaded", "rest_loaded")]
        passed = {n: ctx.enter_context(nc.semaphore(n + "_passed")) for n in ("dve", "pool")}
        with ExitStack() as first:
            load_constants(nc, first, x, resid, ident, identb, half_power, loaded)
        attention(nc, "a", resid, ident, identb, half_power, passed, a, (rel_emb, onehot, vectors), scratch, maxima, zeros, loaded)
        ffn(nc, "f", resid, ident, identb, half_power, passed, f)
        attention(nc, "m", resid, ident, identb, half_power, passed, m, None, scratch, maxima, zeros, None)
        ffn(nc, "g", resid, ident, identb, half_power, passed, f, out)


def distance_onehot():
    import math
    import numpy as np

    n = np.maximum(np.stack([np.arange(NV) - (P - 1), 2 * P - 1 - np.arange(NV)]), 0)
    exact = BUCKETS // 2
    far = exact + (np.log(np.maximum(n, 1).astype(np.float32) / exact) / math.log(MAX_DIST / exact)
                   * (BUCKETS - exact)).astype(np.int32)
    bucket = np.where(n < exact, n, np.minimum(far, BUCKETS - 1))
    return (bucket[:, None, :] == np.arange(BUCKETS)[None, :, None]).astype(np.float32)


def kernel(**inputs):
    import numpy as np
    import concourse.bacc as bacc
    from concourse.bass_utils import run_bass_kernel_spmd

    nc = bacc.Bacc("TRN2", target_bir_lowering=False, num_devices=1)
    arrays = {}

    def given(name, a):
        a = np.ascontiguousarray(a)
        arrays[f"in_{name}"] = a
        return nc.dram_tensor(f"in_{name}", a.shape, mybir.dt.from_np(a.dtype), kind="ExternalInput").ap()

    def of(prefix, name):
        return np.asarray(inputs[f"L0_{prefix}_{name}"])

    x = given("x", of("attn_a", "x"))
    a = {n: given("a_" + n, of("attn_a", n.replace("w", "W")).T) for n in ("wq", "wk", "wv", "wo")}
    m = {n: given("b_" + n, of("attn_b", k)) for n, k in (("wq", "Wq"), ("wk", "Wk"), ("wv", "Wv"), ("wo", "Wp"))}
    for n in ("bq", "bk", "bv"):
        a[n], m[n] = given("a_" + n, of("attn_a", n)), given("b_" + n, of("attn_b", n))
    a["bo"], m["bo"] = given("a_bo", of("attn_a", "bo")), given("b_bo", of("attn_b", "bp"))
    w1 = np.concatenate([of("ffn", "ws1")[None], of("ffn", "w1")])
    w2 = np.concatenate([of("ffn", "ws2")[None], of("ffn", "w2")])
    b1 = np.concatenate([of("ffn", "bs1")[None], of("ffn", "b1")])
    b2 = np.concatenate([of("ffn", "bs2")[None], of("ffn", "b2")])
    f = {
        "gate_w": given("gate_w", of("ffn", "gate_w")), "gate_b": given("gate_b", of("ffn", "gate_b")),
        "w1": given("w1", w1), "w2": given("w2", w2.reshape(NE, HC, P, D).transpose(0, 2, 1, 3)),
        "b1": given("b1", b1.reshape(NE, HC, P).transpose(2, 0, 1)), "b2": given("b2", b2.T),
    }
    rel_emb = given("rel_emb", of("attn_a", "rel_emb"))
    onehot = given("onehot", distance_onehot())
    out = nc.dram_tensor("out", (NB, SEQ, D), F32, kind="ExternalOutput").ap()
    hybrid(nc, x, a, m, f, rel_emb, onehot, out)
    r = run_bass_kernel_spmd(nc, [arrays], core_ids=[0])
    return r.results[0]["out"]
```
